# Optimizing a Trainium2 kernel written in Bass

```python
import numpy as np
import jax
import jax.numpy as jnp

def _softmax(x, axis=-1):
    return jax.nn.softmax(x, axis=axis)
def _gelu(x):
    return jax.nn.gelu(x, approximate=True)
def _silu(x):
    return jax.nn.silu(x)
def _sigmoid(x):
    return jax.nn.sigmoid(x)
def _layernorm(x, axis=-1, eps=1e-5):
    m = jnp.mean(x, axis=axis, keepdims=True)
    v = jnp.var(x, axis=axis, keepdims=True)
    return (x - m) / jnp.sqrt(v + eps)
def _scatter_add(tgt, idx, src, axis=0):
    return tgt.at[idx].add(src)
def _segment_sum(src, seg, n):
    return jax.ops.segment_sum(src, seg, n)

kernel_name = 'mk_metaformer_d2_conv_nchw256_c907f2'

def setup_inputs(seed: int = 0):
    np.random.seed(seed)
    _w = jnp.asarray
    def _rec_inputs():
        import jax
        import jax.numpy as jnp
        _gk = jax.random.key(seed)
        x = -0.000929 + 1 * jax.random.normal(jax.random.fold_in(_gk, 1), (1, 256, 64, 64), jnp.float32)
        return x
    x = _rec_inputs()
    def _L0_conv_setup():
        import jax, jax.numpy as jnp
        import numpy as np
        N_FEAT = 256
        NUM_HEADS = 8
        EPS = 1e-12

        def _l2norm(t):
            n = jnp.linalg.norm(t, axis=-1, keepdims=True)
            return t / jnp.maximum(n, EPS)
        key = jax.random.key(seed)
        k1, k2, k3 = jax.random.split(key, 3)
        b, c, h, w = (1, N_FEAT, 64, 64)
        x = jax.random.normal(k1, (b, c, h, w), dtype=jnp.float32)
        w_qkv = jax.random.normal(k2, (3 * c, c), dtype=jnp.float32) * (1.0 / np.sqrt(c))
        w_proj = jax.random.normal(k3, (c, c), dtype=jnp.float32) * (1.0 / np.sqrt(c))
        temperature = jnp.ones((NUM_HEADS, 1, 1), dtype=jnp.float32)
        return {'x': x, 'w_qkv': w_qkv, 'w_proj': w_proj, 'temperature': temperature}
    _L0_conv_all = _L0_conv_setup()
    _L0_conv_in = {k: v for k, v in _L0_conv_all.items() if k in ('w_qkv', 'w_proj', 'temperature', )}
    del _L0_conv_all

    def _L0_ffn_setup():
        import jax, jax.numpy as jnp
        import numpy as np
        NUM_EXPERTS = 8
        TOP_K = 2
        B, S, D = (8, 8192, 256)

        def _moe(tokens, router_w, w1, b1, w2, b2):
            N = tokens.shape[0]
            E = router_w.shape[0]
            logits = tokens.astype(jnp.float32) @ router_w.astype(jnp.float32).T
            probs = jax.nn.softmax(logits, axis=-1)
            rw, re = jax.lax.top_k(probs, TOP_K)
            if TOP_K > 1:
                rw = rw / jnp.maximum(rw.sum(-1, keepdims=True), 1e-12)
            rw = rw.astype(tokens.dtype)
            combine = jnp.zeros((N, E), tokens.dtype).at[jnp.arange(N)[:, None], re].set(rw)
            out = tokens
            for e in range(E):
                h = jax.nn.gelu(tokens @ w1[e] + b1[e], approximate=False)
                y = h @ w2[e] + b2[e]
                out = out + combine[:, e:e + 1] * y
            return out
        key = jax.random.key(seed)
        ks = jax.random.split(key, 4)
        scale = 1.0 / np.sqrt(D).astype(np.float32)
        return {'input_embeddings': jax.random.normal(ks[0], (B, S, D), jnp.float32), 'router_w': jax.random.normal(ks[1], (NUM_EXPERTS, D), jnp.float32) * scale, 'w1': jax.random.normal(ks[2], (NUM_EXPERTS, D, D), jnp.float32) * scale, 'b1': jnp.zeros((NUM_EXPERTS, D), jnp.float32), 'w2': jax.random.normal(ks[3], (NUM_EXPERTS, D, D), jnp.float32) * scale, 'b2': jnp.zeros((NUM_EXPERTS, D), jnp.float32)}
    _L0_ffn_all = _L0_ffn_setup()
    _L0_ffn_in = {k: v for k, v in _L0_ffn_all.items() if k in ('router_w', 'w1', 'b1', 'w2', 'b2', )}
    del _L0_ffn_all

    def _L1_conv_setup():
        import jax, jax.numpy as jnp
        import numpy as np

        def _conv1x1(x, w, b):
            return jnp.einsum('bchw,oc->bohw', x, w) + b[None, :, None, None]

        def _maxpool2x2(x):
            return jax.lax.reduce_window(x, -jnp.inf, jax.lax.max, window_dimensions=(1, 1, 2, 2), window_strides=(1, 1, 2, 2), padding='VALID')
        key = jax.random.key(seed)
        ks = jax.random.split(key, 9)
        B, C, H, W = (8, 256, 64, 64)
        c = 128
        s = 0.05
        return {'x': jax.random.normal(ks[0], (B, C, H, W), jnp.float32), 'theta_w': jax.random.normal(ks[1], (c, C), jnp.float32) * s, 'theta_b': jax.random.normal(ks[2], (c,), jnp.float32) * s, 'phi_w': jax.random.normal(ks[3], (c, C), jnp.float32) * s, 'phi_b': jax.random.normal(ks[4], (c,), jnp.float32) * s, 'g_w': jax.random.normal(ks[5], (c, C), jnp.float32) * s, 'g_b': jax.random.normal(ks[6], (c,), jnp.float32) * s, 'wz_w': jax.random.normal(ks[7], (C, c), jnp.float32) * s, 'wz_b': jax.random.normal(ks[8], (C,), jnp.float32) * s}
    _L1_conv_all = _L1_conv_setup()
    _L1_conv_in = {k: v for k, v in _L1_conv_all.items() if k in ('theta_w', 'theta_b', 'phi_w', 'phi_b', 'g_w', 'g_b', 'wz_w', 'wz_b', )}
    del _L1_conv_all

    def _L1_ffn_setup():
        import jax, jax.numpy as jnp
        import numpy as np
        TOP_K = 2
        key = jax.random.key(seed)
        ks = jax.random.split(key, 4)
        B, L, D, H, E = (8, 4096, 256, 1024, 8)
        s = 0.02
        return {'x': jax.random.normal(ks[0], (B, L, D), jnp.float32), 'Wg': jax.random.normal(ks[1], (D, E), jnp.float32) * s, 'bg': jnp.zeros((E,), jnp.float32), 'W1': jax.random.normal(ks[2], (E, D, H), jnp.float32) * s, 'b1': jnp.zeros((E, H), jnp.float32), 'W2': jax.random.normal(ks[3], (E, H, D), jnp.float32) * s, 'b2': jnp.zeros((E, D), jnp.float32)}
    _L1_ffn_all = _L1_ffn_setup()
    _L1_ffn_in = {k: v for k, v in _L1_ffn_all.items() if k in ('Wg', 'bg', 'W1', 'b1', 'W2', 'b2', )}
    del _L1_ffn_all

    return {
        "x": x,
        "L0_conv_w_qkv": _L0_conv_in["w_qkv"],
        "L0_conv_w_proj": _L0_conv_in["w_proj"],
        "L0_conv_temperature": _L0_conv_in["temperature"],
        "L0_ffn_router_w": _L0_ffn_in["router_w"],
        "L0_ffn_w1": _L0_ffn_in["w1"],
        "L0_ffn_b1": _L0_ffn_in["b1"],
        "L0_ffn_w2": _L0_ffn_in["w2"],
        "L0_ffn_b2": _L0_ffn_in["b2"],
        "L1_conv_theta_w": _L1_conv_in["theta_w"],
        "L1_conv_theta_b": _L1_conv_in["theta_b"],
        "L1_conv_phi_w": _L1_conv_in["phi_w"],
        "L1_conv_phi_b": _L1_conv_in["phi_b"],
        "L1_conv_g_w": _L1_conv_in["g_w"],
        "L1_conv_g_b": _L1_conv_in["g_b"],
        "L1_conv_wz_w": _L1_conv_in["wz_w"],
        "L1_conv_wz_b": _L1_conv_in["wz_b"],
        "L1_ffn_Wg": _L1_ffn_in["Wg"],
        "L1_ffn_bg": _L1_ffn_in["bg"],
        "L1_ffn_W1": _L1_ffn_in["W1"],
        "L1_ffn_b1": _L1_ffn_in["b1"],
        "L1_ffn_W2": _L1_ffn_in["W2"],
        "L1_ffn_b2": _L1_ffn_in["b2"],
    }

def reference(x, L0_conv_w_qkv, L0_conv_w_proj, L0_conv_temperature, L0_ffn_router_w, L0_ffn_w1, L0_ffn_b1, L0_ffn_w2, L0_ffn_b2, L1_conv_theta_w, L1_conv_theta_b, L1_conv_phi_w, L1_conv_phi_b, L1_conv_g_w, L1_conv_g_b, L1_conv_wz_w, L1_conv_wz_b, L1_ffn_Wg, L1_ffn_bg, L1_ffn_W1, L1_ffn_b1, L1_ffn_W2, L1_ffn_b2):
    import jax
    import jax.numpy as jnp
    def _L0_conv_ref(x, w_qkv, w_proj, temperature):
        import jax, jax.numpy as jnp
        import numpy as np
        N_FEAT = 256
        NUM_HEADS = 8
        EPS = 1e-12

        def _l2norm(t):
            n = jnp.linalg.norm(t, axis=-1, keepdims=True)
            return t / jnp.maximum(n, EPS)
        b, c, h, w = x.shape
        heads = temperature.shape[0]
        d = c // heads
        hw = h * w
        xf = x.reshape(b, c, hw)
        qkv = jnp.einsum('oc,bcs->bos', w_qkv, xf)
        qkv = qkv.reshape(b, 3, heads, d, hw)
        q, k, v = (qkv[:, 0], qkv[:, 1], qkv[:, 2])
        q = jnp.swapaxes(q, -2, -1)
        k = jnp.swapaxes(k, -2, -1)
        v = jnp.swapaxes(v, -2, -1)
        q = _l2norm(q)
        k = _l2norm(k)
        attn = jnp.einsum('bhsd,bhtd->bhst', q, k) * temperature[None]
        attn = jax.nn.softmax(attn, axis=-1)
        out = jnp.einsum('bhst,bhtd->bhsd', attn, v)
        out = out.transpose(0, 2, 1, 3).reshape(b, c, h, w)
        out = jnp.einsum('oc,bchw->bohw', w_proj, out)
        return out

    def _L0_ffn_ref(input_embeddings, router_w, w1, b1, w2, b2):
        import jax, jax.numpy as jnp
        import numpy as np
        NUM_EXPERTS = 8
        TOP_K = 2
        B, S, D = (8, 8192, 256)

        def _moe(tokens, router_w, w1, b1, w2, b2):
            N = tokens.shape[0]
            E = router_w.shape[0]
            logits = tokens.astype(jnp.float32) @ router_w.astype(jnp.float32).T
            probs = jax.nn.softmax(logits, axis=-1)
            rw, re = jax.lax.top_k(probs, TOP_K)
            if TOP_K > 1:
                rw = rw / jnp.maximum(rw.sum(-1, keepdims=True), 1e-12)
            rw = rw.astype(tokens.dtype)
            combine = jnp.zeros((N, E), tokens.dtype).at[jnp.arange(N)[:, None], re].set(rw)
            out = tokens
            for e in range(E):
                h = jax.nn.gelu(tokens @ w1[e] + b1[e], approximate=False)
                y = h @ w2[e] + b2[e]
                out = out + combine[:, e:e + 1] * y
            return out
        b, s, d = input_embeddings.shape
        tokens = input_embeddings.reshape(b * s, d)
        return _moe(tokens, router_w, w1, b1, w2, b2).reshape(b, s, d)

    def _L1_conv_ref(x, theta_w, theta_b, phi_w, phi_b, g_w, g_b, wz_w, wz_b):
        import jax, jax.numpy as jnp
        import numpy as np

        def _conv1x1(x, w, b):
            return jnp.einsum('bchw,oc->bohw', x, w) + b[None, :, None, None]

        def _maxpool2x2(x):
            return jax.lax.reduce_window(x, -jnp.inf, jax.lax.max, window_dimensions=(1, 1, 2, 2), window_strides=(1, 1, 2, 2), padding='VALID')
        B, C, H, W = x.shape
        c = theta_w.shape[0]
        ox = x
        theta = _conv1x1(x, theta_w, theta_b)
        xp = _maxpool2x2(x)
        phi = _conv1x1(xp, phi_w, phi_b)
        gi = _conv1x1(xp, g_w, g_b)
        N = H * W
        M = phi.shape[2] * phi.shape[3]
        theta1 = theta.reshape(B, c, N).transpose(0, 2, 1)
        phi1 = phi.reshape(B, c, M)
        gi1 = gi.reshape(B, c, M).transpose(0, 2, 1)
        m1 = jnp.einsum('bnc,bcm->bnm', theta1, phi1)
        m1 = jax.nn.softmax(m1, axis=2)
        m2 = jnp.einsum('bnm,bmc->bnc', m1, gi1)
        m3 = m2.reshape(B, c, H, W)
        m4 = _conv1x1(m3, wz_w, wz_b)
        return m4 + ox

    def _L1_ffn_ref(x, Wg, bg, W1, b1, W2, b2):
        import jax, jax.numpy as jnp
        import numpy as np
        TOP_K = 2
        B, L, D = x.shape
        E = W1.shape[0]
        xf = x.reshape(-1, D)
        gate_logits = xf @ Wg + bg
        top_w, top_i = jax.lax.top_k(gate_logits, TOP_K)
        top_w = jax.nn.softmax(top_w, axis=-1)
        w_dense = jnp.sum(jax.nn.one_hot(top_i, E, dtype=xf.dtype) * top_w[..., None], axis=1)
        out = jnp.zeros_like(xf)
        for e in range(E):
            h = jax.nn.gelu(xf @ W1[e] + b1[e], approximate=False)
            out = out + w_dense[:, e:e + 1] * (h @ W2[e] + b2[e])
        return out.reshape(B, L, D)

    def _gn(v, G=32, eps=1e-5):
        B_, C_, H_, W_ = v.shape
        g = v.reshape(B_, G, C_ // G, H_, W_)
        m = jnp.mean(g, axis=(2, 3, 4), keepdims=True)
        s = jnp.var(g, axis=(2, 3, 4), keepdims=True)
        return ((g - m) / jnp.sqrt(s + eps)).reshape(v.shape)

    def _ln_c(v, eps=1e-6):
        m = jnp.mean(v, axis=1, keepdims=True)
        s = jnp.var(v, axis=1, keepdims=True)
        return (v - m) / jnp.sqrt(s + eps)

    def _ln_t(v, eps=1e-5):
        m = jnp.mean(v, axis=-1, keepdims=True)
        s = jnp.var(v, axis=-1, keepdims=True)
        return (v - m) / jnp.sqrt(s + eps)

    def _to_tokens(v):
        B_, C_, H_, W_ = v.shape
        return v.reshape(B_, C_, H_ * W_).transpose(0, 2, 1)
    def _from_tokens(t, like):
        B_, C_, H_, W_ = like.shape
        return t.transpose(0, 2, 1).reshape(B_, C_, H_, W_)

    x = x + _L0_conv_ref(_ln_c(x), L0_conv_w_qkv, L0_conv_w_proj, L0_conv_temperature)
    t = _to_tokens(x)
    t = t + _L0_ffn_ref(_ln_t(t), L0_ffn_router_w, L0_ffn_w1, L0_ffn_b1, L0_ffn_w2, L0_ffn_b2)
    x = _from_tokens(t, x)
    x = x + _L1_conv_ref(_ln_c(x), L1_conv_theta_w, L1_conv_theta_b, L1_conv_phi_w, L1_conv_phi_b, L1_conv_g_w, L1_conv_g_b, L1_conv_wz_w, L1_conv_wz_b)
    t = _to_tokens(x)
    t = t + _L1_ffn_ref(_ln_t(t), L1_ffn_Wg, L1_ffn_bg, L1_ffn_W1, L1_ffn_b1, L1_ffn_W2, L1_ffn_b2)
    x = _from_tokens(t, x)
    return x


_drawn_inputs = setup_inputs


def setup_inputs(seed=0):
    import zlib

    import numpy as np

    out = dict(_drawn_inputs(seed))
    spreads = {'L0_conv_temperature': (1.0, 0.6),
     'L0_ffn_b1': (0.0, 0.31),
     'L0_ffn_b2': (0.0, 0.1),
     'L1_ffn_bg': (0.0, 0.422),
     'L1_ffn_b1': (0.0, 0.8),
     'L1_ffn_b2': (0.0, 0.348)}
    factors = {'L1_conv_theta_b': 5.798,
     'L1_conv_phi_b': 8.0,
     'L1_conv_g_b': 5.606,
     'L1_conv_wz_b': 3.567}
    for name, (base, spread) in spreads.items():
        noise = np.random.default_rng([zlib.crc32(name.encode()), seed]).standard_normal(out[name].shape)
        drawn = base * np.exp(spread * noise) if base else spread * noise
        out[name] = jnp.asarray(drawn.astype(out[name].dtype))
    for name, factor in factors.items():
        out[name] = (out[name] * factor).astype(out[name].dtype)
    return out
```

```python
from contextlib import ExitStack

import concourse.bass as bass
from concourse import mybir

F32 = mybir.dt.float32
F16 = mybir.dt.float16
BF16 = mybir.dt.bfloat16
I32 = mybir.dt.int32
ACT = mybir.ActivationFunctionType
ALU = mybir.AluOpType
AX = mybir.AxisListType
ds = bass.ds

P = 128
D = 256
KB = D // P
HW = 64
S = HW * HW
NT = S // P
GT = 4
NG = NT // GT
HEADS = 8
DH = D // HEADS
LN_C_EPS = 1e-6
LN_T_EPS = 1e-5
NORM_EPS = 1e-12
W_SCALE = 64.0
QK_SCALE = 64.0
P_SHIFT = 20.0
LN2 = 0.6931471805599453
VW = 2 * DH + 2
VN = 2 * DH + 1

GROUP = 2
NGRP = NT // GROUP
CHUNK = 512
SPT = CHUNK // P
NCH = S // CHUNK
PBUF = 4
AHEAD = 3
LOOK = 3
DVE_COLS = 720
ROWS_PER = S // D


IN_USE = []


def semaphore(nc, name):
    IN_USE.append(nc.alloc_semaphore(name))
    return IN_USE[-1]


def clear_semaphores(nc):
    nc.clear_and_free_semaphores(IN_USE)
    IN_USE.clear()
    nc.all_engine_barrier()


def make_identities(nc, ident32, ident16):
    ident_zero = semaphore(nc, "ident_zero")
    ident_done = semaphore(nc, "ident_done")
    with nc.Block() as block:
        @block.gpsimd
        def _(pool):
            pool.memset(ident32[:, :], 0.0).then_inc(ident_zero, 1)
            pool.memset(ident16[:, :], 0.0).then_inc(ident_zero, 1)
            pool.wait_ge(ident_zero, 2)
            for m in (ident32, ident16):
                pool.affine_select(out=m[:, :], in_=m[:, :], compare_op=ALU.not_equal, fill=1.0,
                                   base=0, pattern=[[-1, P]], channel_multiplier=1).then_inc(ident_done, 1)
            pool.wait_ge(ident_done, 2)


def load_and_split_tokens(nc, x_dram, w_dram, temp_dram, ident32, xc, xp, xh, xl, rstd, tau, wh, wl):
    MO = 3 * D // P
    ctx = ExitStack()
    with ctx:
        sb = lambda name, shape, dt: ctx.enter_context(nc.sbuf_tensor(name, shape, dt))
        ps = lambda name, shape: ctx.enter_context(nc.psum_tensor(name, shape, F32))
        sem = lambda name: semaphore(nc, name)
        XQ = 4
        QC = S // XQ

        wn = sb("wn", [P, MO, D], F32)
        wt = sb("wt", [P, KB, 3 * D], F32)
        wmean = sb("wmean", [P, MO], F32)
        stats = sb("stats", [P, NT, 6], F32)
        mv = sb("mv", [P, NT, 2], F32)
        sd = sb("sd", [P, NT], F32)
        eps = sb("eps", [P, 1], F32)
        ptx = [ps(f"ptx{i}", [P, 2, D]) for i in range(3)]
        ptw = [ps(f"ptw{i}", [P, 4, P]) for i in range(2)]
        w_in = sem("w_in")
        t_in = sem("t_in")
        x_in = [sem(f"x_in{i}") for i in range(XQ)]
        w_step = sem("w_step")
        w_cent = sem("w_cent")
        wt_ready = sem("wt_ready")
        wt_used = sem("wt_used")
        wh_ready = sem("wh_ready")
        xp_ready = sem("xp_ready")
        xh_ready = sem("xh_ready")
        xt_ready = sem("xt_ready")
        xt_used = sem("xt_used")
        agg = sem("agg")
        eps_ready = sem("eps_ready")
        sd_ready = sem("sd_ready")
        done = sem("done")
        block = ctx.enter_context(nc.Block())

        @block.sync
        def _(sp):
            sp.dma_start(wn[:, :, :], w_dram.rearrange("(m p) c -> p m c", p=P)).then_inc(w_in, 16)
            for q in range(XQ):
                sp.dma_start(xc[:, :, q * QC:(q + 1) * QC],
                             x_dram.rearrange("b (k p) h w -> p (b k) (h w)", p=P)[:, :, q * QC:(q + 1) * QC]
                             ).then_inc(x_in[q], 16)
            sp.dma_start(tau[:, :], temp_dram.rearrange("h a b -> (h a b)").partition_broadcast(P)).then_inc(t_in, 16)
            sp.wait_ge(t_in, 16)

        @block.vector
        def _(dve):
            dve.memset(eps[:, :], LN_C_EPS).then_inc(eps_ready, 1)
            dve.wait_ge(w_in, 16)
            dve.tensor_reduce(wmean[:, :], wn[:, :, :], AX.X, ALU.add).then_inc(w_step, 1)
            dve.wait_ge(w_step, 1)
            dve.tensor_scalar(wmean[:, :], wmean[:, :], -1.0 / D, None, ALU.mult).then_inc(w_step, 1)
            dve.wait_ge(w_step, 2)
            for m in range(MO):
                dve.tensor_scalar(wn[:, m, :], wn[:, m, :], wmean[:, m:m + 1], None, ALU.add).then_inc(w_cent, 1)
            for k in range(KB):
                for i, (m0, m1) in enumerate(((0, 4), (4, MO))):
                    n = 2 * k + i
                    dve.wait_ge(wt_ready, n + 1)
                    dve.tensor_scalar(wt[:, k, m0 * P:m1 * P], ptw[n % 2][:, 0:m1 - m0, :].rearrange("p a b -> p (a b)"),
                                      W_SCALE, None, ALU.mult).then_inc(wt_used, 1)
            dve.wait_ge(wh_ready, 1)
            dve.tensor_tensor(wl[:, :, :], wt[:, :, :], wh[:, :, :], ALU.subtract).then_inc(done, 1)
            for q in range(XQ):
                dve.wait_ge(xh_ready, q + 1)
                dve.tensor_tensor(xl[:, :, q * QC:(q + 1) * QC], xp[:, :, q * QC:(q + 1) * QC],
                                  xh[:, :, q * QC:(q + 1) * QC], ALU.subtract).then_inc(done, 1)
                for n in range(q * NT // XQ // 2, (q + 1) * NT // XQ // 2):
                    dve.wait_ge(xt_ready, n + 1)
                    for j in range(2):
                        last = dve.bn_stats(stats[:, 2 * n + j, :], ptx[n % 3][:, j, :])
                    last.then_inc(xt_used, 1)
            dve.wait_ge(xt_used, NT // 2)
            for t in range(NT):
                last = dve.bn_aggr(mv[:, t, :], stats[:, t, :])
            last.then_inc(agg, 1)
            dve.wait_ge(sd_ready, 1)
            dve.reciprocal(rstd[:, :], sd[:, :]).then_inc(done, 1)
            dve.wait_ge(done, 2 + XQ)

        @block.scalar
        def _(act):
            act.wait_ge(wt_used, 2 * KB)
            act.activation(wh[:, :, :], wt[:, :, :], ACT.Copy).then_inc(wh_ready, 1)
            for q in range(XQ):
                act.wait_ge(x_in[q], 16)
                for k in range(KB):
                    c = slice(q * QC, (q + 1) * QC)
                    act.activation(xp[:, k, c].rearrange("p (b r i) -> p b r i", b=QC // CHUNK, r=ROWS_PER),
                                   xc[:, k, c].rearrange("p (b i r) -> p b r i", b=QC // CHUNK, r=ROWS_PER),
                                   ACT.Copy).then_inc(xp_ready, 1)
                act.wait_ge(xp_ready, KB * (q + 1))
                act.activation(xh[:, :, c], xp[:, :, c], ACT.Copy).then_inc(xh_ready, 1)
            act.wait_ge(agg, 1)
            act.wait_ge(eps_ready, 1)
            act.activation(sd[:, :], mv[:, :, 1], ACT.Sqrt, bias=eps[:, 0:1]).then_inc(sd_ready, 1)

        @block.tensor
        def _(pe):
            pe.wait_ge(w_cent, MO)
            for k in range(KB):
                for i, (m0, m1) in enumerate(((0, 4), (4, MO))):
                    n = 2 * k + i
                    if n >= 2:
                        pe.wait_ge(wt_used, n - 1)
                    for m in range(m0, m1):
                        last = pe.transpose(ptw[n % 2][:, m - m0, :], wn[:, m, k * P:(k + 1) * P], ident32[:, :])
                    last.then_inc(wt_ready, 1)
            for n in range(NT // 2):
                pe.wait_ge(xp_ready, KB * (n * XQ * 2 // NT + 1))
                if n >= 3:
                    pe.wait_ge(xt_used, n - 2)
                for j in range(2):
                    for k in range(KB):
                        last = pe.transpose(ptx[n % 3][:, j, k * P:(k + 1) * P],
                                            xp[:, k, (2 * n + j) * P:(2 * n + j + 1) * P], ident32[:, :])
                last.then_inc(xt_ready, 1)


def project_qkv(nc, xh, xl, rstd, tau, wh, wl, scratch, qk, vs):
    assert QK_SCALE == W_SCALE
    ctx = ExitStack()
    with ctx:
        sb = lambda name, shape, dt: ctx.enter_context(nc.sbuf_tensor(name, shape, dt))
        ps = lambda name, shape: ctx.enter_context(nc.psum_tensor(name, shape, F32))
        sem = lambda name: semaphore(nc, name)
        QK = 2 * D
        NH2 = 2 * HEADS
        qs, ks = qk[:, :, :, 0:2 * DH], qk[:, :, :, 2 * DH:4 * DH]
        part = lambda n: scratch[:, n // 2, n % 2 * GT * QK:(n % 2 + 1) * GT * QK].rearrange("p (t c) -> p t c", t=GT)
        raw = [part(u) for u in range(2)]
        vraw = [sb(f"vraw{u}", [P, GT, D], F32) for u in range(2)]
        sq = [part(2 + u) for u in range(2)]
        ss = sb("ss", [P, GT, NH2], F32)
        nrm = sb("nrm", [P, GT, NH2], F32)
        inv = sb("inv", [P, GT, NH2], F32)
        pqk = [ps(f"pqk{u}", [P, QK]) for u in range(2)]
        pv = [ps(f"pv{u}", [P, 512]) for u in range(2)]
        qkv_ready = sem("qkv_ready")
        qkv_taken = sem("qkv_taken")
        sq_free = sem("sq_free")
        raw_free = [sem(f"raw_free{u}") for u in range(2)]
        ss_ready = sem("ss_ready")
        nrm_ready = sem("nrm_ready")
        dchain = sem("dchain")
        unit_ready = sem("unit_ready")
        hi_ready = sem("hi_ready")
        pool_going = sem("pool_going")
        ones_set = sem("ones_set")
        block = ctx.enter_context(nc.Block())

        @block.tensor
        def _(pe):
            with pe.Fori(0, NT // 2) as it:
                for u in range(2):
                    tile = it * 2 + u
                    pe.wait_ge(qkv_taken, tile + 1)
                    first, last_of = {}, {}
                    n = 0
                    for k in range(KB):
                        for xx, ww in ((xh, wh), (xl, wh), (xh, wl)):
                            lhs = xx[:, k, ds(tile * P, P)]
                            pe.matmul(pqk[u][:, :], lhs, ww[:, k, 0:QK], start=(n == 0), stop=(n == 5))
                            last = pe.matmul(pv[u][:, 0:D], lhs, ww[:, k, QK:QK + D], start=(n == 0), stop=(n == 5))
                            n += 1
                    last.then_inc(qkv_ready, 1)

        @block.scalar
        def _(act):
            def root(g):
                act.wait_ge(ss_ready, g + 1)
                act.activation(nrm[:, :, :], ss[:, :, :], ACT.Sqrt).then_inc(nrm_ready, 1)

            def fill(g, u, it):
                act.wait_ge(raw_free[u], 2 * it + 2)
                act.wait_ge(sq_free, g + 1)
                for t in range(GT):
                    act.wait_ge(qkv_ready, g * GT + t + 1)
                    act.activation(raw[u][:, t, :], pqk[t % 2][:, :], ACT.Copy)
                    act.activation(sq[u][:, t, :], pqk[t % 2][:, :], ACT.Square)
                    act.activation(vraw[u][:, t, :], pv[t % 2][:, 0:D], ACT.Copy, scale=1.0 / W_SCALE
                                   ).then_inc(qkv_taken, 1)

            act.sem_inc(qkv_taken, 2)
            with act.Fori(0, NG // 2) as it:
                for u in range(2):
                    fill(it * 2 + u, u, it)
                    root(it * 2 + u)

        @block.vector
        def _(dve):
            links = 0

            def chained(ins):
                nonlocal links
                links += 1
                ins.then_inc(dchain, 1)
                dve.wait_ge(dchain, it * (2 * PER) + links)

            PER = 6
            for u in range(2):
                dve.sem_inc(raw_free[u], 2)
            dve.sem_inc(sq_free, 2)
            dve.memset(vs[:, :, :, 2 * DH:VW], 1.0).then_inc(ones_set, 1)
            with dve.Fori(0, NG // 2) as it:
                links = 0
                for u in range(2):
                    g = it * 2 + u
                    dve.wait_ge(qkv_taken, g * GT + GT + 2)
                    dve.tensor_reduce(ss[:, :, :], sq[u][:, :, :].rearrange("p t (h d) -> p t h d", d=DH), AX.X,
                                      ALU.add).then_inc(sq_free, 1)
                    dve.wait_ge(sq_free, g + 3)
                    dve.sem_inc(ss_ready, 1)
                    rb = rstd[:, ds(g * GT, GT)].unsqueeze(2)
                    chained(dve.tensor_tensor(vraw[u][:, :, :], vraw[u][:, :, :], rb.broadcast_to([P, GT, D]), ALU.mult))
                    dve.wait_ge(nrm_ready, g + 1)
                    chained(dve.tensor_tensor(nrm[:, :, :], nrm[:, :, :], rb.broadcast_to([P, GT, NH2]), ALU.mult))
                    chained(dve.tensor_scalar(nrm[:, :, :], nrm[:, :, :], 1.0 / W_SCALE, NORM_EPS, ALU.mult, ALU.max))
                    chained(dve.reciprocal(inv[:, :, :], nrm[:, :, :]))
                    chained(dve.tensor_tensor(inv[:, :, :], inv[:, :, :], rb.broadcast_to([P, GT, NH2]), ALU.mult))
                    chained(dve.tensor_tensor(inv[:, :, 0:HEADS], inv[:, :, 0:HEADS],
                                              tau[:, :].unsqueeze(1).broadcast_to([P, GT, HEADS]), ALU.mult))
                    for t in range(GT):
                        rv = raw[u][:, t, :].rearrange("p (h d) -> p h d", d=DH)
                        iv = inv[:, t, :].unsqueeze(2).broadcast_to([P, NH2, DH])
                        last = dve.tensor_tensor(rv, rv, iv, ALU.mult)
                    last.then_inc(unit_ready, 1)
                    dve.wait_ge(unit_ready, g + 1)
                    for t in range(GT):
                        rv = raw[u][:, t, :].rearrange("p (m h d) -> p m h d", m=2, d=DH)
                        vv = vraw[u][:, t, :].rearrange("p (h d) -> p h d", d=DH)
                        dve.tensor_copy(qs[:, ds(g * GT + t, 1), :, 0:DH].squeeze(1), rv[:, 0])
                        dve.tensor_copy(ks[:, ds(g * GT + t, 1), :, DH:2 * DH].squeeze(1), rv[:, 1])
                        dve.tensor_copy(vs[:, ds(g * GT + t, 1), :, 0:DH].squeeze(1), vv).then_inc(hi_ready, 1)

        @block.gpsimd
        def _(pool):
            pool.wait_ge(ones_set, 1)
            with pool.Fori(0, NG // 2) as it:
                for u in range(2):
                    g = it * 2 + u
                    for t in range(GT):
                        pool.wait_ge(hi_ready, g * GT + t + 1)
                        pool.sem_inc(pool_going, 1)
                        rv = raw[u][:, t, :].rearrange("p (m h d) -> p m h d", m=2, d=DH)
                        vv = vraw[u][:, t, :].rearrange("p (h d) -> p h d", d=DH)
                        for dst, src, hi, lo in ((qs, rv[:, 0], 0, DH), (ks, rv[:, 1], DH, 0), (vs, vv, 0, DH)):
                            row = dst[:, ds(g * GT + t, 1), :, :].squeeze(1)
                            last = pool.tensor_tensor(row[:, :, lo:lo + DH], src, row[:, :, hi:hi + DH], ALU.subtract)
                    last.then_inc(raw_free[u], 2)


def attention(nc, qk, vs, tau, ident16, aout, sorted_dram):
    ctx = ExitStack()
    with ctx:
        sb = lambda name, shape, dt: ctx.enter_context(nc.sbuf_tensor(name, shape, dt))
        ps = lambda name, shape, dt=F32: ctx.enter_context(nc.psum_tensor(name, shape, dt))
        sem = lambda name: semaphore(nc, name)
        GC = GROUP * CHUNK
        ZROWS = -(-ROWS // (HEADS * NCH * P))
        ZP = ROWS // (HEADS * NCH * ZROWS)
        assert ZP * ZROWS * HEADS * NCH == ROWS

        def high(p):
            return p[:, :].bitcast(BF16).rearrange("p (n two) -> p n two", two=2)[:, :, 1]

        qT = sb("qT", [P, 2 * S], F16)
        kT = sb("kT", [P, 2 * S], F16)
        halves = [sb(f"halves{u}", [P, CHUNK], F16) for u in range(2)]
        staged = [sb(f"staged{u}", [P, GT, 4 * DH], F16) for u in range(2)]
        shift_rows = sb("shift_rows", [P, HEADS, CHUNK], F16)
        prob = [sb(f"prob{i}", [P, GC], F32) for i in range(PBUF)]
        plow = [sb(f"plow{i}", [P, GC], F16) for i in range(PBUF)]
        shift = sb("shift", [P, HEADS], F32)
        warm = sb("warm", [P, 1], F32)
        zero = sb("zero", [P, ZROWS, 2 * D], F16)
        osb = sb("osb", [P, SPT, VN], F32)
        rec = sb("rec", [P, SPT], F32)
        osum = sb("osum", [P, SPT, DH], F32)
        scores = [ps(f"scores{i}", [P, GC]) for i in range(2)]
        outp = ps("outp", [P, 2, 512])
        turned = ps("turned", [P, 2 * GT, P], F16)[:, 0:GT, :]
        score_ready = sem("score_ready")
        prob_ready = sem("prob_ready")
        low_ready = sem("low_ready")
        lowp_ready = sem("lowp_ready")
        prob_used = sem("prob_used")
        out_taken = sem("out_taken")
        rec_ready = sem("rec_ready")
        osb_used = sem("osb_used")
        turned_ready = sem("turned_ready")
        turned_taken = sem("turned_taken")
        shift_ready = sem("shift_ready")
        sum_step = sem("sum_step")
        shift_set = sem("shift_set")
        stage_in = [sem(f"stage_in{u}") for u in range(2)]
        q_const = sem("q_const")
        zero_set = sem("zero_set")
        zeroed = sem("zeroed")
        placed = [sem(f"placed{u}") for u in range(2)]
        PLACE = 5 * 16
        block = ctx.enter_context(nc.Block())

        def pairs_of_chunks(eng, step):
            with eng.Fori(0, HEADS * NCH // 2 - 1) as it:
                for u in range(2):
                    step(it * 2 + u, u, True)
            step(HEADS * NCH - 2, 0, True)
            step(HEADS * NCH - 1, 1, False)

        @block.gpsimd
        def _(pool):
            def low(c, g):
                pool.wait_ge(prob_ready, c * NGRP + g + 1)
                p, l = prob[g % PBUF], plow[g % PBUF]
                pool.tensor_tensor(l[:, DVE_COLS:GC], p[:, DVE_COLS:GC], high(p)[:, DVE_COLS:GC],
                                   ALU.subtract).then_inc(lowp_ready, 1)

            def add_halves(c):
                pool.wait_ge(rec_ready, c + 1)
                pool.tensor_tensor(osum[:, :, :], osb[:, :, 0:DH], osb[:, :, DH:2 * DH], ALU.add).then_inc(sum_step, 1)

            def divide(c):
                pool.wait_ge(sum_step, c + 1)
                image = aout[:, :, :].rearrange("p k (r h d) -> p (k r) h d", h=HEADS, d=DH)
                pool.tensor_tensor(image[:, ds((c % NCH) * SPT, SPT), ds(c // NCH, 1), :].squeeze(2), osum[:, :, :],
                                   rec[:, :].unsqueeze(2).broadcast_to([P, SPT, DH]), ALU.mult).then_inc(osb_used, 1)

            pool.sem_inc(osb_used, 1)
            pool.memset(qT[3 * DH:4 * DH, :], QK_SCALE / DH).then_inc(q_const, 1)
            pool.wait_ge(q_const, 1)
            pool.memset(zero[:, :, :], 0.0).then_inc(zero_set, 1)
            pool.wait_ge(zero_set, 1)
            for g in range(AHEAD):
                low(0, g)

            def step(c, u, more, before=True):
                for g in range(AHEAD, NGRP):
                    low(c, g)
                    if before and g == 5:
                        add_halves(c - 1)
                    if before and g == 9:
                        divide(c - 1)
                if more:
                    for g in range(AHEAD):
                        low(c + 1, g)

            step(0, 0, True, False)
            with pool.Fori(0, HEADS * NCH // 2 - 1) as it:
                for u in range(2):
                    step(it * 2 + 1 + u, 1 - u, True)
            step(HEADS * NCH - 1, 1, False)
            add_halves(HEADS * NCH - 1)
            divide(HEADS * NCH - 1)
            pool.wait_ge(osb_used, HEADS * NCH + 1)

        @block.scalar
        def _(act):
            act.activation(warm[:, :], tau[:, 0:1], ACT.Exp)
            with act.Fori(0, HEADS * NCH // 2) as it:
                for g in range(2 * NGRP):
                    n = it * (2 * NGRP) + g
                    act.wait_ge(score_ready, n + 1)
                    act.wait_ge(prob_used, n + 1)
                    act.activation(prob[g % PBUF][:, :], scores[g % 2][:, :], ACT.Exp,
                                   scale=1.0 / (QK_SCALE * QK_SCALE)).then_inc(prob_ready, 1)

        @block.sync
        def _(sp):
            def stage(turn, u):
                h, j = turn // NCH % HEADS, turn % NCH
                sp.dma_start(staged[u][:, :, :], qk[:, ds(j * GT, GT), ds(h, 1), :].squeeze(2)).then_inc(stage_in[u], 16)

            def place(turn, u):
                h, j = turn // NCH, turn % NCH
                sp.wait_ge(turned_taken, turn + 2)
                k_cols = ds((h % 2) * S + j * CHUNK, CHUNK)
                q_from = lambda rows: halves[u][0:rows, :].rearrange("p (r i) -> p r i", r=ROWS_PER)
                q_to = lambda r0, r1: qT[r0:r1, :].rearrange("p (b r i) -> p b r i", r=ROWS_PER, i=P)[
                    :, ds((h % 2) * 2 + j // 4, 1), :, ds((j % 4) * (CHUNK // ROWS_PER), CHUNK // ROWS_PER)].squeeze(1)
                sp.dma_start(kT[0:2 * DH, k_cols], halves[u][2 * DH:4 * DH, :]).then_inc(placed[u], 16)
                sp.dma_start(kT[2 * DH:3 * DH, k_cols], halves[u][3 * DH:4 * DH, :]).then_inc(placed[u], 16)
                sp.dma_start(kT[3 * DH:4 * DH, k_cols], shift_rows[3 * DH:4 * DH, ds(h % HEADS, 1), :].squeeze(1)
                             ).then_inc(placed[u], 16)
                sp.dma_start(q_to(0, 2 * DH), q_from(2 * DH)).then_inc(placed[u], 16)
                sp.dma_start(q_to(2 * DH, 3 * DH), q_from(DH)).then_inc(placed[u], 16)

            def zero_rows(c):
                sp.dma_start(sorted_dram[ds(c * ZP * ZROWS, ZP * ZROWS), :].rearrange("(p a) c -> p a c", a=ZROWS),
                             zero[0:ZP, :, :]).then_inc(zeroed, 16)

            stage(0, 0)
            stage(1, 1)
            sp.wait_ge(shift_set, 1)
            with sp.Fori(0, NCH // 2) as it:
                for u in range(2):
                    turn = it * 2 + u
                    sp.wait_ge(turned_ready, turn + 1)
                    stage(turn + 2, u)
                    place(turn, u)
            sp.wait_ge(zero_set, 1)

            def step(c, u, more):
                if more:
                    place(c + NCH, u)
                    stage(c + NCH + 2, u)
                zero_rows(c)

            pairs_of_chunks(sp, step)
            sp.wait_ge(zeroed, 16 * HEADS * NCH)
            for u in range(2):
                sp.wait_ge(stage_in[u], 16 * ((HEADS * NCH + NCH - u) // 2 + 1))

        @block.vector
        def _(dve):
            dve.sem_inc(out_taken, 2)
            dve.sem_inc(turned_taken, 1)
            for u in range(2):
                dve.sem_inc(placed[u], 16)
            dve.tensor_scalar(shift[:, :], tau[:, :], -1.0, None, ALU.mult).then_inc(shift_ready, 1)
            dve.wait_ge(shift_ready, 1)
            dve.tensor_tensor(shift[:, :], shift[:, :], tau[:, :], ALU.max).then_inc(shift_ready, 1)
            dve.wait_ge(shift_ready, 2)
            dve.tensor_scalar(shift[:, :], shift[:, :], -1.0, P_SHIFT * LN2, ALU.mult, ALU.add).then_inc(shift_ready, 1)
            dve.wait_ge(shift_ready, 3)
            dve.tensor_scalar(shift_rows[3 * DH:4 * DH, :, :], shift[3 * DH:4 * DH, :].unsqueeze(2)
                              .broadcast_to([DH, HEADS, CHUNK]), QK_SCALE, None, ALU.mult).then_inc(shift_set, 1)

            def take_turned(turn, u):
                dve.wait_ge(turned_ready, turn + 1)
                dve.wait_ge(placed[u], (turn - u) // 2 * PLACE + 16)
                dve.tensor_copy(halves[u][:, :], turned[:, :, :].rearrange("p a b -> p (a b)")).then_inc(turned_taken, 1)

            def low(c, g):
                dve.wait_ge(prob_ready, c * NGRP + g + 1)
                p, l = prob[g % PBUF], plow[g % PBUF]
                dve.tensor_tensor(l[:, 0:DVE_COLS], p[:, 0:DVE_COLS], high(p)[:, 0:DVE_COLS],
                                  ALU.subtract).then_inc(low_ready, 1)

            def take_out(c, u):
                dve.wait_ge(prob_used, c * NGRP + NGRP + PBUF)
                dve.wait_ge(osb_used, c + 1)
                dve.tensor_copy(osb[:, :, :], outp[:, u, 0:SPT * VN]
                                .rearrange("p (j v) -> p j v", v=VN)).then_inc(out_taken, 1)
                dve.wait_ge(out_taken, c + 3)
                dve.reciprocal(rec[:, :], osb[:, :, 2 * DH]).then_inc(rec_ready, 1)

            with dve.Fori(0, NCH // 2) as it:
                for u in range(2):
                    take_turned(it * 2 + u, u)
            for g in range(AHEAD):
                low(0, g)
            def step(c, u, more):
                for g in range(AHEAD, NGRP):
                    low(c, g)
                    if g == 3 and more:
                        take_turned(c + NCH, u)
                if more:
                    for g in range(AHEAD):
                        low(c + 1, g)
                take_out(c, u)

            pairs_of_chunks(dve, step)

        @block.tensor
        def _(pe):
            def turn(i, u):
                pe.wait_ge(stage_in[u], (i // 2) * 16 + 16)
                pe.wait_ge(turned_taken, i + 1)
                for t in range(GT):
                    last = pe.transpose(turned[:, t, :], staged[u][:, t, :], ident16[:, :])
                last.then_inc(turned_ready, 1)

            def score(c, g, buf):
                for i in range(GROUP):
                    last = pe.matmul(scores[buf][:, i * CHUNK:(i + 1) * CHUNK],
                                     kT[:, ds(c // NCH % 2 * S + (g * GROUP + i) * P, P)],
                                     qT[:, ds(c % (2 * NCH) * CHUNK, CHUNK)], start=True, stop=True)
                last.then_inc(score_ready, 1)

            def times_v(c, g, u):
                pe.wait_ge(low_ready, c * NGRP + g + 1)
                pe.wait_ge(lowp_ready, c * NGRP + g + 1)
                for i in range(GROUP):
                    v = vs[:, g * GROUP + i, ds(c // NCH, 1), 0:VN].squeeze(1)
                    for j in range(SPT):
                        cols = slice(i * CHUNK + j * P, i * CHUNK + (j + 1) * P)
                        to = outp[:, u, j * VN:(j + 1) * VN]
                        pe.matmul(to, high(prob[g % PBUF])[:, cols], v, start=(g == 0 and i == 0 and j == 0),
                                  stop=False, skip_group_check=True)
                        last = pe.matmul(to, plow[g % PBUF][:, cols], v, start=False,
                                         stop=(g == NGRP - 1 and i == GROUP - 1), skip_group_check=True)
                last.then_inc(prob_used, 1)

            with pe.Fori(0, NCH // 2) as it:
                for u in range(2):
                    turn(it * 2 + u, u)
            pe.sem_inc(prob_used, PBUF)
            pe.wait_ge(q_const, 1)
            for u in range(2):
                pe.wait_ge(placed[u], PLACE * NCH // 2 + 16)
            for g in range(LOOK):
                if g >= 2:
                    pe.wait_ge(prob_ready, g - 1)
                score(0, g, g % 2)
            def step(c, u, more):
                for g in range(NGRP):
                    n = g + LOOK
                    if n == NGRP and more:
                        pe.wait_ge(placed[u], (c + NCH - u) // 2 * PLACE + PLACE + 16)
                    if n < NGRP or more:
                        pe.wait_ge(prob_ready, c * NGRP + n - 1)
                        score(c + n // NGRP, n % NGRP, n % 2)
                    if g == 0:
                        pe.wait_ge(out_taken, c + 1)
                    times_v(c, g, u)
                    if g == 1 and more:
                        turn(c + NCH, u)

            pairs_of_chunks(pe, step)


E_N = 8
TOP = 2
ET = 256
EH = ET // P
MAXT = (TOP * S + E_N * (ET - 1)) // ET
ROWS = MAXT * ET
BIG = 1e30


def turn_and_split_weights(nc, name, w_dram, rows, cols, ident32, wh, wl):
    RB, CB = rows // P, cols // P
    ctx = ExitStack()
    with ctx:
        sb = lambda name, shape, dt: ctx.enter_context(nc.sbuf_tensor(name, shape, dt))
        wn = sb(name + "turn_wn", [P, RB, cols], F32)
        wt = sb(name + "turn_wt", [P, CB, rows], F32)
        pt = ctx.enter_context(nc.psum_tensor(name + "turn_pt", [P, CB, 512], F32))
        w_in = semaphore(nc, name + "turn_in")
        turned = semaphore(nc, name + "turn_turned")
        scaled = semaphore(nc, name + "turn_scaled")
        halves = semaphore(nc, name + "turn_halves")
        block = ctx.enter_context(nc.Block())

        @block.sync
        def _(sp):
            sp.dma_start(wn[:, :, :], w_dram.rearrange("(m p) c -> p m c", p=P)).then_inc(w_in, 16)

        @block.tensor
        def _(pe):
            pe.wait_ge(w_in, 16)
            for k in range(CB):
                for m in range(RB):
                    last = pe.transpose(pt[:, k, m * P:(m + 1) * P], wn[:, m, k * P:(k + 1) * P], ident32[:, :])
            last.then_inc(turned, 1)

        @block.vector
        def _(dve):
            dve.wait_ge(turned, 1)
            dve.tensor_scalar(wt[:, :, :], pt[:, :, 0:rows], W_SCALE, None, ALU.mult).then_inc(scaled, 1)
            dve.wait_ge(scaled, 1)
            dve.tensor_copy(wh, wt[:, :, :]).then_inc(halves, 1)
            dve.wait_ge(halves, 1)
            dve.tensor_tensor(wl, wt[:, :, :], wh, ALU.subtract).then_inc(halves, 1)
            dve.wait_ge(halves, 2)


def project_attention(nc, x_dram, w_dram, aout, ident32, tok):
    ctx = ExitStack()
    with ctx:
        sb = lambda name, shape, dt: ctx.enter_context(nc.sbuf_tensor(name, shape, dt))
        ps = lambda name, shape: ctx.enter_context(nc.psum_tensor(name, shape, F32))
        sem = lambda name: semaphore(nc, name)
        wh = sb("pj_wh", [P, KB, D], F16)
        wl = sb("pj_wl", [P, KB, D], F16)
        turn_and_split_weights(nc, "pjw", w_dram, D, D, ident32, wh[:, :, :], wl[:, :, :])
        ah = sb("pj_ah", [P, KB, S], F16)
        al = sb("pj_al", [P, KB, S], F16)
        xg = [sb(f"pj_xg{u}", [P, KB, GT * P], F32) for u in range(2)]
        px = [ps(f"pj_px{u}", [P, 512]) for u in range(2)]
        pp = [ps(f"pj_pp{u}", [P, 512]) for u in range(2)]
        x_in = [sem(f"pj_x_in{u}") for u in range(2)]
        x_used = sem("pj_x_used")
        ah_ready = sem("pj_ah_ready")
        al_ready = sem("pj_al_ready")
        pe_ready = sem("pj_pe_ready")
        x_taken = sem("pj_x_taken")
        x_going = sem("pj_x_going")
        summed = sem("pj_summed")
        block = ctx.enter_context(nc.Block())
        AQ = 4
        AC = S // AQ

        @block.sync
        def _(sp):
            src = x_dram.rearrange("b (k p) h w -> p (b k) (h w)", p=P)
            with sp.Fori(0, NG // 2) as it:
                for u in range(2):
                    sp.wait_ge(x_used, it * 2 + u + 1)
                    sp.dma_start(xg[u][:, :, :], src[:, :, ds((it * 2 + u) * GT * P, GT * P)]).then_inc(x_in[u], 16)

        @block.scalar
        def _(act):
            for q in range(AQ):
                act.activation(ah[:, :, q * AC:(q + 1) * AC], aout[:, :, q * AC:(q + 1) * AC], ACT.Copy).then_inc(ah_ready, 1)
            with act.Fori(0, NG // 2) as it:
                for u in range(2 * GT):
                    tile = it * (2 * GT) + u
                    act.wait_ge(pe_ready, tile + 1)
                    act.sem_inc(x_going, 1)
                    act.activation(tok[:, ds(tile, 1), :].squeeze(1), px[u % 2][:, 0:D], ACT.Copy).then_inc(x_taken, 1)

        @block.vector
        def _(dve):
            for q in range(AQ):
                dve.wait_ge(ah_ready, q + 1)
                dve.tensor_tensor(al[:, :, q * AC:(q + 1) * AC], aout[:, :, q * AC:(q + 1) * AC],
                                  ah[:, :, q * AC:(q + 1) * AC], ALU.subtract).then_inc(al_ready, 1)
            dve.sem_inc(summed, 2)
            with dve.Fori(0, NG // 2) as it:
                for u in range(2 * GT):
                    tile = it * (2 * GT) + u
                    dve.wait_ge(x_taken, tile + 1)
                    t = tok[:, ds(tile, 1), :].squeeze(1)
                    dve.scalar_tensor_tensor(out=t, in0=pp[u % 2][:, 0:D], scalar=1.0 / W_SCALE, in1=t,
                                             op0=ALU.mult, op1=ALU.add).then_inc(summed, 1)

        @block.tensor
        def _(pe):
            pe.sem_inc(x_used, 2)
            pe.wait_ge(al_ready, AQ)
            with pe.Fori(0, NG // 2) as it:
                for u in range(2):
                    pe.wait_ge(x_in[u], it * 16 + 16)
                    for t in range(GT):
                        i = u * GT + t
                        tile = it * (2 * GT) + i
                        pe.wait_ge(summed, tile + 1)
                        for k in range(KB):
                            last = pe.transpose(px[i % 2][:, k * P:(k + 1) * P], xg[u][:, k, t * P:(t + 1) * P], ident32[:, :])
                        if t == GT - 1:
                            last.then_inc(x_used, 1)
                        n = 0
                        for k in range(KB):
                            for aa, ww in ((ah, wh), (al, wh), (ah, wl)):
                                last = pe.matmul(pp[i % 2][:, 0:D], aa[:, k, ds(tile * P, P)], ww[:, k, :],
                                                 start=(n == 0), stop=(n == 5))
                                n += 1
                        last.then_inc(pe_ready, 1)


def token_norm(nc, name, tok, eps_value, mean, rstd):
    ctx = ExitStack()
    with ctx:
        sb = lambda n, shape, dt: ctx.enter_context(nc.sbuf_tensor(name + n, shape, dt))
        sem = lambda n: semaphore(nc, name + n)
        stats = sb("stats", [P, NT, 6], F32)
        mv = sb("mv", [P, NT, 2], F32)
        sd = sb("sd", [P, NT], F32)
        eps = sb("eps", [P, 1], F32)
        st = sem("st")
        ag = sem("ag")
        sq = sem("sq")
        out = sem("out")
        block = ctx.enter_context(nc.Block())

        @block.vector
        def _(dve):
            dve.memset(eps[:, :], eps_value).then_inc(st, 1)
            for t in range(NT):
                last = dve.bn_stats(stats[:, t, :], tok[:, t, :])
            last.then_inc(st, 1)
            dve.wait_ge(st, 2)
            for t in range(NT):
                last = dve.bn_aggr(mv[:, t, :], stats[:, t, :])
            last.then_inc(ag, 1)
            dve.wait_ge(ag, 1)
            dve.tensor_copy(mean[:, :], mv[:, :, 0]).then_inc(out, 1)
            dve.wait_ge(sq, 1)
            dve.reciprocal(rstd[:, :], sd[:, :]).then_inc(out, 1)
            dve.wait_ge(out, 2)

        @block.scalar
        def _(act):
            act.wait_ge(ag, 1)
            act.activation(sd[:, :], mv[:, :, 1], ACT.Sqrt, bias=eps[:, 0:1]).then_inc(sq, 1)


def logits_and_rows(nc, name, tok, mean, rstd, gate_dram, gate_by_expert, ident32, logits, rows16, add_norm):
    ctx = ExitStack()
    with ctx:
        sb = lambda n, shape, dt: ctx.enter_context(nc.sbuf_tensor(name + n, shape, dt))
        ps = lambda n, shape: ctx.enter_context(nc.psum_tensor(name + n, shape, F32))
        sem = lambda n: semaphore(nc, name + n)
        gate = sb("gate", [P, KB, E_N], F32)
        xn = [sb(f"xn{u}", [P, D], F32) for u in range(2)]
        xt = [sb(f"xt{u}", [P, D], F32) for u in range(2)]
        pt = [ps(f"pt{u}", [P, 512]) for u in range(2)]
        pl = [ps(f"pl{u}", [P, 512]) for u in range(2)]
        gate_in = sem("gate_in")
        xn_ready = sem("xn_ready")
        hi_ready = sem("hi_ready")
        turned = sem("turned")
        xt_ready = sem("xt_ready")
        multiplied = sem("multiplied")
        taken = sem("taken")
        lo_ready = sem("lo_ready")
        block = ctx.enter_context(nc.Block())

        @block.sync
        def _(sp):
            with nc.allow_non_contiguous_dma(reason="the gate's few weights"):
                src = gate_dram.rearrange("e (k p) -> p k e", p=P) if gate_by_expert else \
                    gate_dram.rearrange("(k p) e -> p k e", p=P)
                for k in range(KB):
                    sp.dma_start(gate[:, k, :], src[:, k, :]).then_inc(gate_in, 16)
            sp.wait_ge(gate_in, 16 * KB)

        @block.vector
        def _(dve):
            def norm(t, u):
                dve.wait_ge(lo_ready, t + 1)
                dve.wait_ge(turned, t + 1)
                dve.tensor_scalar(xn[u][:, :], tok[:, ds(t, 1), :].squeeze(1), mean[:, ds(t, 1)], rstd[:, ds(t, 1)],
                                  ALU.subtract, ALU.mult).then_inc(xn_ready, 1)
                dve.wait_ge(xn_ready, t + 1)
                dve.tensor_copy(rows16[:, ds(t, 1), 0:D].squeeze(1), xn[u][:, :]).then_inc(hi_ready, 1)

            def take(t, u):
                dve.wait_ge(multiplied, t + 3)
                dve.tensor_copy(logits[:, ds(t, 1), :].squeeze(1), pl[u][:, 0:E_N]).then_inc(taken, 1)

            dve.sem_inc(taken, 2)
            norm(0, 0)
            norm(1, 1)
            with dve.Fori(0, NT // 2 - 1) as it:
                for u in range(2):
                    norm(it * 2 + u + 2, u)
                    take(it * 2 + u, u)
            for u in range(2):
                take(NT - 2 + u, u)

        @block.tensor
        def _(pe):
            def turn(t, u):
                pe.wait_ge(xn_ready, t + 1)
                pe.wait_ge(xt_ready, t + 1)
                for k in range(KB):
                    last = pe.transpose(pt[u][:, k * P:(k + 1) * P], xn[u][:, k * P:(k + 1) * P], ident32[:, :])
                last.then_inc(turned, 1)

            def mult(t, u):
                pe.wait_ge(xt_ready, t + 3)
                pe.wait_ge(taken, t + 1)
                for k in range(KB):
                    last = pe.matmul(pl[u][:, 0:E_N], xt[u][:, k * P:(k + 1) * P], gate[:, k, :],
                                     start=(k == 0), stop=(k == KB - 1))
                last.then_inc(multiplied, 1)

            pe.sem_inc(turned, 2)
            pe.sem_inc(multiplied, 2)
            pe.wait_ge(gate_in, 16 * KB)
            turn(0, 0)
            with pe.Fori(0, NT // 2 - 1) as it:
                for u in range(2):
                    turn(it * 2 + u + 1, 1 - u)
                    mult(it * 2 + u, u)
            turn(NT - 1, 1)
            mult(NT - 2, 0)
            mult(NT - 1, 1)

        @block.scalar
        def _(act):
            act.sem_inc(xt_ready, 2)
            with act.Fori(0, NT // 2) as it:
                for u in range(2):
                    t = it * 2 + u
                    act.wait_ge(turned, t + 3)
                    act.wait_ge(multiplied, t + 1)
                    act.activation(xt[u][:, :], pt[u][:, 0:D], ACT.Copy).then_inc(xt_ready, 1)

        @block.gpsimd
        def _(pool):
            pool.sem_inc(lo_ready, 2)
            with pool.Fori(0, NT // 2) as it:
                for u in range(2):
                    t = it * 2 + u
                    pool.wait_ge(hi_ready, t + 1)
                    if add_norm:
                        x = tok[:, ds(t, 1), :].squeeze(1)
                        pool.tensor_tensor(x, x, xn[u][:, :], ALU.add)
                    row = rows16[:, ds(t, 1), :].squeeze(1)
                    pool.tensor_tensor(row[:, D:2 * D], xn[u][:, :], row[:, 0:D], ALU.subtract).then_inc(lo_ready, 1)


def make_routing_constants(nc, below, ones, steps, first, tile_no):
    made = semaphore(nc, "rc_set")
    with nc.Block() as block:
        @block.gpsimd
        def _(pool):
            pool.memset(ones[:, :], 1.0).then_inc(made, 1)
            pool.wait_ge(made, 1)
            pool.affine_select(out=below[:, :], in_=ones[:, :], compare_op=ALU.is_gt, fill=0.0, base=0,
                               pattern=[[1, P]], channel_multiplier=-1).then_inc(made, 1)
            pool.iota(steps[:, :], pattern=[[ET, S // ET]], base=0, channel_multiplier=0,
                      allow_small_or_imprecise_dtypes=True).then_inc(made, 1)
            pool.iota(first[:, :], pattern=[[-1, E_N]], base=E_N, channel_multiplier=0,
                      allow_small_or_imprecise_dtypes=True).then_inc(made, 1)
            pool.iota(tile_no[:, :], pattern=[[1, MAXT]], base=0, channel_multiplier=0,
                      allow_small_or_imprecise_dtypes=True).then_inc(made, 1)
            pool.wait_ge(made, 5)


def route(nc, name, logits, by_probs, gate_bias_dram, consts, weights, slots, tile_expert):
    below, ones, steps, first, tile_no = consts
    ctx = ExitStack()
    with ctx:
        sb = lambda n, shape, dt=F32: ctx.enter_context(nc.sbuf_tensor(name + n, shape, dt))
        sem = lambda n: semaphore(nc, name + n)
        A = [P, NT, E_N]
        val = sb("val", A)
        tmp = sb("tmp", A)
        tmp2 = sb("tmp2", A)
        hot = [sb(f"hot{i}", A) for i in range(TOP)]
        best = [sb(f"best{i}", [P, NT]) for i in range(TOP)]
        r1 = sb("r1", [P, NT])
        mask = sb("mask", A, F16)
        tot = [sb(f"tot{i}", A) for i in range(2)]
        cnt = sb("cnt", [P, E_N])
        over = sb("over", [P, E_N, S // ET])
        tiles = [sb(f"tiles{i}", [P, E_N]) for i in range(2)]
        start = sb("start", [P, E_N])
        stop = sb("stop", [P, E_N])
        past = sb("past", [P, MAXT, E_N])
        owner = sb("owner", [P, MAXT])
        bias = sb("bias", [P, E_N])
        pc = ctx.enter_context(nc.psum_tensor(name + "pc", [P, 512], F32))
        pt = ctx.enter_context(nc.psum_tensor(name + "pt", [P, 512], F32))
        step = sem("step")
        exped = sem("exped")
        summed = sem("summed")
        bias_in = sem("bias_in")
        marks = {}
        block = ctx.enter_context(nc.Block())

        @block.sync
        def _(sp):
            if gate_bias_dram is not None:
                sp.dma_start(bias[:, :], gate_bias_dram.partition_broadcast(P)).then_inc(bias_in, 16)
                sp.wait_ge(bias_in, 16)

        @block.vector
        def _(dve):
            n = 0

            def link(ins):
                nonlocal n
                n += 1
                ins.then_inc(step, 1)
                dve.wait_ge(step, n)
                return n

            per_tile = lambda x: x[:, :].unsqueeze(2).broadcast_to(A)
            per_expert = lambda x: x[:, :].unsqueeze(1).broadcast_to(A)
            if gate_bias_dram is not None:
                dve.wait_ge(bias_in, 16)
                link(dve.tensor_tensor(val[:, :, :], logits[:, :, :], per_expert(bias), ALU.add))
            if by_probs:
                link(dve.tensor_reduce(r1[:, :], logits[:, :, :], AX.X, ALU.max))
                marks["shifted"] = link(dve.tensor_tensor(val[:, :, :], logits[:, :, :], per_tile(r1), ALU.subtract))
                dve.wait_ge(exped, 1)
                link(dve.tensor_reduce(r1[:, :], val[:, :, :], AX.X, ALU.add))
                link(dve.reciprocal(r1[:, :], r1[:, :]))
                link(dve.tensor_tensor(val[:, :, :], val[:, :, :], per_tile(r1), ALU.mult))
            for i in range(TOP):
                link(dve.tensor_reduce(best[i][:, :], val[:, :, :], AX.X, ALU.max))
                link(dve.tensor_tensor(tmp[:, :, :], val[:, :, :], per_tile(best[i]), ALU.is_equal))
                link(dve.tensor_tensor(tmp[:, :, :], tmp[:, :, :], per_expert(first), ALU.mult))
                link(dve.tensor_reduce(r1[:, :], tmp[:, :, :], AX.X, ALU.max))
                link(dve.tensor_tensor(hot[i][:, :, :], per_expert(first), per_tile(r1), ALU.is_equal))
                if i == 0:
                    link(dve.tensor_scalar(tmp2[:, :, :], hot[0][:, :, :], -BIG, None, ALU.mult))
                    link(dve.tensor_tensor(val[:, :, :], val[:, :, :], tmp2[:, :, :], ALU.add))
            marks["mask"] = link(dve.tensor_tensor(mask[:, :, :], hot[0][:, :, :], hot[1][:, :, :], ALU.add))
            w = weights
            if by_probs:
                link(dve.tensor_tensor(r1[:, :], best[0][:, :], best[1][:, :], ALU.add))
                link(dve.tensor_scalar(r1[:, :], r1[:, :], 1e-12, None, ALU.max))
                link(dve.reciprocal(r1[:, :], r1[:, :]))
                link(dve.tensor_tensor(w[0][:, :], best[0][:, :], r1[:, :], ALU.mult))
                link(dve.tensor_tensor(w[1][:, :], best[1][:, :], r1[:, :], ALU.mult))
            else:
                marks["gap"] = link(dve.tensor_tensor(r1[:, :], best[1][:, :], best[0][:, :], ALU.subtract))
                dve.wait_ge(exped, 1)
                link(dve.tensor_scalar(w[0][:, :], r1[:, :], 1.0, None, ALU.add))
                link(dve.reciprocal(w[0][:, :], w[0][:, :]))
                link(dve.tensor_tensor(w[1][:, :], w[0][:, :], r1[:, :], ALU.mult))
            dve.wait_ge(summed, 1)
            link(dve.tensor_copy(tot[0][:, :, :], pt[:, 0:NT * E_N].rearrange("p (t e) -> p t e", e=E_N)))
            a, d = 0, 1
            while d < NT:
                dve.tensor_copy(tot[1 - a][:, 0:d, :], tot[a][:, 0:d, :])
                link(dve.tensor_tensor(tot[1 - a][:, d:NT, :], tot[a][:, d:NT, :], tot[a][:, 0:NT - d, :], ALU.add))
                a, d = 1 - a, 2 * d
            incl = tot[a]
            link(dve.tensor_copy(cnt[:, :], incl[:, NT - 1, :]))
            OV = [P, E_N, S // ET]
            link(dve.tensor_tensor(over[:, :, :], cnt[:, :].unsqueeze(2).broadcast_to(OV),
                                   steps[:, :].unsqueeze(1).broadcast_to(OV), ALU.is_gt))
            link(dve.tensor_reduce(tiles[0][:, :], over[:, :, :], AX.X, ALU.add))
            link(dve.tensor_scalar(cnt[:, :], tiles[0][:, :], 1.0, None, ALU.mult))
            b, d = 0, 1
            while d < E_N:
                dve.tensor_copy(tiles[1 - b][:, 0:d], tiles[b][:, 0:d])
                link(dve.tensor_tensor(tiles[1 - b][:, d:E_N], tiles[b][:, d:E_N], tiles[b][:, 0:E_N - d], ALU.add))
                b, d = 1 - b, 2 * d
            link(dve.tensor_copy(stop[:, :], tiles[b][:, :]))
            link(dve.tensor_tensor(start[:, :], stop[:, :], cnt[:, :], ALU.subtract))
            link(dve.tensor_scalar(start[:, :], start[:, :], float(ET), None, ALU.mult))
            OW = [P, MAXT, E_N]
            link(dve.tensor_tensor(past[:, :, :], tile_no[:, :].unsqueeze(2).broadcast_to(OW),
                                   stop[:, :].unsqueeze(1).broadcast_to(OW), ALU.is_ge))
            link(dve.tensor_reduce(owner[:, :], past[:, :, :], AX.X, ALU.add))
            link(dve.tensor_scalar(tile_expert[:, :], owner[:, :], float(E_N - 1), None, ALU.min))
            link(dve.tensor_tensor(tmp[:, :, :], pc[:, 0:NT * E_N].rearrange("p (t e) -> p t e", e=E_N), per_expert(start),
                                   ALU.add))
            link(dve.tensor_tensor(tmp[:, 1:NT, :], tmp[:, 1:NT, :], incl[:, 0:NT - 1, :], ALU.add))
            for i in range(TOP):
                link(dve.tensor_tensor(tmp2[:, :, :], tmp[:, :, :], hot[i][:, :, :], ALU.mult))
                link(dve.tensor_reduce(r1[:, :], tmp2[:, :, :], AX.X, ALU.add))
                link(dve.tensor_copy(slots[i][:, :], r1[:, :]))

        @block.scalar
        def _(act):
            if by_probs:
                act.wait_ge(step, marks["shifted"])
                act.activation(val[:, :, :], val[:, :, :], ACT.Exp).then_inc(exped, 1)
            else:
                act.wait_ge(step, marks["gap"])
                act.activation(r1[:, :], r1[:, :], ACT.Exp).then_inc(exped, 1)

        @block.tensor
        def _(pe):
            m = mask[:, :, :].rearrange("p t e -> p (t e)")
            pe.wait_ge(step, marks["mask"])
            pe.matmul(pt[:, 0:NT * E_N], ones[:, :], m, start=True, stop=True)
            pe.matmul(pc[:, 0:NT * E_N], below[:, :], m, start=True, stop=True).then_inc(summed, 1)


def experts(nc, name, F, w1, shared, rows16, slots, w1_dram, b1_dram, w2_dram, b2_dram, sorted_dram, y_dram, tile_expert, ident16, ident32):
    NF = F // P
    ctx = ExitStack()
    with ctx:
        sb = lambda n, shape, dt: ctx.enter_context(nc.sbuf_tensor(name + n, shape, dt))
        ps = lambda n, shape, dt=F32: ctx.enter_context(nc.psum_tensor(name + n, shape, dt))
        sem = lambda n: semaphore(nc, name + n)
        w1h, w1l = w1[:, :, 0], w1[:, :, 1]
        w2h = sb("w2h", [P, E_N, NF, D], F16)
        w2l = sb("w2l", [P, E_N, NF, D], F16)
        b1t = sb("b1t", [P, E_N, NF], F32)
        b2h = sb("b2h", [1, E_N, D], F16)
        b2l = sb("b2l", [1, E_N, D], F16)
        one = sb("one", [1, P], F16)

        with ExitStack() as c2:
            WC = KB * F
            stg = [c2.enter_context(nc.sbuf_tensor(name + f"stg{u}", [P, WC], F32)) for u in range(3)]
            b1n = c2.enter_context(nc.sbuf_tensor(name + "b1n", [E_N * NF, P], F32))
            b2n = c2.enter_context(nc.sbuf_tensor(name + "b2n", [1, E_N, D], F32))
            pb = c2.enter_context(nc.psum_tensor(name + "pb", [P, 512], F32))
            w_in = [semaphore(nc, name + f"w_in{u}") for u in range(3)]
            b_in = semaphore(nc, name + "b_in")
            b_turned = semaphore(nc, name + "b_turned")
            scaled = semaphore(nc, name + "scaled")
            split = semaphore(nc, name + "split")
            bstep = semaphore(nc, name + "bstep")
            sent = semaphore(nc, name + "sent")
            block = c2.enter_context(nc.Block())
            w1_part = lambda e: (w1_dram[e].rearrange("(k p) f -> p k f", p=P), w1h[:, e], w1l[:, e], KB, F)
            parts = [w1_part(e) for e in range(shared)]
            parts += [(w2_dram[e].rearrange("(n p) d -> p n d", p=P), w2h[:, e], w2l[:, e], NF, D) for e in range(E_N)]
            parts += [w1_part(e) for e in range(shared, E_N)]

            @block.gpsimd
            def _(pool):
                for t in range(NT):
                    for i in range(TOP):
                        pool.indirect_dma_start(out=sorted_dram, out_offset=bass.IndirectOffsetOnAxis(ap=slots[i][:, t:t + 1], axis=0),
                                                in_=rows16[:, t, :], in_offset=None).then_inc(sent, 16)
                pool.wait_ge(sent, 16 * NT * TOP)

            @block.sync
            def _(sp):
                sp.dma_start(b1n[:, :], b1_dram.rearrange("e (n p) -> (e n) p", p=P)).then_inc(b_in, 16)
                sp.dma_start(b2n[0:1, :, :], b2_dram.rearrange("(a e) d -> a e d", a=1)).then_inc(b_in, 16)
                for i, (src, _, _, a, b) in enumerate(parts):
                    if i >= 3:
                        sp.wait_ge(split, i - 2)
                    sp.dma_start(stg[i % 3][:, :].rearrange("p (a b) -> p a b", b=b), src).then_inc(w_in[i % 3], 16)

            @block.scalar
            def _(act):
                for i, (_, hi, lo, a, b) in enumerate(parts):
                    act.wait_ge(w_in[i % 3], 16 * (i // 3 + 1))
                    if i == shared + E_N:
                        act.wait_ge(sent, 16 * NT * TOP)
                    act.activation(hi, stg[i % 3][:, :].rearrange("p (a b) -> p a b", b=b), ACT.Copy,
                                   scale=W_SCALE).then_inc(scaled, 1)

            @block.vector
            def _(dve):
                dve.wait_ge(b_in, 32)
                dve.memset(one[:, :], 1.0).then_inc(bstep, 1)
                dve.tensor_scalar(b2n[:, :, :], b2n[:, :, :], W_SCALE, None, ALU.mult).then_inc(bstep, 1)
                dve.wait_ge(bstep, 2)
                dve.tensor_copy(b2h[:, :, :], b2n[:, :, :]).then_inc(bstep, 1)
                dve.wait_ge(bstep, 3)
                dve.tensor_tensor(b2l[:, :, :], b2n[:, :, :], b2h[:, :, :], ALU.subtract).then_inc(bstep, 1)
                dve.wait_ge(b_turned, 1)
                dve.tensor_copy(b1t[:, :, :], pb[:, 0:E_N * NF].rearrange("p (e n) -> p e n", n=NF)).then_inc(bstep, 1)
                for i, (_, hi, lo, a, b) in enumerate(parts):
                    dve.wait_ge(scaled, i + 1)
                    dve.scalar_tensor_tensor(out=lo, in0=stg[i % 3][:, :].rearrange("p (a b) -> p a b", b=b),
                                             scalar=W_SCALE, in1=hi, op0=ALU.mult, op1=ALU.subtract).then_inc(split, 1)
                dve.wait_ge(bstep, 5)

            @block.tensor
            def _(pe):
                pe.wait_ge(b_in, 32)
                pe.transpose(pb[:, 0:E_N * NF], b1n[:, :], ident32[0:E_N * NF, 0:E_N * NF]).then_inc(b_turned, 1)

        xr = [sb(f"xr{u}", [P, EH, 2 * D], F16) for u in range(2)]
        xT = [sb(f"xT{u}", [P, 2 * KB, ET], F16) for u in range(2)]
        b1c = [sb(f"b1c{u}", [P, NF], F32) for u in range(2)]
        hf = [sb(f"hf{u}", [P, ET], F32) for u in range(4)]
        hh = [sb(f"hh{u}", [P, NF, ET], F16) for u in range(2)]
        hl = [sb(f"hl{u}", [P, NF, ET], F16) for u in range(2)]
        yo = [sb(f"yo{u}", [P, EH, D], F32) for u in range(2)]
        px = [ps(f"px{u}", [P, 2 * KB, ET], F16) for u in range(2)]
        ph = [ps(f"ph{u}", [P, 512]) for u in range(4)]
        py = [ps(f"py{u}", [P, 512]) for u in range(2)]
        x_in = [sem(f"x_in{u}") for u in range(2)]
        turned = sem("turned")
        xt_ready = sem("xt_ready")
        h_ready = sem("h_ready")
        act_ready = sem("act_ready")
        b1_ready = sem("b1_ready")
        hh_ready = sem("hh_ready")
        hl_ready = sem("hl_ready")
        y_ready = sem("y_ready")
        y_taken = sem("y_taken")
        y_out = [sem(f"y_out{u}") for u in range(2)]
        block = ctx.enter_context(nc.Block())
        BODY = (MAXT - 2) // 2 * 2

        def pipelined(eng, step, *args):
            with eng.Fori(0, BODY // 2) as it:
                for u in range(2):
                    step(it * 2 + u, u, it, True, True, *args)
            for i in range(BODY, MAXT):
                step(i, i % 2, i // 2, i + 1 < MAXT, i + 2 < MAXT, *args)

        def expert_of(eng, reg, i):
            eng.reg_load(reg, tile_expert[0:1, ds(i, 1)])
            return eng.snap(reg, min_val=0, max_val=E_N - 1)

        @block.sync
        def _(sp):
            def load(i, u):
                sp.wait_ge(turned, i + 1)
                sp.dma_start(xr[u][:, :, :], sorted_dram[ds(i * ET, ET), :].rearrange("(h p) c -> p h c", p=P)
                             ).then_inc(x_in[u], 16)

            def step(i, u, it, one_more, two_more):
                if two_more:
                    load(i + 2, u)

            for u in range(2):
                sp.sem_inc(y_out[u], 16)
                load(u, u)
            pipelined(sp, step)

        @block.tensor
        def _(pe):
            reg = pe.alloc_register(name + "pe_expert")

            def turn(i, u, it):
                pe.wait_ge(x_in[u], it * 16 + 16)
                pe.wait_ge(xt_ready, i + 1)
                for q in range(2 * KB):
                    for h in range(EH):
                        last = pe.transpose(px[u][:, q, h * P:(h + 1) * P], xr[u][:, h, q * P:(q + 1) * P], ident16[:, :])
                last.then_inc(turned, 1)

            def first(i, u):
                e = expert_of(pe, reg, i)
                pe.wait_ge(xt_ready, i + 3)
                for f in range(NF):
                    pe.wait_ge(act_ready, i * NF + f + 1)
                    k6 = 0
                    for k in range(KB):
                        for w, x in ((w1h, k), (w1h, KB + k), (w1l, k)):
                            last = pe.matmul(ph[(u * NF + f) % 4][:, 0:ET],
                                             w[:, ds(e, 1), k, f * P:(f + 1) * P].squeeze(1), xT[u][:, x, :],
                                             start=(k6 == 0), stop=(k6 == 3 * KB - 1))
                            k6 += 1
                    last.then_inc(h_ready, 1)

            def second(i, u):
                e = expert_of(pe, reg, i)
                for h in range(EH):
                    pe.wait_ge(y_taken, i * EH + h + 1)
                    to = py[h % 2][:, 0:D]
                    c = slice(h * P, (h + 1) * P)
                    for f in range(NF):
                        if h == 0:
                            pe.wait_ge(hl_ready, i * NF + f + 5)
                        wh_e = w2h[:, ds(e, 1), f, :].squeeze(1)
                        pe.matmul(to, hh[u][:, f, c], wh_e, start=(f == 0), stop=False)
                        pe.matmul(to, hl[u][:, f, c], wh_e, start=False, stop=False)
                        pe.matmul(to, hh[u][:, f, c], w2l[:, ds(e, 1), f, :].squeeze(1), start=False, stop=False)
                    pe.matmul(to, one[0:1, :], b2h[0:1, ds(e, 1), :].squeeze(1), start=False, stop=False)
                    last = pe.matmul(to, one[0:1, :], b2l[0:1, ds(e, 1), :].squeeze(1), start=False, stop=True)
                    last.then_inc(y_ready, 1)

            def step(i, u, it, one_more, two_more):
                if two_more:
                    turn(i + 2, u, it + 1)
                if one_more:
                    first(i + 1, 1 - u)
                second(i, u)

            pe.sem_inc(turned, 2)
            pe.sem_inc(y_ready, 2 * EH)
            turn(0, 0, 0)
            turn(1, 1, 0)
            first(0, 0)
            pipelined(pe, step)

        @block.scalar
        def _(act):
            def gelus(i, u):
                act.wait_ge(xt_ready, i + 3)
                for f in range(NF):
                    b = (u * NF + f) % 4
                    act.wait_ge(h_ready, i * NF + f + 1)
                    act.wait_ge(hl_ready, i * NF + f + 1)
                    act.activation(hf[b][:, :], ph[b][:, 0:ET], ACT.Gelu, bias=b1c[u][:, f:f + 1],
                                   scale=1.0 / W_SCALE).then_inc(act_ready, 1)

            def step(i, u, it, one_more, two_more):
                if one_more:
                    gelus(i + 1, 1 - u)
                act.wait_ge(y_out[u], it * 16 + 16)
                for h in range(EH):
                    act.wait_ge(y_ready, i * EH + h + 1 + 2 * EH)
                    act.activation(yo[u][:, h, :], py[h % 2][:, 0:D], ACT.Copy, scale=1.0 / W_SCALE).then_inc(y_taken, 1)
                act.wait_ge(y_taken, i * EH + EH + 2)
                act.dma_start(y_dram[ds(i * ET, ET), :].rearrange("(h p) c -> p h c", p=P), yo[u][:, :, :]
                              ).then_inc(y_out[u], 16)

            act.sem_inc(act_ready, 4)
            act.sem_inc(y_taken, 2)
            gelus(0, 0)
            pipelined(act, step)
            act.wait_ge(y_out[0], 16 * ((MAXT + 1) // 2 + 1))
            act.wait_ge(y_out[1], 16 * (MAXT // 2 + 1))

        @block.vector
        def _(dve):
            reg = dve.alloc_register(name + "dve_expert")

            def take_x(i, u):
                e = expert_of(dve, reg, i)
                dve.wait_ge(turned, i + 3)
                dve.tensor_copy(b1c[u][:, :], b1t[:, ds(e, 1), :].squeeze(1))
                dve.tensor_copy(xT[u][:, :, :], px[u][:, :, :]).then_inc(xt_ready, 1)

            def highs(i, u):
                dve.wait_ge(y_ready, i * EH + EH)
                for f in range(NF):
                    dve.wait_ge(act_ready, i * NF + f + 5)
                    dve.tensor_copy(hh[u][:, f, :], hf[(u * NF + f) % 4][:, :]).then_inc(hh_ready, 1)

            def step(i, u, it, one_more, two_more):
                if two_more:
                    take_x(i + 2, u)
                if one_more:
                    highs(i + 1, 1 - u)

            dve.sem_inc(xt_ready, 2)
            take_x(0, 0)
            take_x(1, 1)
            highs(0, 0)
            pipelined(dve, step)

        @block.gpsimd
        def _(pool):
            def lows(i, u):
                for f in range(NF):
                    pool.wait_ge(hh_ready, i * NF + f + 1)
                    pool.tensor_tensor(hl[u][:, f, :], hf[(u * NF + f) % 4][:, :], hh[u][:, f, :],
                                       ALU.subtract).then_inc(hl_ready, 1)

            def step(i, u, it, one_more, two_more):
                if one_more:
                    lows(i + 1, 1 - u)

            pool.sem_inc(hl_ready, 4)
            lows(0, 0)
            pipelined(pool, step)


def combine_experts(nc, name, tok, slots, weights, y_dram):
    NB = 8
    ctx = ExitStack()
    with ctx:
        got = [ctx.enter_context(nc.sbuf_tensor(name + f"got{b}", [P, D], F32)) for b in range(NB)]
        arrived = [semaphore(nc, name + f"arrived{b}") for b in range(NB)]
        added = semaphore(nc, name + "added")
        block = ctx.enter_context(nc.Block())

        @block.gpsimd
        def _(pool):
            for n in range(NT * TOP):
                if n >= NB:
                    pool.wait_ge(added, n - NB + 1)
                pool.indirect_dma_start(out=got[n % NB][:, :], out_offset=None, in_=y_dram,
                                        in_offset=bass.IndirectOffsetOnAxis(ap=slots[n % TOP][:, n // TOP:n // TOP + 1], axis=0)
                                        ).then_inc(arrived[n % NB], 16)

        @block.vector
        def _(dve):
            for n in range(NT * TOP):
                t = n // TOP
                dve.wait_ge(arrived[n % NB], 16 * (n // NB + 1))
                if n:
                    dve.wait_ge(added, n)
                dve.scalar_tensor_tensor(out=tok[:, t, :], in0=got[n % NB][:, :], scalar=weights[n % TOP][:, t:t + 1],
                                         in1=tok[:, t, :], op0=ALU.mult, op1=ALU.add).then_inc(added, 1)


def moe(nc, name, tok, F, by_probs, gate, gate_by_expert, gate_bias, w1, b1, w2, b2, sorted_dram, y_dram,
        ident16, ident32, consts, add_norm):
    ctx = ExitStack()
    with ctx:
        sb = lambda n, shape, dt=F32: ctx.enter_context(nc.sbuf_tensor(name + n, shape, dt))
        weights = [sb(f"share{i}", [P, NT]) for i in range(TOP)]
        slots = [sb(f"slot{i}", [P, NT], I32) for i in range(TOP)]
        tile_expert = sb("tile_expert", [P, MAXT], I32)
        w1_halves = sb("w1", [P, E_N, 2, KB, F], F16)
        shared = E_N - -(-NT * 2 * D // (2 * KB * F))
        if shared > 0:
            rows16 = w1_halves[:, shared:E_N].rearrange("p e i k f -> p (e i k f)").rearrange("p (t c) -> p t c", t=NT)
        else:
            shared = E_N
            rows16 = sb("rows16", [P, NT, 2 * D], F16)
        with nc.sbuf_tensor(name + "mean", [P, NT], F32) as mean, nc.sbuf_tensor(name + "rstd", [P, NT], F32) as rstd, \
                nc.sbuf_tensor(name + "logits", [P, NT, E_N], F32) as logits:
            token_norm(nc, name + "n", tok, LN_T_EPS, mean, rstd)
            logits_and_rows(nc, name + "l", tok, mean, rstd, gate, gate_by_expert, ident32, logits, rows16, add_norm)
            route(nc, name + "r", logits, by_probs, gate_bias, consts, weights, slots, tile_expert)
        experts(nc, name + "e", F, w1_halves, shared, rows16, slots, w1, b1, w2, b2, sorted_dram, y_dram, tile_expert, ident16, ident32)
        combine_experts(nc, name + "c", tok, slots, weights, y_dram)

M_KEYS = S // 4
MT = M_KEYS // P
C1 = 128
R1 = S // C1


def tokens_to_channels(nc, name, tok, mean, rstd, bias_dram, ident32, xc):
    ctx = ExitStack()
    with ctx:
        sb = lambda n, shape, dt=F32: ctx.enter_context(nc.sbuf_tensor(name + n, shape, dt))
        sem = lambda n: semaphore(nc, name + n)
        xn = [sb(f"xn{u}", [P, D]) for u in range(2)]
        bias = sb("bias", [P, D])
        pt = [ctx.enter_context(nc.psum_tensor(name + f"pt{u}", [P, 512], F32)) for u in range(2)]
        bias_in = sem("bias_in")
        xn_ready = sem("xn_ready")
        turned = sem("turned")
        taken = sem("taken")
        going = sem("going")
        added = sem("added")
        plus = sem("plus")
        pool_going = sem("pool_going")
        sum_ = [sb(f"sum{u}", [P, D]) for u in range(2)]
        block = ctx.enter_context(nc.Block())

        @block.sync
        def _(sp):
            sp.dma_start(bias[:, :], bias_dram.partition_broadcast(P)).then_inc(bias_in, 16)

        @block.vector
        def _(dve):
            with dve.Fori(0, NT // 2) as it:
                for u in range(2):
                    t = it * 2 + u
                    dve.wait_ge(turned, t + 1)
                    dve.wait_ge(added, t + 1)
                    dve.tensor_scalar(xn[u][:, :], tok[:, ds(t, 1), :].squeeze(1), mean[:, ds(t, 1)], rstd[:, ds(t, 1)],
                                      ALU.subtract, ALU.mult).then_inc(xn_ready, 1)

        @block.gpsimd
        def _(pool):
            pool.sem_inc(added, 2)
            pool.wait_ge(bias_in, 16)
            with pool.Fori(0, NT // 2) as it:
                for u in range(2):
                    t = it * 2 + u
                    x = tok[:, ds(t, 1), :].squeeze(1)
                    pool.wait_ge(added, t + 1)
                    pool.wait_ge(xn_ready, t + 1)
                    pool.tensor_tensor(sum_[u][:, :], xn[u][:, :], bias[:, :], ALU.add).then_inc(plus, 1)
                    pool.wait_ge(plus, t + 1)
                    pool.sem_inc(pool_going, 1)
                    pool.tensor_tensor(x, x, sum_[u][:, :], ALU.add).then_inc(added, 1)

        @block.tensor
        def _(pe):
            pe.sem_inc(turned, 2)
            with pe.Fori(0, NT // 2) as it:
                for u in range(2):
                    t = it * 2 + u
                    pe.wait_ge(xn_ready, t + 1)
                    pe.wait_ge(taken, t + 1)
                    for k in range(KB):
                        last = pe.transpose(pt[u][:, k * P:(k + 1) * P], xn[u][:, k * P:(k + 1) * P], ident32[:, :])
                    last.then_inc(turned, 1)

        @block.scalar
        def _(act):
            act.sem_inc(taken, 2)
            with act.Fori(0, NT // 2) as it:
                for u in range(2):
                    t = it * 2 + u
                    act.wait_ge(turned, t + 3)
                    act.sem_inc(going, 1)
                    act.activation(xc[:, :, ds(t * P, P)], pt[u][:, 0:D].rearrange("p (k s) -> p k s", k=KB),
                                   ACT.Copy).then_inc(taken, 1)


def keys_and_queries(nc, xc, tw, pw, gw, tb_dram, pb_dram, gb_dram, qh, ql, kh, kl, gh, gl):
    ctx = ExitStack()
    with ctx:
        sb = lambda n, shape, dt=F32: ctx.enter_context(nc.sbuf_tensor("kq_" + n, shape, dt))
        sem = lambda n: semaphore(nc, "kq_" + n)
        xh = sb("xh", [P, KB, S], F16)
        xl = sb("xl", [P, KB, S], F16)
        half = sb("half", [P, KB, HW // 2, HW])
        xp = sb("xp", [P, KB, M_KEYS])
        xph = sb("xph", [P, KB, M_KEYS], F16)
        xpl = sb("xpl", [P, KB, M_KEYS], F16)
        tbias = sb("tbias", [P, 1])
        pbias = sb("pbias", [P, 1])
        gbias = sb("gbias", [P, C1])
        thf = [sb(f"thf{u}", [P, CHUNK]) for u in range(2)]
        phf = sb("phf", [P, M_KEYS])
        gf = sb("gf", [P, MT, C1])
        pth = [ctx.enter_context(nc.psum_tensor(f"kq_pth{u}", [P, 512], F32)) for u in range(2)]
        pph = ctx.enter_context(nc.psum_tensor("kq_pph", [P, 2, 512], F32))
        pg = ctx.enter_context(nc.psum_tensor("kq_pg", [P, 2, 512], F32))
        b_in = sem("b_in")
        xh_ready = sem("xh_ready")
        xl_ready = sem("xl_ready")
        pooled = sem("pooled")
        p_halves = sem("p_halves")
        th_ready = sem("th_ready")
        thf_ready = sem("thf_ready")
        qh_ready = sem("qh_ready")
        ql_ready = sem("ql_ready")
        ph_ready = sem("ph_ready")
        phf_ready = sem("phf_ready")
        g_ready = sem("g_ready")
        gstep = sem("gstep")
        block = ctx.enter_context(nc.Block())
        XQ = 4
        XC = S // XQ
        JQ = S // CHUNK

        @block.sync
        def _(sp):
            with nc.allow_non_contiguous_dma(reason="one bias for a partition"):
                sp.dma_start(tbias[:, :], tb_dram.rearrange("(p a) -> p a", a=1)).then_inc(b_in, 16)
                sp.dma_start(pbias[:, :], pb_dram.rearrange("(p a) -> p a", a=1)).then_inc(b_in, 16)
            sp.dma_start(gbias[:, :], gb_dram.partition_broadcast(P)).then_inc(b_in, 16)

        @block.scalar
        def _(act):
            for q in range(XQ):
                act.activation(xh[:, :, q * XC:(q + 1) * XC], xc[:, :, q * XC:(q + 1) * XC], ACT.Copy).then_inc(xh_ready, 1)
            act.wait_ge(b_in, 48)
            for m in range(2):
                act.wait_ge(ph_ready, m + 1)
                act.activation(phf[:, m * 512:(m + 1) * 512], pph[:, m, :], ACT.Identity, bias=pbias[:, 0:1],
                               scale=1.0 / W_SCALE).then_inc(phf_ready, 1)
            with act.Fori(0, JQ // 2) as it:
                for u in range(2):
                    j = it * 2 + u
                    act.wait_ge(th_ready, j + 1)
                    act.wait_ge(ql_ready, j + 1)
                    act.activation(thf[u][:, :], pth[u][:, :], ACT.Identity, bias=tbias[:, 0:1],
                                   scale=1.0 / W_SCALE).then_inc(thf_ready, 1)

        @block.vector
        def _(dve):
            rows = xc[:, :, :].rearrange("p k (y a x) -> p k y a x", a=2, x=HW)
            dve.tensor_tensor(half[:, :, :, :], rows[:, :, :, 0, :], rows[:, :, :, 1, :], ALU.max).then_inc(pooled, 1)
            dve.wait_ge(pooled, 1)
            cols = half[:, :, :, :].rearrange("p k y (x a) -> p k (y x) a", a=2)
            dve.tensor_tensor(xp[:, :, :], cols[:, :, :, 0], cols[:, :, :, 1], ALU.max).then_inc(pooled, 1)
            dve.wait_ge(pooled, 2)
            dve.tensor_copy(xph[:, :, :], xp[:, :, :]).then_inc(p_halves, 1)
            dve.wait_ge(p_halves, 1)
            dve.tensor_tensor(xpl[:, :, :], xp[:, :, :], xph[:, :, :], ALU.subtract).then_inc(p_halves, 1)
            for q in range(XQ):
                dve.wait_ge(xh_ready, q + 1)
                dve.tensor_tensor(xl[:, :, q * XC:(q + 1) * XC], xc[:, :, q * XC:(q + 1) * XC],
                                  xh[:, :, q * XC:(q + 1) * XC], ALU.subtract).then_inc(xl_ready, 1)
            dve.wait_ge(b_in, 48)
            for m in range(2):
                dve.wait_ge(g_ready, m + 1)
                dve.scalar_tensor_tensor(out=gf[:, m * 4:m * 4 + 4, :], in0=pg[:, m, :].rearrange("p (a c) -> p a c", c=C1),
                                         scalar=1.0 / W_SCALE, in1=gbias[:, :].unsqueeze(1).broadcast_to([P, 4, C1]),
                                         op0=ALU.mult, op1=ALU.add).then_inc(gstep, 1)
            dve.wait_ge(gstep, 2)
            dve.tensor_copy(gh[:, :, :], gf[:, :, :]).then_inc(gstep, 1)
            dve.wait_ge(gstep, 3)
            dve.tensor_tensor(gl[:, :, :], gf[:, :, :], gh[:, :, :], ALU.subtract).then_inc(gstep, 1)
            dve.wait_ge(phf_ready, 2)
            dve.tensor_copy(kh[:, :], phf[:, :]).then_inc(gstep, 1)
            dve.wait_ge(gstep, 5)
            dve.tensor_tensor(kl[:, :], phf[:, :], kh[:, :], ALU.subtract).then_inc(gstep, 1)
            with dve.Fori(0, JQ // 2) as it:
                for u in range(2):
                    j = it * 2 + u
                    dve.wait_ge(thf_ready, j + 1)
                    to = lambda q: q[:, :].rearrange("p (r i) -> p i r", r=R1)[:, ds(j * (CHUNK // R1), CHUNK // R1), :]
                    src = thf[u][:, :].rearrange("p (i r) -> p i r", r=R1)
                    dve.tensor_copy(to(qh), src).then_inc(qh_ready, 1)
                    dve.wait_ge(qh_ready, j + 1)
                    dve.tensor_tensor(to(ql), src, to(qh), ALU.subtract).then_inc(ql_ready, 1)
            dve.wait_ge(gstep, 6)
            dve.wait_ge(ql_ready, JQ + 2)

        @block.tensor
        def _(pe):
            def three(to, pairs, inc):
                n = 0
                for lhs, rhs in pairs:
                    last = pe.matmul(to, lhs, rhs, start=(n == 0), stop=(n == len(pairs) - 1))
                    n += 1
                return last

            pe.sem_inc(ql_ready, 2)
            pe.wait_ge(p_halves, 2)
            for m in range(2):
                c = slice(m * 512, (m + 1) * 512)
                last = three(pph[:, m, :], [x for k in range(KB) for x in
                                            ((pw[0][:, k, :], xph[:, k, c]), (pw[1][:, k, :], xph[:, k, c]),
                                             (pw[0][:, k, :], xpl[:, k, c]))], None)
                last.then_inc(ph_ready, 1)
            for m in range(MT):
                c = slice(m * P, (m + 1) * P)
                last = three(pg[:, m // 4, (m % 4) * C1:(m % 4 + 1) * C1],
                             [x for k in range(KB) for x in
                              ((xph[:, k, c], gw[0][:, k, :]), (xpl[:, k, c], gw[0][:, k, :]),
                               (xph[:, k, c], gw[1][:, k, :]))], None)
                if m % 4 == 3:
                    last.then_inc(g_ready, 1)
            pe.wait_ge(xl_ready, XQ)
            with pe.Fori(0, JQ // 2) as it:
                for u in range(2):
                    j = it * 2 + u
                    pe.wait_ge(ql_ready, j + 1)
                    last = three(pth[u][:, :], [x for k in range(KB) for x in
                                                ((tw[0][:, k, :], xh[:, k, ds(j * CHUNK, CHUNK)]),
                                                 (tw[1][:, k, :], xh[:, k, ds(j * CHUNK, CHUNK)]),
                                                 (tw[0][:, k, :], xl[:, k, ds(j * CHUNK, CHUNK)]))], None)
                    last.then_inc(th_ready, 1)


def nonlocal_attention(nc, qh, ql, kh, kl, gh, gl, zw, ident32, tok):
    ctx = ExitStack()
    with ctx:
        sb = lambda n, shape, dt=F32: ctx.enter_context(nc.sbuf_tensor("na_" + n, shape, dt))
        ps = lambda n, shape: ctx.enter_context(nc.psum_tensor("na_" + n, shape, F32))
        sem = lambda n: semaphore(nc, "na_" + n)
        prob = [sb(f"prob{u}", [P, M_KEYS]) for u in range(2)]
        pth = [sb(f"pth{u}", [P, M_KEYS], F16) for u in range(2)]
        ptl = [sb(f"ptl{u}", [P, M_KEYS], F16) for u in range(2)]
        negmax = [sb(f"negmax{u}", [P, 1]) for u in range(4)]
        den = [sb(f"den{u}", [P, 1]) for u in range(4)]
        rec = sb("rec", [P, 1])
        m3 = sb("m3", [P, C1])
        m3h = [sb(f"m3h{u}", [P, C1], F16) for u in range(2)]
        m3l = [sb(f"m3l{u}", [P, C1], F16) for u in range(2)]
        score = [ps(f"score{u}", [P, M_KEYS]) for u in range(2)]
        turned = ps("turned", [P, M_KEYS])
        outp = ps("outp", [P, 512])
        proj = ps("proj", [P, 512])
        s_ready = sem("s_ready")
        max_ready = sem("max_ready")
        exp_ready = sem("exp_ready")
        t_ready = sem("t_ready")
        hi_ready = sem("hi_ready")
        lo_ready = sem("lo_ready")
        o_ready = sem("o_ready")
        m3_step = sem("m3_step")
        m3_ready = sem("m3_ready")
        z_ready = sem("z_ready")
        added = sem("added")
        block = ctx.enter_context(nc.Block())
        U = 4
        BODY = (R1 - 3) // U * U

        def pipelined(eng, step):
            with eng.Fori(0, BODY // U) as it:
                for u in range(U):
                    step(it * U + u, u, R1)
            for r in range(BODY, R1):
                step(r, r % U, R1 - r)

        @block.tensor
        def _(pe):
            def scores(r, u):
                pe.wait_ge(exp_ready, r + 1)
                q = ds(r * P, P)
                for m in range(2):
                    c = slice(m * 512, (m + 1) * 512)
                    to = score[u % 2][:, c]
                    pe.matmul(to, qh[:, q], kh[:, c], start=True, stop=False)
                    pe.matmul(to, qh[:, q], kl[:, c], start=False, stop=False)
                    last = pe.matmul(to, ql[:, q], kh[:, c], start=False, stop=True)
                last.then_inc(s_ready, 1)

            def turn(r, u):
                pe.wait_ge(exp_ready, r + 3)
                pe.wait_ge(lo_ready, r + 1)
                for m in range(MT):
                    c = slice(m * P, (m + 1) * P)
                    last = pe.transpose(turned[:, c], prob[u % 2][:, c], ident32[:, :])
                last.then_inc(t_ready, 1)

            def times_g(r, u):
                pe.wait_ge(lo_ready, r + 2)
                pe.wait_ge(m3_ready, r + 4)
                for m in range(MT):
                    c = slice(m * P, (m + 1) * P)
                    to = outp[:, 0:C1]
                    pe.matmul(to, pth[u % 2][:, c], gh[:, m, :], start=(m == 0), stop=False)
                    pe.matmul(to, pth[u % 2][:, c], gl[:, m, :], start=False, stop=False)
                    last = pe.matmul(to, ptl[u % 2][:, c], gh[:, m, :], start=False, stop=(m == MT - 1))
                last.then_inc(o_ready, 1)

            def project(r, u):
                pe.wait_ge(m3_ready, r + 5)
                pe.wait_ge(added, r + 1)
                to = proj[:, 0:D]
                pe.matmul(to, m3h[u % 2][:, :], zw[0][:, 0, :], start=True, stop=False)
                pe.matmul(to, m3h[u % 2][:, :], zw[1][:, 0, :], start=False, stop=False)
                pe.matmul(to, m3l[u % 2][:, :], zw[0][:, 0, :], start=False, stop=True).then_inc(z_ready, 1)

            def step(r, u, left):
                if left > 3:
                    scores(r + 3, u + 3)
                if left > 2:
                    turn(r + 2, u + 2)
                if left > 1:
                    times_g(r + 1, u + 1)
                project(r, u)

            pe.sem_inc(t_ready, 2)
            pe.sem_inc(o_ready, 2)
            pe.sem_inc(z_ready, 2)
            scores(0, 0)
            scores(1, 1)
            turn(0, 0)
            scores(2, 2)
            turn(1, 1)
            times_g(0, 0)
            pipelined(pe, step)

        @block.scalar
        def _(act):
            def exps(r, u):
                act.wait_ge(max_ready, r + 1)
                act.wait_ge(t_ready, r + 1)
                act.wait_ge(m3_ready, r + 1)
                act.activation(prob[u % 2][:, :], score[u % 2][:, :], ACT.Exp, bias=negmax[u % 4][:, 0:1],
                               accum_out=den[u % 4][:, 0:1]).then_inc(exp_ready, 1)

            def high(r, u):
                act.wait_ge(t_ready, r + 3)
                act.wait_ge(o_ready, r + 1)
                act.activation(pth[u % 2][:, :], turned[:, :], ACT.Copy).then_inc(hi_ready, 1)

            def step(r, u, left):
                if left > 2:
                    high(r + 2, u + 2)
                if left > 3:
                    exps(r + 3, u + 3)

            act.sem_inc(exp_ready, 2)
            exps(0, 0)
            exps(1, 1)
            high(0, 0)
            exps(2, 2)
            high(1, 1)
            pipelined(act, step)

        @block.vector
        def _(dve):
            def maxima(r, u):
                dve.wait_ge(s_ready, r + 1)
                dve.tensor_reduce(negmax[u % 4][:, :], score[u % 2][:, :], AX.X, ALU.max, negate=True).then_inc(max_ready, 1)

            def low(r, u):
                dve.wait_ge(hi_ready, r + 1)
                dve.tensor_tensor(ptl[u % 2][:, :], turned[:, :], pth[u % 2][:, :], ALU.subtract).then_inc(lo_ready, 1)

            def image(r, u):
                dve.wait_ge(o_ready, r + 3)
                dve.wait_ge(z_ready, r + 1)
                dve.reciprocal(rec[:, :], den[u % 4][:, :]).then_inc(m3_step, 1)
                dve.wait_ge(m3_step, r * 3 + 1)
                dve.tensor_scalar(m3[:, :], outp[:, 0:C1], rec[:, 0:1], None, ALU.mult).then_inc(m3_step, 1)
                dve.wait_ge(m3_step, r * 3 + 2)
                dve.tensor_copy(m3h[u % 2][:, :], m3[:, :]).then_inc(m3_step, 1)
                dve.wait_ge(m3_step, r * 3 + 3)
                dve.tensor_tensor(m3l[u % 2][:, :], m3[:, :], m3h[u % 2][:, :], ALU.subtract).then_inc(m3_ready, 1)

            def add(r, u):
                dve.wait_ge(z_ready, r + 3)
                t = tok[:, ds(r, 1), :].squeeze(1)
                dve.scalar_tensor_tensor(out=t, in0=proj[:, 0:D], scalar=1.0 / W_SCALE, in1=t, op0=ALU.mult,
                                         op1=ALU.add).then_inc(added, 1)

            def step(r, u, left):
                if left > 3:
                    maxima(r + 3, u + 3)
                if left > 2:
                    low(r + 2, u + 2)
                if left > 1:
                    image(r + 1, u + 1)
                add(r, u)

            dve.sem_inc(lo_ready, 1)
            dve.sem_inc(m3_ready, 4)
            dve.sem_inc(added, 1)
            maxima(0, 0)
            maxima(1, 1)
            low(0, 0)
            maxima(2, 2)
            low(1, 1)
            image(0, 0)
            pipelined(dve, step)


def store_image(nc, tok, ident32, out_dram):
    ctx = ExitStack()
    with ctx:
        outc = ctx.enter_context(nc.sbuf_tensor("st_outc", [P, KB, S], F32))
        pt = [ctx.enter_context(nc.psum_tensor(f"st_pt{u}", [P, KB, 256], F32)) for u in range(4)]
        turned = semaphore(nc, "st_turned")
        taken_a = semaphore(nc, "st_taken_a")
        taken_d = semaphore(nc, "st_taken_d")
        out = semaphore(nc, "st_out")
        block = ctx.enter_context(nc.Block())
        PAIRS = NT // 2

        @block.tensor
        def _(pe):
            for n in range(PAIRS):
                if n >= 4:
                    pe.wait_ge(taken_a if n % 2 == 0 else taken_d, (n - 4) // 2 + 1)
                for k in range(KB):
                    for j in range(2):
                        last = pe.transpose(pt[n % 4][:, k, j * P:(j + 1) * P], tok[:, 2 * n + j, k * P:(k + 1) * P],
                                            ident32[:, :])
                last.then_inc(turned, 1)

        @block.scalar
        def _(act):
            for n in range(0, PAIRS, 2):
                act.wait_ge(turned, n + 1)
                act.activation(outc[:, :, n * 256:(n + 1) * 256], pt[n % 4][:, :, :], ACT.Copy).then_inc(taken_a, 1)

        @block.vector
        def _(dve):
            for n in range(1, PAIRS, 2):
                dve.wait_ge(turned, n + 1)
                dve.tensor_copy(outc[:, :, n * 256:(n + 1) * 256], pt[n % 4][:, :, :]).then_inc(taken_d, 1)

        @block.sync
        def _(sp):
            Q = 4
            dst = out_dram.rearrange("b (k p) h w -> p (b k) (h w)", p=P)
            for q in range(Q):
                sp.wait_ge(taken_a, (q + 1) * PAIRS // 2 // Q)
                sp.wait_ge(taken_d, (q + 1) * PAIRS // 2 // Q)
                c = slice(q * S // Q, (q + 1) * S // Q)
                sp.dma_start(dst[:, :, c], outc[:, :, c]).then_inc(out, 16)
            sp.wait_ge(out, 16 * Q)


def layer1_attention(nc, tok, theta_w, theta_b, phi_w, phi_b, g_w, g_b, wz_w, wz_b, ident32):
    ctx = ExitStack()
    with ctx:
        sb = lambda n, shape, dt=F16: ctx.enter_context(nc.sbuf_tensor("l1_" + n, shape, dt))
        mean = sb("mean", [P, NT], F32)
        rstd = sb("rstd", [P, NT], F32)
        tw = [sb(f"tw{i}", [P, KB, C1]) for i in range(2)]
        pw = [sb(f"pw{i}", [P, KB, C1]) for i in range(2)]
        gw = [sb(f"gw{i}", [P, KB, C1]) for i in range(2)]
        zw = [sb(f"zw{i}", [P, 1, D]) for i in range(2)]
        qh, ql = sb("qh", [P, S]), sb("ql", [P, S])
        kh, kl = sb("kh", [P, M_KEYS]), sb("kl", [P, M_KEYS])
        gh, gl = sb("gh", [P, MT, C1]), sb("gl", [P, MT, C1])
        for n, w, dst in (("tht", theta_w, tw), ("phi", phi_w, pw), ("gee", g_w, gw)):
            turn_and_split_weights(nc, n, w, C1, D, ident32, dst[0][:, :, :], dst[1][:, :, :])
        turn_and_split_weights(nc, "wz", wz_w, D, C1, ident32, zw[0][:, :, :], zw[1][:, :, :])
        token_norm(nc, "l1n", tok, LN_C_EPS, mean, rstd)
        with nc.sbuf_tensor("l1_xc", [P, KB, S], F32) as xc:
            tokens_to_channels(nc, "tc", tok, mean, rstd, wz_b, ident32, xc)
            keys_and_queries(nc, xc, tw, pw, gw, theta_b, phi_b, g_b, qh, ql, kh, kl, gh, gl)
        nonlocal_attention(nc, qh, ql, kh, kl, gh, gl, zw, ident32, tok)


def build(nc, x, w_qkv, w_proj, temperature, router_w, w1_0, b1_0, w2_0, b2_0, theta_w, theta_b, phi_w, phi_b,
          g_w, g_b, wz_w, wz_b, gate_w, gate_b, w1_1, b1_1, w2_1, b2_1, out):
    sorted_dram = nc.dram_tensor("sorted_rows", (ROWS, 2 * D), F16, kind="Internal").ap()
    y_dram = nc.dram_tensor("expert_rows", (ROWS, D), F32, kind="Internal").ap()
    ctx = ExitStack()
    with ctx:
        sb = lambda name, shape, dt: ctx.enter_context(nc.sbuf_tensor(name, shape, dt))
        ident32 = sb("ident32", [P, P], F32)
        ident16 = sb("ident16", [P, P], F16)
        below = sb("below", [P, P], F16)
        ones = sb("ones", [P, P], F16)
        steps = sb("steps", [P, S // ET], F32)
        first = sb("first", [P, E_N], F32)
        tile_no = sb("tile_no", [P, MAXT], F32)
        consts = (below, ones, steps, first, tile_no)
        make_identities(nc, ident32, ident16)
        make_routing_constants(nc, *consts)
        tok = sb("tok", [P, NT, D], F32)
        image = tok[:, :, :].rearrange("p t c -> p (t c)").rearrange("p (k s) -> p k s", k=KB)
        with ExitStack() as c2:
            sb2 = lambda name, shape, dt: c2.enter_context(nc.sbuf_tensor(name, shape, dt))
            tau = sb2("tau", [P, HEADS], F32)
            rstd = sb2("rstd", [P, NT], F32)
            qk = sb2("qk", [P, NT, HEADS, 4 * DH], F16)
            vs = sb2("vs", [P, NT, HEADS, VW], F16)
            with nc.sbuf_tensor("xh", [P, KB, S], F16) as xh, nc.sbuf_tensor("xl", [P, KB, S], F16) as xl, \
                    nc.sbuf_tensor("wh", [P, KB, 3 * D], F16) as wh, nc.sbuf_tensor("wl", [P, KB, 3 * D], F16) as wl:
                xp = qk[:, :, :, :].rearrange("p t h c -> p (t h c)")[:, 0:2 * KB * S].bitcast(F32)
                load_and_split_tokens(nc, x, w_qkv, temperature, ident32, image,
                                      xp.rearrange("p (k s) -> p k s", k=KB), xh, xl, rstd, tau, wh, wl)
                project_qkv(nc, xh, xl, rstd, tau, wh, wl, image, qk, vs)
            attention(nc, qk, vs, tau, ident16, image, sorted_dram)
        project_attention(nc, x, w_proj, image, ident32, tok)
        moe(nc, "m0", tok, D, True, router_w, True, None, w1_0, b1_0, w2_0, b2_0, sorted_dram, y_dram, ident16,
            ident32, consts, True)
        clear_semaphores(nc)
        layer1_attention(nc, tok, theta_w, theta_b, phi_w, phi_b, g_w, g_b, wz_w, wz_b, ident32)
        moe(nc, "m1", tok, 4 * D, False, gate_w, False, gate_b, w1_1, b1_1, w2_1, b2_1, sorted_dram, y_dram, ident16,
            ident32, consts, False)
        store_image(nc, tok, ident32, out)


_INS = ['x', 'L0_conv_w_qkv', 'L0_conv_w_proj', 'L0_conv_temperature', 'L0_ffn_router_w', 'L0_ffn_w1', 'L0_ffn_b1',
        'L0_ffn_w2', 'L0_ffn_b2', 'L1_conv_theta_w', 'L1_conv_theta_b', 'L1_conv_phi_w', 'L1_conv_phi_b', 'L1_conv_g_w',
        'L1_conv_g_b', 'L1_conv_wz_w', 'L1_conv_wz_b', 'L1_ffn_Wg', 'L1_ffn_bg', 'L1_ffn_W1', 'L1_ffn_b1', 'L1_ffn_W2',
        'L1_ffn_b2']
_OUTS = [((1, D, HW, HW), 'float32')]


def kernel(**inputs):
    import numpy as _np
    import concourse.bacc as _bacc
    from concourse import mybir as _mybir
    from concourse.bass_utils import run_bass_kernel_spmd as _run

    nc = _bacc.Bacc("TRN2", target_bir_lowering=False, num_devices=1)
    arrays, args = {}, []
    for name in _INS:
        a = _np.ascontiguousarray(inputs[name])
        arrays[f"in_{name}_dram"] = a
        args.append(nc.dram_tensor(f"in_{name}_dram", a.shape, _mybir.dt.from_np(a.dtype), kind="ExternalInput").ap())
    for i, (shape, dtype) in enumerate(_OUTS):
        dt = _mybir.dt.from_np(_np.dtype(dtype))
        args.append(nc.dram_tensor(f"out_{i}_dram", shape, dt, kind="ExternalOutput").ap())
    build(nc, *args)
    r = _run(nc, [arrays], core_ids=[0])
    got = tuple(r.results[0][f"out_{i}_dram"] for i in range(len(_OUTS)))
    return got[0]
```

```python
from contextlib import ExitStack

import concourse.bass as bass
from concourse import mybir

F32 = mybir.dt.float32
F16 = mybir.dt.float16
BF16 = mybir.dt.bfloat16
I32 = mybir.dt.int32
ACT = mybir.ActivationFunctionType
ALU = mybir.AluOpType
AX = mybir.AxisListType
ds = bass.ds

P = 128
D = 256
KB = D // P
HW = 64
S = HW * HW
NT = S // P
GT = 4
NG = NT // GT
HEADS = 8
DH = D // HEADS
LN_C_EPS = 1e-6
LN_T_EPS = 1e-5
NORM_EPS = 1e-12
W_SCALE = 64.0
QK_SCALE = 64.0
P_SHIFT = 20.0
LN2 = 0.6931471805599453
VW = 2 * DH + 2
VN = 2 * DH + 1

GROUP = 2
NGRP = NT // GROUP
CHUNK = 512
SPT = CHUNK // P
NCH = S // CHUNK
PBUF = 4
AHEAD = 3
LOOK = 3
DVE_COLS = 720
ROWS_PER = S // D


IN_USE = []


def semaphore(nc, name):
    IN_USE.append(nc.alloc_semaphore(name))
    return IN_USE[-1]


def clear_semaphores(nc):
    nc.clear_and_free_semaphores(IN_USE)
    IN_USE.clear()
    nc.all_engine_barrier()


def make_identities(nc, ident32, ident16):
    ident_zero = semaphore(nc, "ident_zero")
    ident_done = semaphore(nc, "ident_done")
    with nc.Block() as block:
        @block.gpsimd
        def _(pool):
            pool.memset(ident32[:, :], 0.0).then_inc(ident_zero, 1)
            pool.memset(ident16[:, :], 0.0).then_inc(ident_zero, 1)
            pool.wait_ge(ident_zero, 2)
            for m in (ident32, ident16):
                pool.affine_select(out=m[:, :], in_=m[:, :], compare_op=ALU.not_equal, fill=1.0,
                                   base=0, pattern=[[-1, P]], channel_multiplier=1).then_inc(ident_done, 1)
            pool.wait_ge(ident_done, 2)


def load_and_split_tokens(nc, x_dram, w_dram, temp_dram, ident32, xc, xp, xh, xl, rstd, tau, wh, wl):
    MO = 3 * D // P
    ctx = ExitStack()
    with ctx:
        sb = lambda name, shape, dt: ctx.enter_context(nc.sbuf_tensor(name, shape, dt))
        ps = lambda name, shape: ctx.enter_context(nc.psum_tensor(name, shape, F32))
        sem = lambda name: semaphore(nc, name)
        XQ = 4
        QC = S // XQ

        wn = sb("wn", [P, MO, D], F32)
        wt = sb("wt", [P, KB, 3 * D], F32)
        wmean = sb("wmean", [P, MO], F32)
        xstats = sb("xstats", [P, NT, 6], F32)
        mv = sb("mv", [P, NT, 2], F32)
        sd = sb("sd", [P, NT], F32)
        eps = sb("eps", [P, 1], F32)
        ptx = [ps(f"ptx{i}", [P, 2, D]) for i in range(3)]
        ptw = [ps(f"ptw{i}", [P, 4, P]) for i in range(2)]
        w_in = sem("w_in")
        t_in = sem("t_in")
        x_in = [sem(f"x_in{i}") for i in range(XQ)]
        w_step = sem("w_step")
        w_cent = sem("w_cent")
        wt_ready = sem("wt_ready")
        wt_used = sem("wt_used")
        wh_ready = sem("wh_ready")
        xp_ready = sem("xp_ready")
        xh_ready = sem("xh_ready")
        xt_ready = sem("xt_ready")
        xt_used = sem("xt_used")
        agg = sem("agg")
        eps_ready = sem("eps_ready")
        sd_ready = sem("sd_ready")
        done = sem("done")
        xl_ready = sem("xl_ready")
        block = ctx.enter_context(nc.Block())

        @block.sync
        def _(sp):
            sp.dma_start(wn[:, :, :], w_dram.rearrange("(m p) c -> p m c", p=P)).then_inc(w_in, 16)
            for q in range(XQ):
                sp.dma_start(xc[:, :, q * QC:(q + 1) * QC],
                             x_dram.rearrange("b (k p) h w -> p (b k) (h w)", p=P)[:, :, q * QC:(q + 1) * QC]
                             ).then_inc(x_in[q], 16)
            sp.dma_start(tau[:, :], temp_dram.rearrange("h a b -> (h a b)").partition_broadcast(P)).then_inc(t_in, 16)
            sp.wait_ge(t_in, 16)

        @block.vector
        def _(dve):
            dve.memset(eps[:, :], LN_C_EPS).then_inc(eps_ready, 1)
            dve.wait_ge(w_in, 16)
            dve.tensor_reduce(wmean[:, :], wn[:, :, :], AX.X, ALU.add).then_inc(w_step, 1)
            dve.wait_ge(w_step, 1)
            dve.tensor_scalar(wmean[:, :], wmean[:, :], -1.0 / D, None, ALU.mult).then_inc(w_step, 1)
            dve.wait_ge(w_step, 2)
            for m in range(MO):
                dve.tensor_scalar(wn[:, m, :], wn[:, m, :], wmean[:, m:m + 1], None, ALU.add).then_inc(w_cent, 1)
            for k in range(KB):
                for i, (m0, m1) in enumerate(((0, 4), (4, MO))):
                    n = 2 * k + i
                    dve.wait_ge(wt_ready, n + 1)
                    dve.tensor_scalar(wt[:, k, m0 * P:m1 * P], ptw[n % 2][:, 0:m1 - m0, :].rearrange("p a b -> p (a b)"),
                                      W_SCALE, None, ALU.mult).then_inc(wt_used, 1)
            dve.wait_ge(wh_ready, 1)
            dve.tensor_tensor(wl[:, :, :], wt[:, :, :], wh[:, :, :], ALU.subtract).then_inc(done, 1)
            for q in range(XQ):
                if q == XQ - 1:
                    dve.wait_ge(xh_ready, XQ)
                    c = slice(q * QC, (q + 1) * QC)
                    dve.tensor_tensor(xl[:, :, c], xp[:, :, c], xh[:, :, c], ALU.subtract).then_inc(done, 1)
                for n in range(q * NT // XQ // 2, (q + 1) * NT // XQ // 2):
                    dve.wait_ge(xt_ready, n + 1)
                    for j in range(2):
                        last = dve.bn_stats(xstats[:, 2 * n + j, :], ptx[n % 3][:, j, :])
                    last.then_inc(xt_used, 1)
            dve.wait_ge(xt_used, NT // 2)
            for t in range(NT):
                last = dve.bn_aggr(mv[:, t, :], xstats[:, t, :])
            last.then_inc(agg, 1)
            dve.wait_ge(sd_ready, 1)
            dve.reciprocal(rstd[:, :], sd[:, :]).then_inc(done, 1)
            dve.wait_ge(done, 3)

        @block.gpsimd
        def _(pool):
            for q in range(XQ - 1):
                c = slice(q * QC, (q + 1) * QC)
                pool.wait_ge(xh_ready, q + 1)
                pool.tensor_tensor(xl[:, :, c], xp[:, :, c], xh[:, :, c], ALU.subtract).then_inc(xl_ready, 1)
                pool.wait_ge(xl_ready, q + 1)

        @block.scalar
        def _(act):
            act.wait_ge(wt_used, 2 * KB)
            act.activation(wh[:, :, :], wt[:, :, :], ACT.Copy).then_inc(wh_ready, 1)
            for q in range(XQ):
                act.wait_ge(x_in[q], 16)
                for k in range(KB):
                    c = slice(q * QC, (q + 1) * QC)
                    act.activation(xp[:, k, c].rearrange("p (b r i) -> p b r i", b=QC // CHUNK, r=ROWS_PER),
                                   xc[:, k, c].rearrange("p (b i r) -> p b r i", b=QC // CHUNK, r=ROWS_PER),
                                   ACT.Copy).then_inc(xp_ready, 1)
                act.wait_ge(xp_ready, KB * (q + 1))
                act.activation(xh[:, :, c], xp[:, :, c], ACT.Copy).then_inc(xh_ready, 1)
            act.wait_ge(agg, 1)
            act.wait_ge(eps_ready, 1)
            act.activation(sd[:, :], mv[:, :, 1], ACT.Sqrt, bias=eps[:, 0:1]).then_inc(sd_ready, 1)

        @block.tensor
        def _(pe):
            pe.wait_ge(w_cent, MO)
            for k in range(KB):
                for i, (m0, m1) in enumerate(((0, 4), (4, MO))):
                    n = 2 * k + i
                    if n >= 2:
                        pe.wait_ge(wt_used, n - 1)
                    for m in range(m0, m1):
                        last = pe.transpose(ptw[n % 2][:, m - m0, :], wn[:, m, k * P:(k + 1) * P], ident32[:, :])
                    last.then_inc(wt_ready, 1)
            for n in range(NT // 2):
                pe.wait_ge(xp_ready, KB * (n * XQ * 2 // NT + 1))
                if n >= 3:
                    pe.wait_ge(xt_used, n - 2)
                for j in range(2):
                    for k in range(KB):
                        last = pe.transpose(ptx[n % 3][:, j, k * P:(k + 1) * P],
                                            xp[:, k, (2 * n + j) * P:(2 * n + j + 1) * P], ident32[:, :])
                last.then_inc(xt_ready, 1)


def project_qkv(nc, xh, xl, rstd, tau, wh, wl, scratch, qk, vs):
    assert QK_SCALE == W_SCALE
    ctx = ExitStack()
    with ctx:
        sb = lambda name, shape, dt: ctx.enter_context(nc.sbuf_tensor(name, shape, dt))
        ps = lambda name, shape: ctx.enter_context(nc.psum_tensor(name, shape, F32))
        sem = lambda name: semaphore(nc, name)
        QK = 2 * D
        halves = lambda tile: qk[:, ds(tile, 1), :, :].squeeze(1).rearrange("p h (m d) -> p m h d", m=4)
        NH2 = 2 * HEADS
        part = lambda n: scratch[:, n // 2, n % 2 * GT * QK:(n % 2 + 1) * GT * QK].rearrange("p (t c) -> p t c", t=GT)
        raw = [part(u) for u in range(2)]
        vraw = [sb(f"vraw{u}", [P, GT, D], F32) for u in range(2)]
        sq = [part(2 + u) for u in range(2)]
        ss = sb("ss", [P, GT, NH2], F32)
        nrm = sb("nrm", [P, GT, NH2], F32)
        inv = sb("inv", [P, GT, NH2], F32)
        pqk = [ps(f"pqk{u}", [P, QK]) for u in range(2)]
        pv = [ps(f"pv{u}", [P, 512]) for u in range(2)]
        qkv_ready = sem("qkv_ready")
        qkv_taken = sem("qkv_taken")
        sq_free = sem("sq_free")
        raw_free = [sem(f"raw_free{u}") for u in range(2)]
        ss_ready = sem("ss_ready")
        nrm_ready = sem("nrm_ready")
        dchain = sem("dchain")
        unit_ready = sem("unit_ready")
        hi_ready = sem("hi_ready")
        pool_going = sem("pool_going")
        ones_set = sem("ones_set")
        block = ctx.enter_context(nc.Block())

        @block.tensor
        def _(pe):
            with pe.Fori(0, NT // 2) as it:
                for u in range(2):
                    tile = it * 2 + u
                    pe.wait_ge(qkv_taken, tile + 1)
                    n = 0
                    for k in range(KB):
                        for xx, ww in ((xh, wh), (xl, wh), (xh, wl)):
                            lhs = xx[:, k, ds(tile * P, P)]
                            pe.matmul(pqk[u][:, :], lhs, ww[:, k, 0:QK], start=(n == 0), stop=(n == 5))
                            last = pe.matmul(pv[u][:, 0:D], lhs, ww[:, k, QK:QK + D], start=(n == 0), stop=(n == 5))
                            n += 1
                    last.then_inc(qkv_ready, 1)

        @block.scalar
        def _(act):
            def root(g):
                act.wait_ge(ss_ready, g + 1)
                act.activation(nrm[:, :, :], ss[:, :, :], ACT.Sqrt).then_inc(nrm_ready, 1)

            def fill(g, u, it):
                act.wait_ge(raw_free[u], 2 * it + 2)
                act.wait_ge(sq_free, g + 1)
                for t in range(GT):
                    act.wait_ge(qkv_ready, g * GT + t + 1)
                    act.activation(raw[u][:, t, :], pqk[t % 2][:, :], ACT.Copy)
                    act.activation(sq[u][:, t, :], pqk[t % 2][:, :], ACT.Square)
                    act.activation(vraw[u][:, t, :], pv[t % 2][:, 0:D], ACT.Copy, scale=1.0 / W_SCALE
                                   ).then_inc(qkv_taken, 1)

            act.sem_inc(qkv_taken, 2)
            with act.Fori(0, NG // 2) as it:
                for u in range(2):
                    fill(it * 2 + u, u, it)
                    root(it * 2 + u)

        @block.vector
        def _(dve):
            links = 0

            def chained(ins):
                nonlocal links
                links += 1
                ins.then_inc(dchain, 1)
                dve.wait_ge(dchain, it * (2 * PER) + links)

            PER = 6
            for u in range(2):
                dve.sem_inc(raw_free[u], 2)
            dve.sem_inc(sq_free, 2)
            dve.memset(vs[:, :, :, 2 * DH:VW], 1.0).then_inc(ones_set, 1)
            with dve.Fori(0, NG // 2) as it:
                links = 0
                for u in range(2):
                    g = it * 2 + u
                    dve.wait_ge(qkv_taken, g * GT + GT + 2)
                    dve.tensor_reduce(ss[:, :, :], sq[u][:, :, :].rearrange("p t (h d) -> p t h d", d=DH), AX.X,
                                      ALU.add).then_inc(sq_free, 1)
                    dve.wait_ge(sq_free, g + 3)
                    dve.sem_inc(ss_ready, 1)
                    rb = rstd[:, ds(g * GT, GT)].unsqueeze(2)
                    chained(dve.tensor_tensor(vraw[u][:, :, :], vraw[u][:, :, :], rb.broadcast_to([P, GT, D]), ALU.mult))
                    dve.wait_ge(nrm_ready, g + 1)
                    chained(dve.tensor_tensor(nrm[:, :, :], nrm[:, :, :], rb.broadcast_to([P, GT, NH2]), ALU.mult))
                    chained(dve.tensor_scalar(nrm[:, :, :], nrm[:, :, :], 1.0 / W_SCALE, NORM_EPS, ALU.mult, ALU.max))
                    chained(dve.reciprocal(inv[:, :, :], nrm[:, :, :]))
                    chained(dve.tensor_tensor(inv[:, :, :], inv[:, :, :], rb.broadcast_to([P, GT, NH2]), ALU.mult))
                    chained(dve.tensor_tensor(inv[:, :, 0:HEADS], inv[:, :, 0:HEADS],
                                              tau[:, :].unsqueeze(1).broadcast_to([P, GT, HEADS]), ALU.mult))
                    for t in range(GT):
                        rv = raw[u][:, t, :].rearrange("p (h d) -> p h d", d=DH)
                        iv = inv[:, t, :].unsqueeze(2).broadcast_to([P, NH2, DH])
                        last = dve.tensor_tensor(rv, rv, iv, ALU.mult)
                    last.then_inc(unit_ready, 1)
                    dve.wait_ge(unit_ready, g + 1)
                    for t in range(GT):
                        rv = raw[u][:, t, :].rearrange("p (m h d) -> p m h d", m=2, d=DH)
                        vv = vraw[u][:, t, :].rearrange("p (h d) -> p h d", d=DH)
                        dve.tensor_copy(halves(g * GT + t)[:, 0:4:3], rv)
                        dve.tensor_copy(vs[:, ds(g * GT + t, 1), :, 0:DH].squeeze(1), vv).then_inc(hi_ready, 1)

        @block.gpsimd
        def _(pool):
            pool.wait_ge(ones_set, 1)
            with pool.Fori(0, NG // 2) as it:
                for u in range(2):
                    g = it * 2 + u
                    for t in range(GT):
                        pool.wait_ge(hi_ready, g * GT + t + 1)
                        pool.sem_inc(pool_going, 1)
                        rv = raw[u][:, t, :].rearrange("p (m h d) -> p m h d", m=2, d=DH)
                        vv = vraw[u][:, t, :].rearrange("p (h d) -> p h d", d=DH)
                        to = halves(g * GT + t)
                        pool.tensor_tensor(to[:, 1:3], rv, to[:, 0:4:3], ALU.subtract)
                        row = vs[:, ds(g * GT + t, 1), :, :].squeeze(1)
                        last = pool.tensor_tensor(row[:, :, DH:2 * DH], vv, row[:, :, 0:DH], ALU.subtract)
                    last.then_inc(raw_free[u], 2)


def attention(nc, qk, vs, tau, ident16, aout, sorted_dram):
    ctx = ExitStack()
    with ctx:
        sb = lambda name, shape, dt: ctx.enter_context(nc.sbuf_tensor(name, shape, dt))
        ps = lambda name, shape, dt=F32: ctx.enter_context(nc.psum_tensor(name, shape, dt))
        sem = lambda name: semaphore(nc, name)
        GC = GROUP * CHUNK
        ZROWS = -(-ROWS // (HEADS * NCH * P))
        ZP = ROWS // (HEADS * NCH * ZROWS)
        assert ZP * ZROWS * HEADS * NCH == ROWS

        def high(p):
            return p[:, :].bitcast(BF16).rearrange("p (n two) -> p n two", two=2)[:, :, 1]

        qT = sb("qT", [P, 2 * S], F16)
        kT = sb("kT", [P, 2 * S], F16)
        halves = [sb(f"halves{u}", [P, CHUNK], F16) for u in range(2)]
        staged = [sb(f"staged{u}", [P, GT, 4 * DH], F16) for u in range(2)]
        shift_rows = sb("shift_rows", [P, HEADS, CHUNK], F16)
        prob = [sb(f"prob{i}", [P, GC], F32) for i in range(PBUF)]
        plow = [sb(f"plow{i}", [P, GC], F16) for i in range(PBUF)]
        shift = sb("shift", [P, HEADS], F32)
        warm = sb("warm", [P, 1], F32)
        zero = sb("zero", [P, ZROWS, 2 * D], F16)
        osb = sb("osb", [P, SPT, VN], F32)
        rec = sb("rec", [P, SPT], F32)
        osum = sb("osum", [P, SPT, DH], F32)
        scores = [ps(f"scores{i}", [P, GC]) for i in range(2)]
        outp = ps("outp", [P, 2, 512])
        turned = ps("turned", [P, GT, P], F16)
        score_ready = sem("score_ready")
        prob_ready = sem("prob_ready")
        low_ready = sem("low_ready")
        lowp_ready = sem("lowp_ready")
        prob_used = sem("prob_used")
        out_taken = sem("out_taken")
        rec_ready = sem("rec_ready")
        osb_used = sem("osb_used")
        turned_ready = sem("turned_ready")
        turned_taken = sem("turned_taken")
        shift_ready = sem("shift_ready")
        sum_step = sem("sum_step")
        shift_set = sem("shift_set")
        stage_in = [sem(f"stage_in{u}") for u in range(2)]
        q_const = sem("q_const")
        zero_set = sem("zero_set")
        zeroed = sem("zeroed")
        placed = [sem(f"placed{u}") for u in range(2)]
        placed_dve = sem("placed_dve")
        placed_act = sem("placed_act")
        placed_shift = sem("placed_shift")
        PLACE = 5 * 16
        block = ctx.enter_context(nc.Block())

        q_from = lambda rows, u: halves[u][0:rows, :].rearrange("p (r i) -> p r i", r=ROWS_PER)
        q_to = lambda r0, r1, h, j: qT[r0:r1, :].rearrange("p (b r i) -> p b r i", r=ROWS_PER, i=P)[
            :, ds((h % 2) * 2 + j // 4, 1), :, ds((j % 4) * (CHUNK // ROWS_PER), CHUNK // ROWS_PER)].squeeze(1)

        def pairs_of_chunks(eng, step):
            with eng.Fori(0, HEADS * NCH // 2 - 1) as it:
                for u in range(2):
                    step(it * 2 + u, u, True)
            step(HEADS * NCH - 2, 0, True)
            step(HEADS * NCH - 1, 1, False)

        @block.gpsimd
        def _(pool):
            def low(c, g):
                pool.wait_ge(prob_ready, c * NGRP + g + 1)
                p, l = prob[g % PBUF], plow[g % PBUF]
                pool.tensor_tensor(l[:, DVE_COLS:GC], p[:, DVE_COLS:GC], high(p)[:, DVE_COLS:GC],
                                   ALU.subtract).then_inc(lowp_ready, 1)

            def add_halves(c):
                pool.wait_ge(rec_ready, c + 1)
                pool.tensor_tensor(osum[:, :, :], osb[:, :, 0:DH], osb[:, :, DH:2 * DH], ALU.add).then_inc(sum_step, 1)

            def divide(c):
                pool.wait_ge(sum_step, c + 1)
                image = aout[:, :, :].rearrange("p k (r h d) -> p (k r) h d", h=HEADS, d=DH)
                pool.tensor_tensor(image[:, ds((c % NCH) * SPT, SPT), ds(c // NCH, 1), :].squeeze(2), osum[:, :, :],
                                   rec[:, :].unsqueeze(2).broadcast_to([P, SPT, DH]), ALU.mult).then_inc(osb_used, 1)

            pool.sem_inc(osb_used, 1)
            pool.memset(qT[3 * DH:4 * DH, :], QK_SCALE / DH).then_inc(q_const, 1)
            pool.wait_ge(q_const, 1)
            pool.memset(zero[:, :, :], 0.0).then_inc(zero_set, 1)
            pool.wait_ge(zero_set, 1)
            for g in range(AHEAD):
                low(0, g)

            def step(c, u, more, before=True):
                for g in range(AHEAD, NGRP):
                    low(c, g)
                    if before and g == 5:
                        add_halves(c - 1)
                    if before and g == 9:
                        divide(c - 1)
                if more:
                    for g in range(AHEAD):
                        low(c + 1, g)

            step(0, 0, True, False)
            with pool.Fori(0, HEADS * NCH // 2 - 1) as it:
                for u in range(2):
                    step(it * 2 + 1 + u, 1 - u, True)
            step(HEADS * NCH - 1, 1, False)
            add_halves(HEADS * NCH - 1)
            divide(HEADS * NCH - 1)
            pool.wait_ge(osb_used, HEADS * NCH + 1)

        @block.scalar
        def _(act):
            act.activation(warm[:, :], tau[:, 0:1], ACT.Exp)
            for j in range(NCH):
                act.wait_ge(turned_taken, j + 2)
                act.activation(kT[2 * DH:3 * DH, j * CHUNK:(j + 1) * CHUNK], halves[j % 2][3 * DH:4 * DH, :],
                               ACT.Copy).then_inc(placed_act, 1)
                act.activation(q_to(2 * DH, 3 * DH, 0, j), q_from(DH, j % 2), ACT.Copy).then_inc(placed_act, 1)
            with act.Fori(0, HEADS * NCH // 2) as it:
                for g in range(2 * NGRP):
                    n = it * (2 * NGRP) + g
                    act.wait_ge(score_ready, n + 1)
                    act.wait_ge(prob_used, n + 1)
                    act.activation(prob[g % PBUF][:, :], scores[g % 2][:, :], ACT.Exp,
                                   scale=1.0 / (QK_SCALE * QK_SCALE)).then_inc(prob_ready, 1)

        @block.sync
        def _(sp):
            def stage(turn, u):
                h, j = turn // NCH % HEADS, turn % NCH
                sp.dma_start(staged[u][:, :, :], qk[:, ds(j * GT, GT), ds(h, 1), :].squeeze(2)).then_inc(stage_in[u], 16)

            def place(turn, u):
                h, j = turn // NCH, turn % NCH
                sp.wait_ge(turned_taken, turn + 2)
                k_cols = ds((h % 2) * S + j * CHUNK, CHUNK)
                sp.dma_start(kT[0:2 * DH, k_cols], halves[u][2 * DH:4 * DH, :]).then_inc(placed[u], 16)
                sp.dma_start(kT[2 * DH:3 * DH, k_cols], halves[u][3 * DH:4 * DH, :]).then_inc(placed[u], 16)
                sp.dma_start(kT[3 * DH:4 * DH, k_cols], shift_rows[3 * DH:4 * DH, ds(h % HEADS, 1), :].squeeze(1)
                             ).then_inc(placed[u], 16)
                sp.dma_start(q_to(0, 2 * DH, h, j), q_from(2 * DH, u)).then_inc(placed[u], 16)
                sp.dma_start(q_to(2 * DH, 3 * DH, h, j), q_from(DH, u)).then_inc(placed[u], 16)

            def zero_rows(c):
                sp.dma_start(sorted_dram[ds(c * ZP * ZROWS, ZP * ZROWS), :].rearrange("(p a) c -> p a c", a=ZROWS),
                             zero[0:ZP, :, :]).then_inc(zeroed, 16)

            stage(0, 0)
            stage(1, 1)
            sp.wait_ge(shift_set, 1)
            for j in range(NCH):
                sp.wait_ge(turned_ready, j + 1)
                stage(j + 2, j % 2)
                sp.dma_start(kT[3 * DH:4 * DH, j * CHUNK:(j + 1) * CHUNK], shift_rows[3 * DH:4 * DH, 0, :]
                             ).then_inc(placed_shift, 16)
            sp.wait_ge(zero_set, 1)

            def step(c, u, more):
                if more:
                    place(c + NCH, u)
                    stage(c + NCH + 2, u)
                zero_rows(c)

            pairs_of_chunks(sp, step)
            sp.wait_ge(zeroed, 16 * HEADS * NCH)
            for u in range(2):
                sp.wait_ge(stage_in[u], 16 * ((HEADS * NCH + NCH - u) // 2 + 1))

        @block.vector
        def _(dve):
            dve.sem_inc(out_taken, 2)
            dve.sem_inc(turned_taken, 1)
            for u in range(2):
                dve.sem_inc(placed[u], 16)
            dve.tensor_scalar(shift[:, :], tau[:, :], -1.0, None, ALU.mult).then_inc(shift_ready, 1)
            dve.wait_ge(shift_ready, 1)
            dve.tensor_tensor(shift[:, :], shift[:, :], tau[:, :], ALU.max).then_inc(shift_ready, 1)
            dve.wait_ge(shift_ready, 2)
            dve.tensor_scalar(shift[:, :], shift[:, :], -1.0, P_SHIFT * LN2, ALU.mult, ALU.add).then_inc(shift_ready, 1)
            dve.wait_ge(shift_ready, 3)
            dve.tensor_scalar(shift_rows[3 * DH:4 * DH, :, :], shift[3 * DH:4 * DH, :].unsqueeze(2)
                              .broadcast_to([DH, HEADS, CHUNK]), QK_SCALE, None, ALU.mult).then_inc(shift_set, 1)

            def take_turned(turn, u):
                dve.wait_ge(turned_ready, turn + 1)
                dve.tensor_copy(halves[u][:, :], turned[:, :, :].rearrange("p a b -> p (a b)")).then_inc(turned_taken, 1)

            def low(c, g):
                dve.wait_ge(prob_ready, c * NGRP + g + 1)
                p, l = prob[g % PBUF], plow[g % PBUF]
                dve.tensor_tensor(l[:, 0:DVE_COLS], p[:, 0:DVE_COLS], high(p)[:, 0:DVE_COLS],
                                  ALU.subtract).then_inc(low_ready, 1)

            def take_out(c, u):
                dve.wait_ge(prob_used, c * NGRP + NGRP + PBUF)
                dve.wait_ge(osb_used, c + 1)
                dve.tensor_copy(osb[:, :, :], outp[:, u, 0:SPT * VN]
                                .rearrange("p (j v) -> p j v", v=VN)).then_inc(out_taken, 1)
                dve.wait_ge(out_taken, c + 3)
                dve.reciprocal(rec[:, :], osb[:, :, 2 * DH]).then_inc(rec_ready, 1)

            for j in range(NCH):
                if j >= 2:
                    dve.wait_ge(placed_act, 2 * (j - 1))
                    dve.wait_ge(placed_dve, 2 * (j - 1))
                take_turned(j, j % 2)
                dve.wait_ge(turned_taken, j + 2)
                dve.tensor_copy(kT[0:2 * DH, j * CHUNK:(j + 1) * CHUNK], halves[j % 2][2 * DH:4 * DH, :]
                                ).then_inc(placed_dve, 1)
                dve.tensor_copy(q_to(0, 2 * DH, 0, j), q_from(2 * DH, j % 2)).then_inc(placed_dve, 1)
            dve.wait_ge(placed_act, 2 * NCH)
            dve.wait_ge(placed_dve, 2 * NCH)
            for g in range(AHEAD):
                low(0, g)
            def step(c, u, more):
                for g in range(AHEAD, NGRP):
                    low(c, g)
                    if g == 3 and more:
                        dve.wait_ge(placed[u], (c - u) // 2 * PLACE + 16)
                        take_turned(c + NCH, u)
                if more:
                    for g in range(AHEAD):
                        low(c + 1, g)
                take_out(c, u)

            pairs_of_chunks(dve, step)

        @block.tensor
        def _(pe):
            def turn(i, u):
                pe.wait_ge(stage_in[u], (i // 2) * 16 + 16)
                pe.wait_ge(turned_taken, i + 1)
                for t in range(GT):
                    last = pe.transpose(turned[:, t, :], staged[u][:, t, :], ident16[:, :])
                last.then_inc(turned_ready, 1)

            def score(c, g, buf):
                for i in range(GROUP):
                    last = pe.matmul(scores[buf][:, i * CHUNK:(i + 1) * CHUNK],
                                     kT[:, ds(c // NCH % 2 * S + (g * GROUP + i) * P, P)],
                                     qT[:, ds(c % (2 * NCH) * CHUNK, CHUNK)], start=True, stop=True)
                last.then_inc(score_ready, 1)

            def times_v(c, g, u):
                pe.wait_ge(low_ready, c * NGRP + g + 1)
                pe.wait_ge(lowp_ready, c * NGRP + g + 1)
                for i in range(GROUP):
                    v = vs[:, g * GROUP + i, ds(c // NCH, 1), 0:VN].squeeze(1)
                    for j in range(SPT):
                        cols = slice(i * CHUNK + j * P, i * CHUNK + (j + 1) * P)
                        to = outp[:, u, j * VN:(j + 1) * VN]
                        pe.matmul(to, high(prob[g % PBUF])[:, cols], v, start=(g == 0 and i == 0 and j == 0),
                                  stop=False, skip_group_check=True)
                        last = pe.matmul(to, plow[g % PBUF][:, cols], v, start=False,
                                         stop=(g == NGRP - 1 and i == GROUP - 1), skip_group_check=True)
                last.then_inc(prob_used, 1)

            with pe.Fori(0, NCH // 2) as it:
                for u in range(2):
                    turn(it * 2 + u, u)
            pe.sem_inc(prob_used, PBUF)
            pe.wait_ge(q_const, 1)
            pe.wait_ge(placed_dve, 2 * NCH)
            pe.wait_ge(placed_act, 2 * NCH)
            pe.wait_ge(placed_shift, 16 * NCH)
            for g in range(LOOK):
                if g >= 2:
                    pe.wait_ge(prob_ready, g - 1)
                score(0, g, g % 2)

            def step(c, u, more):
                for g in range(NGRP):
                    n = g + LOOK
                    if n == NGRP and more:
                        pe.wait_ge(placed[u], (c - u) // 2 * PLACE + PLACE + 16)
                    if n < NGRP or more:
                        pe.wait_ge(prob_ready, c * NGRP + n - 1)
                        score(c + n // NGRP, n % NGRP, n % 2)
                    if g == 0:
                        pe.wait_ge(out_taken, c + 1)
                    times_v(c, g, u)
                    if g == 1 and more:
                        turn(c + NCH, u)

            pairs_of_chunks(pe, step)


E_N = 8
TOP = 2
ET = 256
EH = ET // P
MAXT = (TOP * S + E_N * (ET - 1)) // ET
ROWS = MAXT * ET
BIG = 1e30


def turn_and_split_weights(nc, name, weights, ident32):
    N = len(weights)
    ctx = ExitStack()
    with ctx:
        sb = lambda n, shape, dt: ctx.enter_context(nc.sbuf_tensor(name + n, shape, dt))
        wn = [sb(f"wn{i}", [P, rows // P, cols], F32) for i, (_, rows, cols, _, _) in enumerate(weights)]
        wt = [sb(f"wt{i}", [P, cols // P, rows], F32) for i, (_, rows, cols, _, _) in enumerate(weights)]
        pt = [ctx.enter_context(nc.psum_tensor(name + f"pt{i}", [P, 512], F32)) for i in range(N)]
        w_in = [semaphore(nc, name + f"w_in{i}") for i in range(N)]
        turned = semaphore(nc, name + "turned")
        scaled = semaphore(nc, name + "scaled")
        high_ready = semaphore(nc, name + "high_ready")
        low_ready = semaphore(nc, name + "low_ready")
        block = ctx.enter_context(nc.Block())

        @block.sync
        def _(sp):
            for i, (w_dram, _, _, _, _) in enumerate(weights):
                sp.dma_start(wn[i][:, :, :], w_dram.rearrange("(m p) c -> p m c", p=P)).then_inc(w_in[i], 16)

        @block.tensor
        def _(pe):
            for i, (_, rows, cols, _, _) in enumerate(weights):
                pe.wait_ge(w_in[i], 16)
                for k in range(cols // P):
                    for m in range(rows // P):
                        last = pe.transpose(pt[i][:, k * rows + m * P:k * rows + (m + 1) * P],
                                            wn[i][:, m, k * P:(k + 1) * P], ident32[:, :])
                last.then_inc(turned, 1)

        @block.vector
        def _(dve):
            for i, (_, rows, cols, _, _) in enumerate(weights):
                dve.wait_ge(turned, i + 1)
                dve.tensor_scalar(wt[i][:, :, :], pt[i][:, 0:rows * cols // P].rearrange("p (k r) -> p k r", r=rows),
                                  W_SCALE, None, ALU.mult).then_inc(scaled, 1)
            for i, (_, _, _, high, _) in enumerate(weights):
                dve.wait_ge(scaled, i + 1)
                dve.tensor_copy(high, wt[i][:, :, :]).then_inc(high_ready, 1)
            for i, (_, _, _, high, low) in enumerate(weights):
                dve.wait_ge(high_ready, i + 1)
                dve.tensor_tensor(low, wt[i][:, :, :], high, ALU.subtract).then_inc(low_ready, 1)
            dve.wait_ge(low_ready, N)


def project_attention(nc, x_dram, w_dram, aout, ident32, tok, stats):
    ctx = ExitStack()
    with ctx:
        sb = lambda name, shape, dt: ctx.enter_context(nc.sbuf_tensor(name, shape, dt))
        ps = lambda name, shape: ctx.enter_context(nc.psum_tensor(name, shape, F32))
        sem = lambda name: semaphore(nc, name)
        wh = sb("pj_wh", [P, KB, D], F16)
        wl = sb("pj_wl", [P, KB, D], F16)
        turn_and_split_weights(nc, "pjw_", [(w_dram, D, D, wh[:, :, :], wl[:, :, :])], ident32)
        ah = sb("pj_ah", [P, KB, S], F16)
        al = sb("pj_al", [P, KB, S], F16)
        xg = [sb(f"pj_xg{u}", [P, KB, GT * P], F32) for u in range(2)]
        px = [ps(f"pj_px{u}", [P, 512]) for u in range(2)]
        pp = [ps(f"pj_pp{u}", [P, 512]) for u in range(2)]
        x_in = [sem(f"pj_x_in{u}") for u in range(2)]
        x_turned = sem("pj_x_turned")
        ah_ready = sem("pj_ah_ready")
        al_ready = sem("pj_al_ready")
        pe_ready = sem("pj_pe_ready")
        x_taken = sem("pj_x_taken")
        x_going = sem("pj_x_going")
        summed = sem("pj_summed")
        block = ctx.enter_context(nc.Block())
        AQ = 4
        AC = S // AQ

        @block.sync
        def _(sp):
            src = x_dram.rearrange("b (k p) h w -> p (b k) (h w)", p=P)
            with sp.Fori(0, NG // 2) as it:
                for u in range(2):
                    sp.wait_ge(x_turned, (it * 2 + u + 1) * GT)
                    sp.dma_start(xg[u][:, :, :], src[:, :, ds((it * 2 + u) * GT * P, GT * P)]).then_inc(x_in[u], 16)

        @block.scalar
        def _(act):
            for q in range(AQ):
                c = slice(q * AC, (q + 1) * AC)
                act.activation(ah[:, :, c], aout[:, :, c], ACT.Copy).then_inc(ah_ready, 1)
            with act.Fori(0, NG // 2) as it:
                for u in range(2 * GT):
                    tile = it * (2 * GT) + u
                    act.wait_ge(x_turned, tile + 1 + 2 * GT)
                    act.sem_inc(x_going, 1)
                    act.activation(tok[:, ds(tile, 1), :].squeeze(1), px[u % 2][:, 0:D], ACT.Copy).then_inc(x_taken, 1)

        @block.vector
        def _(dve):
            for q in range(AQ):
                dve.wait_ge(ah_ready, q + 1)
                dve.tensor_tensor(al[:, :, q * AC:(q + 1) * AC], aout[:, :, q * AC:(q + 1) * AC],
                                  ah[:, :, q * AC:(q + 1) * AC], ALU.subtract).then_inc(al_ready, 1)
            dve.sem_inc(summed, 2)
            with dve.Fori(0, NG // 2) as it:
                for u in range(2 * GT):
                    tile = it * (2 * GT) + u
                    dve.wait_ge(x_taken, tile + 1)
                    dve.wait_ge(pe_ready, tile + 1)
                    t = tok[:, ds(tile, 1), :].squeeze(1)
                    dve.scalar_tensor_tensor(out=t, in0=pp[u % 2][:, 0:D], scalar=1.0 / W_SCALE, in1=t,
                                             op0=ALU.mult, op1=ALU.add).then_inc(summed, 1)
                    dve.wait_ge(summed, tile + 3)
                    dve.bn_stats(stats[:, ds(tile, 1), :].squeeze(1), t)

        @block.tensor
        def _(pe):
            pe.sem_inc(x_turned, 2 * GT)
            pe.wait_ge(al_ready, AQ)
            with pe.Fori(0, NG // 2) as it:
                for u in range(2):
                    pe.wait_ge(x_in[u], it * 16 + 16)
                    for t in range(GT):
                        i = u * GT + t
                        tile = it * (2 * GT) + i
                        pe.wait_ge(summed, tile + 1)
                        for k in range(KB):
                            last = pe.transpose(px[i % 2][:, k * P:(k + 1) * P], xg[u][:, k, t * P:(t + 1) * P],
                                                ident32[:, :])
                        last.then_inc(x_turned, 1)
                        n = 0
                        for k in range(KB):
                            for aa, ww in ((ah, wh), (al, wh), (ah, wl)):
                                last = pe.matmul(pp[i % 2][:, 0:D], aa[:, k, ds(tile * P, P)], ww[:, k, :],
                                                 start=(n == 0), stop=(n == 5))
                                n += 1
                        last.then_inc(pe_ready, 1)


def token_norm(nc, name, stats, eps_value, mean, rstd):
    ctx = ExitStack()
    with ctx:
        sb = lambda n, shape, dt: ctx.enter_context(nc.sbuf_tensor(name + n, shape, dt))
        mv = sb("mv", [P, NT, 2], F32)
        sd = sb("sd", [P, NT], F32)
        eps = sb("eps", [P, 1], F32)
        aggregated = semaphore(nc, name + "aggregated")
        rooted = semaphore(nc, name + "rooted")
        out = semaphore(nc, name + "out")
        block = ctx.enter_context(nc.Block())

        @block.vector
        def _(dve):
            dve.memset(eps[:, :], eps_value)
            for t in range(NT):
                last = dve.bn_aggr(mv[:, t, :], stats[:, t, :])
            last.then_inc(aggregated, 1)
            dve.wait_ge(aggregated, 1)
            dve.tensor_copy(mean[:, :], mv[:, :, 0]).then_inc(out, 1)
            dve.wait_ge(rooted, 1)
            dve.reciprocal(rstd[:, :], sd[:, :]).then_inc(out, 1)
            dve.wait_ge(out, 2)

        @block.scalar
        def _(act):
            act.wait_ge(aggregated, 1)
            act.activation(sd[:, :], mv[:, :, 1], ACT.Sqrt, bias=eps[:, 0:1]).then_inc(rooted, 1)


def logits_and_rows(nc, name, tok, mean, rstd, gate_dram, gate_by_expert, ident32, logits, rows16, add_norm):
    NX = 4
    ctx = ExitStack()
    with ctx:
        sb = lambda n, shape, dt: ctx.enter_context(nc.sbuf_tensor(name + n, shape, dt))
        ps = lambda n, shape: ctx.enter_context(nc.psum_tensor(name + n, shape, F32))
        sem = lambda n: semaphore(nc, name + n)
        gate = sb("gate", [P, KB, E_N], F32)
        xn = [sb(f"xn{u}", [P, D], F32) for u in range(NX)]
        xt = [sb(f"xt{u}", [P, D], F32) for u in range(2)]
        pt = [ps(f"pt{u}", [P, 512]) for u in range(2)]
        pl = [ps(f"pl{u}", [P, 512]) for u in range(2)]
        gate_in = sem("gate_in")
        xn_ready = sem("xn_ready")
        hi_ready = sem("hi_ready")
        turned = sem("turned")
        xt_ready = sem("xt_ready")
        multiplied = sem("multiplied")
        taken = sem("taken")
        lo_ready = sem("lo_ready")
        block = ctx.enter_context(nc.Block())

        @block.sync
        def _(sp):
            with nc.allow_non_contiguous_dma(reason="the gate's few weights"):
                src = gate_dram.rearrange("e (k p) -> p k e", p=P) if gate_by_expert else \
                    gate_dram.rearrange("(k p) e -> p k e", p=P)
                for k in range(KB):
                    sp.dma_start(gate[:, k, :], src[:, k, :]).then_inc(gate_in, 16)
            sp.wait_ge(gate_in, 16 * KB)

        @block.vector
        def _(dve):
            def norm(t, u):
                x = tok[:, ds(t, 1), :].squeeze(1)
                dve.wait_ge(lo_ready, t + 1)
                dve.wait_ge(turned, t + 1)
                dve.tensor_scalar(xn[u][:, :], x, mean[:, ds(t, 1)], rstd[:, ds(t, 1)],
                                  ALU.subtract, ALU.mult).then_inc(xn_ready, 1)
                dve.wait_ge(xn_ready, t + 1)
                if add_norm:
                    dve.tensor_tensor(x, x, xn[u][:, :], ALU.add)
                dve.tensor_copy(rows16[:, ds(t, 1), 0:D].squeeze(1), xn[u][:, :]).then_inc(hi_ready, 1)

            def take(t, u):
                dve.wait_ge(multiplied, t + 3)
                dve.tensor_copy(logits[:, ds(t, 1), :].squeeze(1), pl[u % 2][:, 0:E_N]).then_inc(taken, 1)

            dve.sem_inc(taken, 2)
            for t in range(NX - 1):
                norm(t, t)
            with dve.Fori(0, NT // NX - 1) as it:
                for u in range(NX):
                    norm(it * NX + u + NX - 1, (u - 1) % NX)
                    take(it * NX + u, u)
            norm(NT - 1, NX - 1)
            for u in range(NX):
                take(NT - NX + u, u)

        @block.tensor
        def _(pe):
            def turn(t, u):
                pe.wait_ge(xn_ready, t + 1)
                pe.wait_ge(xt_ready, t + 1)
                for k in range(KB):
                    last = pe.transpose(pt[u % 2][:, k * P:(k + 1) * P], xn[u % NX][:, k * P:(k + 1) * P], ident32[:, :])
                last.then_inc(turned, 1)

            def mult(t, u):
                pe.wait_ge(xt_ready, t + 3)
                pe.wait_ge(taken, t + 1)
                for k in range(KB):
                    last = pe.matmul(pl[u % 2][:, 0:E_N], xt[u % 2][:, k * P:(k + 1) * P], gate[:, k, :],
                                     start=(k == 0), stop=(k == KB - 1))
                last.then_inc(multiplied, 1)

            pe.sem_inc(turned, NX)
            pe.sem_inc(multiplied, 2)
            pe.wait_ge(gate_in, 16 * KB)
            turn(0, 0)
            with pe.Fori(0, NT // NX - 1) as it:
                for u in range(NX):
                    turn(it * NX + u + 1, u + 1)
                    mult(it * NX + u, u)
            for u in range(NX):
                if u + 1 < NX:
                    turn(NT - NX + u + 1, u + 1)
                mult(NT - NX + u, u)

        @block.scalar
        def _(act):
            act.sem_inc(xt_ready, 2)
            with act.Fori(0, NT // 2) as it:
                for u in range(2):
                    t = it * 2 + u
                    act.wait_ge(turned, t + 1 + NX)
                    act.wait_ge(multiplied, t + 1)
                    act.activation(xt[u][:, :], pt[u][:, 0:D], ACT.Copy).then_inc(xt_ready, 1)

        @block.gpsimd
        def _(pool):
            pool.sem_inc(lo_ready, NX)
            with pool.Fori(0, NT // NX) as it:
                for u in range(NX):
                    t = it * NX + u
                    row = rows16[:, ds(t, 1), :].squeeze(1)
                    pool.wait_ge(hi_ready, t + 1)
                    pool.tensor_tensor(row[:, D:2 * D], xn[u][:, :], row[:, 0:D], ALU.subtract).then_inc(lo_ready, 1)


def make_routing_constants(nc, below, ones, steps, first, tile_no):
    made = semaphore(nc, "rc_set")
    with nc.Block() as block:
        @block.gpsimd
        def _(pool):
            pool.memset(ones[:, :], 1.0).then_inc(made, 1)
            pool.wait_ge(made, 1)
            pool.affine_select(out=below[:, :], in_=ones[:, :], compare_op=ALU.is_gt, fill=0.0, base=0,
                               pattern=[[1, P]], channel_multiplier=-1).then_inc(made, 1)
            pool.iota(steps[:, :], pattern=[[ET, S // ET]], base=0, channel_multiplier=0,
                      allow_small_or_imprecise_dtypes=True).then_inc(made, 1)
            pool.iota(first[:, :], pattern=[[-1, E_N]], base=E_N, channel_multiplier=0,
                      allow_small_or_imprecise_dtypes=True).then_inc(made, 1)
            pool.iota(tile_no[:, :], pattern=[[1, MAXT]], base=0, channel_multiplier=0,
                      allow_small_or_imprecise_dtypes=True).then_inc(made, 1)
            pool.wait_ge(made, 5)


def route(nc, name, logits, by_probs, gate_bias_dram, consts, weights, slots, tile_expert):
    below, ones, steps, first, tile_no = consts
    ctx = ExitStack()
    with ctx:
        sb = lambda n, shape, dt=F32: ctx.enter_context(nc.sbuf_tensor(name + n, shape, dt))
        sem = lambda n: semaphore(nc, name + n)
        A = [P, NT, E_N]
        val = sb("val", A)
        tmp = sb("tmp", A)
        tmp2 = sb("tmp2", A)
        hot = [sb(f"hot{i}", A) for i in range(TOP)]
        best = [sb(f"best{i}", [P, NT]) for i in range(TOP)]
        r1 = sb("r1", [P, NT])
        mask = sb("mask", A, F16)
        tot = [sb(f"tot{i}", A) for i in range(2)]
        cnt = sb("cnt", [P, E_N])
        over = sb("over", [P, E_N, S // ET])
        tiles = [sb(f"tiles{i}", [P, E_N]) for i in range(2)]
        start = sb("start", [P, E_N])
        stop = sb("stop", [P, E_N])
        past = sb("past", [P, MAXT, E_N])
        owner = sb("owner", [P, MAXT])
        bias = sb("bias", [P, E_N])
        pc = ctx.enter_context(nc.psum_tensor(name + "pc", [P, 512], F32))
        pt = ctx.enter_context(nc.psum_tensor(name + "pt", [P, 512], F32))
        step = sem("step")
        exped = sem("exped")
        summed = sem("summed")
        bias_in = sem("bias_in")
        marks = {}
        block = ctx.enter_context(nc.Block())

        @block.sync
        def _(sp):
            if gate_bias_dram is not None:
                sp.dma_start(bias[:, :], gate_bias_dram.partition_broadcast(P)).then_inc(bias_in, 16)
                sp.wait_ge(bias_in, 16)

        @block.vector
        def _(dve):
            n = 0

            def link(ins):
                nonlocal n
                n += 1
                ins.then_inc(step, 1)
                dve.wait_ge(step, n)
                return n

            per_tile = lambda x: x[:, :].unsqueeze(2).broadcast_to(A)
            per_expert = lambda x: x[:, :].unsqueeze(1).broadcast_to(A)
            if gate_bias_dram is not None:
                dve.wait_ge(bias_in, 16)
                link(dve.tensor_tensor(val[:, :, :], logits[:, :, :], per_expert(bias), ALU.add))
            if by_probs:
                link(dve.tensor_reduce(r1[:, :], logits[:, :, :], AX.X, ALU.max))
                marks["shifted"] = link(dve.tensor_tensor(val[:, :, :], logits[:, :, :], per_tile(r1), ALU.subtract))
                dve.wait_ge(exped, 1)
                link(dve.tensor_reduce(r1[:, :], val[:, :, :], AX.X, ALU.add))
                link(dve.reciprocal(r1[:, :], r1[:, :]))
                link(dve.tensor_tensor(val[:, :, :], val[:, :, :], per_tile(r1), ALU.mult))
            for i in range(TOP):
                link(dve.tensor_reduce(best[i][:, :], val[:, :, :], AX.X, ALU.max))
                link(dve.tensor_tensor(tmp[:, :, :], val[:, :, :], per_tile(best[i]), ALU.is_equal))
                link(dve.tensor_tensor(tmp[:, :, :], tmp[:, :, :], per_expert(first), ALU.mult))
                link(dve.tensor_reduce(r1[:, :], tmp[:, :, :], AX.X, ALU.max))
                link(dve.tensor_tensor(hot[i][:, :, :], per_expert(first), per_tile(r1), ALU.is_equal))
                if i == 0:
                    link(dve.tensor_scalar(tmp2[:, :, :], hot[0][:, :, :], -BIG, None, ALU.mult))
                    link(dve.tensor_tensor(val[:, :, :], val[:, :, :], tmp2[:, :, :], ALU.add))
            marks["mask"] = link(dve.tensor_tensor(mask[:, :, :], hot[0][:, :, :], hot[1][:, :, :], ALU.add))
            w = weights
            if by_probs:
                link(dve.tensor_tensor(r1[:, :], best[0][:, :], best[1][:, :], ALU.add))
                link(dve.tensor_scalar(r1[:, :], r1[:, :], 1e-12, None, ALU.max))
                link(dve.reciprocal(r1[:, :], r1[:, :]))
                link(dve.tensor_tensor(w[0][:, :], best[0][:, :], r1[:, :], ALU.mult))
                link(dve.tensor_tensor(w[1][:, :], best[1][:, :], r1[:, :], ALU.mult))
            else:
                marks["gap"] = link(dve.tensor_tensor(r1[:, :], best[1][:, :], best[0][:, :], ALU.subtract))
                dve.wait_ge(exped, 1)
                link(dve.tensor_scalar(w[0][:, :], r1[:, :], 1.0, None, ALU.add))
                link(dve.reciprocal(w[0][:, :], w[0][:, :]))
                link(dve.tensor_tensor(w[1][:, :], w[0][:, :], r1[:, :], ALU.mult))
            dve.wait_ge(summed, 1)
            link(dve.tensor_copy(tot[0][:, :, :], pt[:, 0:NT * E_N].rearrange("p (t e) -> p t e", e=E_N)))
            a, d = 0, 1
            while d < NT:
                dve.tensor_copy(tot[1 - a][:, 0:d, :], tot[a][:, 0:d, :])
                link(dve.tensor_tensor(tot[1 - a][:, d:NT, :], tot[a][:, d:NT, :], tot[a][:, 0:NT - d, :], ALU.add))
                a, d = 1 - a, 2 * d
            incl = tot[a]
            link(dve.tensor_copy(cnt[:, :], incl[:, NT - 1, :]))
            OV = [P, E_N, S // ET]
            link(dve.tensor_tensor(over[:, :, :], cnt[:, :].unsqueeze(2).broadcast_to(OV),
                                   steps[:, :].unsqueeze(1).broadcast_to(OV), ALU.is_gt))
            link(dve.tensor_reduce(tiles[0][:, :], over[:, :, :], AX.X, ALU.add))
            link(dve.tensor_scalar(cnt[:, :], tiles[0][:, :], 1.0, None, ALU.mult))
            b, d = 0, 1
            while d < E_N:
                dve.tensor_copy(tiles[1 - b][:, 0:d], tiles[b][:, 0:d])
                link(dve.tensor_tensor(tiles[1 - b][:, d:E_N], tiles[b][:, d:E_N], tiles[b][:, 0:E_N - d], ALU.add))
                b, d = 1 - b, 2 * d
            link(dve.tensor_copy(stop[:, :], tiles[b][:, :]))
            link(dve.tensor_tensor(start[:, :], stop[:, :], cnt[:, :], ALU.subtract))
            link(dve.tensor_scalar(start[:, :], start[:, :], float(ET), None, ALU.mult))
            OW = [P, MAXT, E_N]
            link(dve.tensor_tensor(past[:, :, :], tile_no[:, :].unsqueeze(2).broadcast_to(OW),
                                   stop[:, :].unsqueeze(1).broadcast_to(OW), ALU.is_ge))
            link(dve.tensor_reduce(owner[:, :], past[:, :, :], AX.X, ALU.add))
            link(dve.tensor_scalar(tile_expert[:, :], owner[:, :], float(E_N - 1), None, ALU.min))
            link(dve.tensor_tensor(tmp[:, :, :], pc[:, 0:NT * E_N].rearrange("p (t e) -> p t e", e=E_N), per_expert(start),
                                   ALU.add))
            link(dve.tensor_tensor(tmp[:, 1:NT, :], tmp[:, 1:NT, :], incl[:, 0:NT - 1, :], ALU.add))
            for i in range(TOP):
                link(dve.tensor_tensor(tmp2[:, :, :], tmp[:, :, :], hot[i][:, :, :], ALU.mult))
                link(dve.tensor_reduce(r1[:, :], tmp2[:, :, :], AX.X, ALU.add))
                link(dve.tensor_copy(slots[i][:, :], r1[:, :]))

        @block.scalar
        def _(act):
            if by_probs:
                act.wait_ge(step, marks["shifted"])
                act.activation(val[:, :, :], val[:, :, :], ACT.Exp).then_inc(exped, 1)
            else:
                act.wait_ge(step, marks["gap"])
                act.activation(r1[:, :], r1[:, :], ACT.Exp).then_inc(exped, 1)

        @block.tensor
        def _(pe):
            m = mask[:, :, :].rearrange("p t e -> p (t e)")
            pe.wait_ge(step, marks["mask"])
            pe.matmul(pt[:, 0:NT * E_N], ones[:, :], m, start=True, stop=True)
            pe.matmul(pc[:, 0:NT * E_N], below[:, :], m, start=True, stop=True).then_inc(summed, 1)


def experts(nc, name, F, w1, shared, rows16, slots, w1_dram, b1_dram, w2_dram, b2_dram, sorted_dram, y_dram,
            tile_expert, ident16, ident32):
    NF = F // P
    ctx = ExitStack()
    with ctx:
        sb = lambda n, shape, dt: ctx.enter_context(nc.sbuf_tensor(name + n, shape, dt))
        ps = lambda n, shape, dt=F32: ctx.enter_context(nc.psum_tensor(name + n, shape, dt))
        sem = lambda n: semaphore(nc, name + n)
        w1h, w1l = w1[:, :, 0], w1[:, :, 1]
        w2h = sb("w2h", [P, E_N, NF, D], F16)
        w2l = sb("w2l", [P, E_N, NF, D], F16)
        b1t = sb("b1t", [P, E_N, NF], F32)
        b2t = sb("b2t", [P, E_N, D], F32)

        with ExitStack() as c2:
            WC = KB * F
            stg = [c2.enter_context(nc.sbuf_tensor(name + f"stg{u}", [P, WC], F32)) for u in range(3)]
            b1n = c2.enter_context(nc.sbuf_tensor(name + "b1n", [E_N * NF, P], F32))
            pb = c2.enter_context(nc.psum_tensor(name + "pb", [P, 512], F32))
            w_in = [semaphore(nc, name + f"w_in{u}") for u in range(3)]
            b_in = semaphore(nc, name + "b_in")
            b_turned = semaphore(nc, name + "b_turned")
            scaled = semaphore(nc, name + "scaled")
            split = semaphore(nc, name + "split")
            bstep = semaphore(nc, name + "bstep")
            PART = NT // (E_N - shared) if shared < E_N else NT
            sent = [semaphore(nc, name + f"sent{i}") for i in range(NT // PART)]
            block = c2.enter_context(nc.Block())
            w1_part = lambda e: (w1_dram[e].rearrange("(k p) f -> p k f", p=P), w1h[:, e], w1l[:, e], KB, F)
            parts = [w1_part(e) for e in range(shared)]
            parts += [(w2_dram[e].rearrange("(n p) d -> p n d", p=P), w2h[:, e], w2l[:, e], NF, D) for e in range(E_N)]
            parts += [w1_part(e) for e in range(shared, E_N)]

            @block.gpsimd
            def _(pool):
                for t in range(NT):
                    for i in range(TOP):
                        to = bass.IndirectOffsetOnAxis(ap=slots[i][:, t:t + 1], axis=0)
                        pool.indirect_dma_start(out=sorted_dram, out_offset=to, in_=rows16[:, t, :], in_offset=None
                                                ).then_inc(sent[t // PART], 16)
                for part in range(NT // PART):
                    pool.wait_ge(sent[part], 16 * TOP * PART)

            @block.sync
            def _(sp):
                sp.dma_start(b1n[:, :], b1_dram.rearrange("e (n p) -> (e n) p", p=P)).then_inc(b_in, 16)
                sp.dma_start(b2t[:, :, :].rearrange("p e d -> p (e d)"), b2_dram.rearrange("e d -> (e d)")
                             .partition_broadcast(P)).then_inc(b_in, 16)
                for i, (src, _, _, a, b) in enumerate(parts):
                    if i >= 3:
                        sp.wait_ge(split, i - 2)
                    sp.dma_start(stg[i % 3][:, :].rearrange("p (a b) -> p a b", b=b), src).then_inc(w_in[i % 3], 16)

            @block.scalar
            def _(act):
                for i, (_, hi, lo, a, b) in enumerate(parts):
                    act.wait_ge(w_in[i % 3], 16 * (i // 3 + 1))
                    if i >= shared + E_N:
                        act.wait_ge(sent[i - shared - E_N], 16 * TOP * PART)
                    act.activation(hi, stg[i % 3][:, :].rearrange("p (a b) -> p a b", b=b), ACT.Copy,
                                   scale=W_SCALE).then_inc(scaled, 1)

            @block.vector
            def _(dve):
                dve.wait_ge(b_turned, 1)
                dve.tensor_copy(b1t[:, :, :], pb[:, 0:E_N * NF].rearrange("p (e n) -> p e n", n=NF)).then_inc(bstep, 1)
                for i, (_, hi, lo, a, b) in enumerate(parts):
                    dve.wait_ge(scaled, i + 1)
                    dve.scalar_tensor_tensor(out=lo, in0=stg[i % 3][:, :].rearrange("p (a b) -> p a b", b=b),
                                             scalar=W_SCALE, in1=hi, op0=ALU.mult, op1=ALU.subtract).then_inc(split, 1)
                dve.wait_ge(bstep, 1)

            @block.tensor
            def _(pe):
                pe.wait_ge(b_in, 32)
                pe.transpose(pb[:, 0:E_N * NF], b1n[:, :], ident32[0:E_N * NF, 0:E_N * NF]).then_inc(b_turned, 1)

        xr = [sb(f"xr{u}", [P, EH, 2 * D], F16) for u in range(2)]
        xT = [sb(f"xT{u}", [P, 2 * KB, ET], F16) for u in range(2)]
        b1c = [sb(f"b1c{u}", [P, NF], F32) for u in range(2)]
        hf = [sb(f"hf{u}", [P, ET], F32) for u in range(4)]
        hh = [sb(f"hh{u}", [P, NF, ET], F16) for u in range(2)]
        hl = [sb(f"hl{u}", [P, NF, ET], F16) for u in range(2)]
        yo = [sb(f"yo{u}", [P, EH, D], F32) for u in range(2)]
        px = [ps(f"px{u}", [P, 2 * KB, ET], F16) for u in range(2)]
        ph = [ps(f"ph{u}", [P, 512]) for u in range(4)]
        py = [ps(f"py{u}", [P, 512]) for u in range(2)]
        x_in = [sem(f"x_in{u}") for u in range(2)]
        turned = sem("turned")
        xt_ready = sem("xt_ready")
        h_ready = sem("h_ready")
        act_ready = sem("act_ready")
        hh_ready = sem("hh_ready")
        hl_ready = sem("hl_ready")
        y_ready = sem("y_ready")
        y_taken = sem("y_taken")
        y_out = [sem(f"y_out{u}") for u in range(2)]
        block = ctx.enter_context(nc.Block())
        BODY = (MAXT - 2) // 2 * 2

        def pipelined(eng, step, *args):
            with eng.Fori(0, BODY // 2) as it:
                for u in range(2):
                    step(it * 2 + u, u, it, True, True, *args)
            for i in range(BODY, MAXT):
                step(i, i % 2, i // 2, i + 1 < MAXT, i + 2 < MAXT, *args)

        def expert_of(eng, reg, i):
            eng.reg_load(reg, tile_expert[0:1, ds(i, 1)])
            return the_expert(eng, reg)

        def the_expert(eng, reg):
            return eng.snap(reg, min_val=0, max_val=E_N - 1)

        @block.sync
        def _(sp):
            def load(i, u):
                sp.wait_ge(turned, i + 1)
                sp.dma_start(xr[u][:, :, :], sorted_dram[ds(i * ET, ET), :].rearrange("(h p) c -> p h c", p=P)
                             ).then_inc(x_in[u], 16)

            def step(i, u, it, one_more, two_more):
                if two_more:
                    load(i + 2, u)

            for u in range(2):
                sp.sem_inc(y_out[u], 16)
                load(u, u)
            pipelined(sp, step)

        @block.tensor
        def _(pe):
            regs = [pe.alloc_register(name + f"pe_expert{u}") for u in range(2)]

            def turn(i, u, it):
                pe.wait_ge(x_in[u], it * 16 + 16)
                pe.wait_ge(xt_ready, i + 1)
                for q in range(2 * KB):
                    for h in range(EH):
                        last = pe.transpose(px[u][:, q, h * P:(h + 1) * P], xr[u][:, h, q * P:(q + 1) * P], ident16[:, :])
                last.then_inc(turned, 1)

            def first(i, u):
                e = expert_of(pe, regs[u], i)
                pe.wait_ge(xt_ready, i + 3)
                for f in range(NF):
                    pe.wait_ge(act_ready, i * NF + f + 1)
                    k6 = 0
                    for k in range(KB):
                        for w, x in ((w1h, k), (w1h, KB + k), (w1l, k)):
                            last = pe.matmul(ph[(u * NF + f) % 4][:, 0:ET],
                                             w[:, ds(e, 1), k, f * P:(f + 1) * P].squeeze(1), xT[u][:, x, :],
                                             start=(k6 == 0), stop=(k6 == 3 * KB - 1))
                            k6 += 1
                    last.then_inc(h_ready, 1)

            def second(i, u):
                e = the_expert(pe, regs[u])
                for h in range(EH):
                    pe.wait_ge(y_taken, i * EH + h + 1)
                    to = py[h % 2][:, 0:D]
                    c = slice(h * P, (h + 1) * P)
                    for f in range(NF):
                        if h == 0:
                            pe.wait_ge(hl_ready, i * NF + f + 5)
                        wh_e = w2h[:, ds(e, 1), f, :].squeeze(1)
                        pe.matmul(to, hh[u][:, f, c], wh_e, start=(f == 0), stop=False)
                        pe.matmul(to, hl[u][:, f, c], wh_e, start=False, stop=False)
                        last = pe.matmul(to, hh[u][:, f, c], w2l[:, ds(e, 1), f, :].squeeze(1), start=False,
                                         stop=(f == NF - 1))
                    last.then_inc(y_ready, 1)

            def step(i, u, it, one_more, two_more):
                if two_more:
                    turn(i + 2, u, it + 1)
                if one_more:
                    first(i + 1, 1 - u)
                second(i, u)

            pe.sem_inc(turned, 2)
            pe.sem_inc(y_ready, 2 * EH)
            turn(0, 0, 0)
            turn(1, 1, 0)
            first(0, 0)
            pipelined(pe, step)

        @block.scalar
        def _(act):
            def gelus(i, u):
                act.wait_ge(xt_ready, i + 3)
                for f in range(NF):
                    b = (u * NF + f) % 4
                    act.wait_ge(h_ready, i * NF + f + 1)
                    act.wait_ge(hl_ready, i * NF + f + 1)
                    act.activation(hf[b][:, :], ph[b][:, 0:ET], ACT.Gelu, bias=b1c[u][:, f:f + 1],
                                   scale=1.0 / W_SCALE).then_inc(act_ready, 1)

            def step(i, u, it, one_more, two_more):
                if one_more:
                    gelus(i + 1, 1 - u)
                act.wait_ge(y_taken, i * EH + EH + 2)
                act.dma_start(y_dram[ds(i * ET, ET), :].rearrange("(h p) c -> p h c", p=P), yo[u][:, :, :]
                              ).then_inc(y_out[u], 16)

            act.sem_inc(act_ready, 4)
            gelus(0, 0)
            pipelined(act, step)
            act.wait_ge(y_out[0], 16 * ((MAXT + 1) // 2 + 1))
            act.wait_ge(y_out[1], 16 * (MAXT // 2 + 1))

        @block.vector
        def _(dve):
            regs = [dve.alloc_register(name + f"dve_expert{u}") for u in range(2)]
            y_reg = dve.alloc_register(name + "dve_y_expert")

            def take_x(i, u):
                e = expert_of(dve, regs[u], i)
                dve.wait_ge(turned, i + 3)
                dve.tensor_copy(b1c[u][:, :], b1t[:, ds(e, 1), :].squeeze(1))
                dve.tensor_copy(xT[u][:, :, :], px[u][:, :, :]).then_inc(xt_ready, 1)

            def highs(i, u):
                dve.wait_ge(y_ready, i * EH + EH)
                for f in range(NF):
                    dve.wait_ge(act_ready, i * NF + f + 5)
                    dve.tensor_copy(hh[u][:, f, :], hf[(u * NF + f) % 4][:, :]).then_inc(hh_ready, 1)

            def step(i, u, it, one_more, two_more):
                if two_more:
                    take_x(i + 2, u)
                if one_more:
                    highs(i + 1, 1 - u)
                rows_out(i, u, it)

            def rows_out(i, u, it):
                e = expert_of(dve, y_reg, i)
                dve.wait_ge(y_out[u], it * 16 + 16)
                for h in range(EH):
                    dve.wait_ge(y_ready, i * EH + h + 1 + 2 * EH)
                    dve.scalar_tensor_tensor(out=yo[u][:, h, :], in0=py[h % 2][:, 0:D], scalar=1.0 / W_SCALE,
                                             in1=b2t[:, ds(e, 1), :].squeeze(1), op0=ALU.mult, op1=ALU.add
                                             ).then_inc(y_taken, 1)

            dve.sem_inc(y_taken, 2)
            dve.sem_inc(xt_ready, 2)
            take_x(0, 0)
            take_x(1, 1)
            highs(0, 0)
            pipelined(dve, step)

        @block.gpsimd
        def _(pool):
            def lows(i, u):
                for f in range(NF):
                    pool.wait_ge(hh_ready, i * NF + f + 1)
                    pool.tensor_tensor(hl[u][:, f, :], hf[(u * NF + f) % 4][:, :], hh[u][:, f, :],
                                       ALU.subtract).then_inc(hl_ready, 1)

            def step(i, u, it, one_more, two_more):
                if one_more:
                    lows(i + 1, 1 - u)

            pool.sem_inc(hl_ready, 4)
            lows(0, 0)
            pipelined(pool, step)


def combine_experts(nc, name, tok, slots, weights, y_dram, stats, ident32, out_dram):
    NB = 8
    PAIRS = NT // 2
    ctx = ExitStack()
    with ctx:
        got = [ctx.enter_context(nc.sbuf_tensor(name + f"got{b}", [P, D], F32)) for b in range(NB)]
        if out_dram is not None:
            outc = ctx.enter_context(nc.sbuf_tensor(name + "outc", [P, KB, S], F32))
            pt = [ctx.enter_context(nc.psum_tensor(name + f"pt{u}", [P, KB, 256], F32)) for u in range(2)]
        arrived = [semaphore(nc, name + f"arrived{b}") for b in range(NB)]
        added = semaphore(nc, name + "added")
        turned = semaphore(nc, name + "turned")
        taken = semaphore(nc, name + "taken")
        stored = semaphore(nc, name + "stored")
        block = ctx.enter_context(nc.Block())

        @block.gpsimd
        def _(pool):
            for n in range(NT * TOP):
                if n >= NB:
                    pool.wait_ge(added, n - NB + 1)
                where = bass.IndirectOffsetOnAxis(ap=slots[n % TOP][:, n // TOP:n // TOP + 1], axis=0)
                pool.indirect_dma_start(out=got[n % NB][:, :], out_offset=None, in_=y_dram, in_offset=where
                                        ).then_inc(arrived[n % NB], 16)

        @block.vector
        def _(dve):
            for n in range(NT * TOP):
                t = n // TOP
                dve.wait_ge(arrived[n % NB], 16 * (n // NB + 1))
                if n:
                    dve.wait_ge(added, n)
                dve.scalar_tensor_tensor(out=tok[:, t, :], in0=got[n % NB][:, :], scalar=weights[n % TOP][:, t:t + 1],
                                         in1=tok[:, t, :], op0=ALU.mult, op1=ALU.add).then_inc(added, 1)
                if out_dram is None and n % TOP == TOP - 1:
                    dve.wait_ge(added, n + 1)
                    dve.bn_stats(stats[:, t, :], tok[:, t, :])

        if out_dram is None:
            return

        @block.tensor
        def _(pe):
            for n in range(PAIRS):
                pe.wait_ge(added, 2 * TOP * (n + 1))
                if n >= 2:
                    pe.wait_ge(taken, n - 1)
                for k in range(KB):
                    for j in range(2):
                        last = pe.transpose(pt[n % 2][:, k, j * P:(j + 1) * P], tok[:, 2 * n + j, k * P:(k + 1) * P],
                                            ident32[:, :])
                last.then_inc(turned, 1)

        @block.scalar
        def _(act):
            for n in range(PAIRS):
                act.wait_ge(turned, n + 1)
                act.activation(outc[:, :, n * 256:(n + 1) * 256], pt[n % 2][:, :, :], ACT.Copy).then_inc(taken, 1)

        @block.sync
        def _(sp):
            Q = 8
            dst = out_dram.rearrange("b (k p) h w -> p (b k) (h w)", p=P)
            for q in range(Q):
                sp.wait_ge(taken, (q + 1) * PAIRS // Q)
                c = slice(q * S // Q, (q + 1) * S // Q)
                sp.dma_start(dst[:, :, c], outc[:, :, c]).then_inc(stored, 16)
            sp.wait_ge(stored, 16 * Q)


def moe(nc, name, tok, F, by_probs, gate, gate_by_expert, gate_bias, w1, b1, w2, b2, sorted_dram, y_dram,
        ident16, ident32, consts, add_norm, stats, out_dram):
    ctx = ExitStack()
    with ctx:
        sb = lambda n, shape, dt=F32: ctx.enter_context(nc.sbuf_tensor(name + n, shape, dt))
        weights = [sb(f"share{i}", [P, NT]) for i in range(TOP)]
        slots = [sb(f"slot{i}", [P, NT], I32) for i in range(TOP)]
        tile_expert = sb("tile_expert", [P, MAXT], I32)
        w1_halves = sb("w1", [P, E_N, 2, KB, F], F16)
        shared = E_N - -(-NT * 2 * D // (2 * KB * F))
        if shared > 0:
            rows16 = w1_halves[:, shared:E_N].rearrange("p e i k f -> p (e i k f)").rearrange("p (t c) -> p t c", t=NT)
        else:
            shared = E_N
            rows16 = sb("rows16", [P, NT, 2 * D], F16)
        with nc.sbuf_tensor(name + "mean", [P, NT], F32) as mean, nc.sbuf_tensor(name + "rstd", [P, NT], F32) as rstd, \
                nc.sbuf_tensor(name + "logits", [P, NT, E_N], F32) as logits:
            token_norm(nc, name + "n", stats, LN_T_EPS, mean, rstd)
            logits_and_rows(nc, name + "l", tok, mean, rstd, gate, gate_by_expert, ident32, logits, rows16, add_norm)
            route(nc, name + "r", logits, by_probs, gate_bias, consts, weights, slots, tile_expert)
        experts(nc, name + "e", F, w1_halves, shared, rows16, slots, w1, b1, w2, b2, sorted_dram, y_dram,
                tile_expert, ident16, ident32)
        combine_experts(nc, name + "c", tok, slots, weights, y_dram, stats, ident32, out_dram)

M_KEYS = S // 4
MT = M_KEYS // P
C1 = 128
R1 = S // C1


def tokens_to_channels(nc, name, tok, mean, rstd, bias_dram, ident32, xc):
    NX = 4
    ctx = ExitStack()
    with ctx:
        sb = lambda n, shape, dt=F32: ctx.enter_context(nc.sbuf_tensor(name + n, shape, dt))
        sem = lambda n: semaphore(nc, name + n)
        xn = [sb(f"xn{u}", [P, D]) for u in range(NX)]
        bias = sb("bias", [P, D])
        pt = [ctx.enter_context(nc.psum_tensor(name + f"pt{u}", [P, 512], F32)) for u in range(2)]
        bias_in = sem("bias_in")
        xn_ready = sem("xn_ready")
        biased = sem("biased")
        turned = sem("turned")
        taken = sem("taken")
        going = sem("going")
        added = sem("added")
        pool_going = sem("pool_going")
        block = ctx.enter_context(nc.Block())

        @block.sync
        def _(sp):
            sp.dma_start(bias[:, :], bias_dram.partition_broadcast(P)).then_inc(bias_in, 16)

        @block.vector
        def _(dve):
            dve.wait_ge(bias_in, 16)
            with dve.Fori(0, NT // NX) as it:
                for u in range(NX):
                    t = it * NX + u
                    x = tok[:, ds(t, 1), :].squeeze(1)
                    dve.wait_ge(turned, t + 1)
                    dve.wait_ge(added, t + 1)
                    dve.tensor_scalar(xn[u][:, :], x, mean[:, ds(t, 1)], rstd[:, ds(t, 1)],
                                      ALU.subtract, ALU.mult).then_inc(xn_ready, 1)
                    dve.wait_ge(xn_ready, t + 1)
                    dve.tensor_tensor(x, x, bias[:, :], ALU.add).then_inc(biased, 1)

        @block.gpsimd
        def _(pool):
            pool.sem_inc(added, NX)
            with pool.Fori(0, NT // NX) as it:
                for u in range(NX):
                    t = it * NX + u
                    x = tok[:, ds(t, 1), :].squeeze(1)
                    pool.wait_ge(biased, t + 1)
                    pool.sem_inc(pool_going, 1)
                    pool.tensor_tensor(x, x, xn[u][:, :], ALU.add).then_inc(added, 1)

        @block.tensor
        def _(pe):
            pe.sem_inc(turned, NX)
            with pe.Fori(0, NT // NX) as it:
                for u in range(NX):
                    t = it * NX + u
                    pe.wait_ge(xn_ready, t + 1)
                    pe.wait_ge(taken, t + 1)
                    for k in range(KB):
                        last = pe.transpose(pt[u % 2][:, k * P:(k + 1) * P], xn[u][:, k * P:(k + 1) * P], ident32[:, :])
                    last.then_inc(turned, 1)

        @block.scalar
        def _(act):
            act.sem_inc(taken, 2)
            with act.Fori(0, NT // NX) as it:
                for u in range(NX):
                    t = it * NX + u
                    act.wait_ge(turned, t + 1 + NX)
                    act.sem_inc(going, 1)
                    act.activation(xc[:, :, ds(t * P, P)], pt[u % 2][:, 0:D].rearrange("p (k s) -> p k s", k=KB),
                                   ACT.Copy).then_inc(taken, 1)


def keys_and_queries(nc, xc, tw, pw, gw, tb_dram, pb_dram, gb_dram, qh, ql, kh, kl, gh, gl):
    ctx = ExitStack()
    with ctx:
        sb = lambda n, shape, dt=F32: ctx.enter_context(nc.sbuf_tensor("kq_" + n, shape, dt))
        sem = lambda n: semaphore(nc, "kq_" + n)
        xh = sb("xh", [P, KB, S], F16)
        xl = sb("xl", [P, KB, S], F16)
        half = sb("half", [P, KB, HW // 2, HW])
        xp = sb("xp", [P, KB, M_KEYS])
        xph = sb("xph", [P, KB, M_KEYS], F16)
        xpl = sb("xpl", [P, KB, M_KEYS], F16)
        tbias = sb("tbias", [P, 1])
        pbias = sb("pbias", [P, 1])
        gbias = sb("gbias", [P, C1])
        thf = [sb(f"thf{u}", [P, CHUNK]) for u in range(2)]
        phf = sb("phf", [P, M_KEYS])
        gf = sb("gf", [P, MT, C1])
        pth = [ctx.enter_context(nc.psum_tensor(f"kq_pth{u}", [P, 512], F32)) for u in range(2)]
        pph = ctx.enter_context(nc.psum_tensor("kq_pph", [P, 2, 512], F32))
        pg = ctx.enter_context(nc.psum_tensor("kq_pg", [P, 2, 512], F32))
        b_in = sem("b_in")
        xh_ready = sem("xh_ready")
        xl_ready = sem("xl_ready")
        pooled = sem("pooled")
        p_halves = sem("p_halves")
        th_ready = sem("th_ready")
        thf_ready = sem("thf_ready")
        qh_ready = sem("qh_ready")
        ql_ready = sem("ql_ready")
        ph_ready = sem("ph_ready")
        phf_ready = sem("phf_ready")
        g_ready = sem("g_ready")
        gstep = sem("gstep")
        block = ctx.enter_context(nc.Block())
        XQ = 4
        XC = S // XQ
        JQ = S // CHUNK

        @block.sync
        def _(sp):
            with nc.allow_non_contiguous_dma(reason="one bias for a partition"):
                sp.dma_start(tbias[:, :], tb_dram.rearrange("(p a) -> p a", a=1)).then_inc(b_in, 16)
                sp.dma_start(pbias[:, :], pb_dram.rearrange("(p a) -> p a", a=1)).then_inc(b_in, 16)
            sp.dma_start(gbias[:, :], gb_dram.partition_broadcast(P)).then_inc(b_in, 16)

        @block.scalar
        def _(act):
            for q in range(XQ):
                act.activation(xh[:, :, q * XC:(q + 1) * XC], xc[:, :, q * XC:(q + 1) * XC], ACT.Copy).then_inc(xh_ready, 1)
            act.wait_ge(b_in, 48)
            for m in range(2):
                act.wait_ge(ph_ready, m + 1)
                act.activation(phf[:, m * 512:(m + 1) * 512], pph[:, m, :], ACT.Identity, bias=pbias[:, 0:1],
                               scale=1.0 / W_SCALE).then_inc(phf_ready, 1)
            with act.Fori(0, JQ // 2) as it:
                for u in range(2):
                    j = it * 2 + u
                    act.wait_ge(th_ready, j + 1)
                    act.wait_ge(ql_ready, j + 1)
                    act.activation(thf[u][:, :], pth[u][:, :], ACT.Identity, bias=tbias[:, 0:1],
                                   scale=1.0 / W_SCALE).then_inc(thf_ready, 1)

        @block.vector
        def _(dve):
            rows = xc[:, :, :].rearrange("p k (y a x) -> p k y a x", a=2, x=HW)
            dve.tensor_tensor(half[:, :, :, :], rows[:, :, :, 0, :], rows[:, :, :, 1, :], ALU.max).then_inc(pooled, 1)
            dve.wait_ge(pooled, 1)
            cols = half[:, :, :, :].rearrange("p k y (x a) -> p k (y x) a", a=2)
            dve.tensor_tensor(xp[:, :, :], cols[:, :, :, 0], cols[:, :, :, 1], ALU.max).then_inc(pooled, 1)
            dve.wait_ge(pooled, 2)
            dve.tensor_copy(xph[:, :, :], xp[:, :, :]).then_inc(p_halves, 1)
            dve.wait_ge(p_halves, 1)
            dve.tensor_tensor(xpl[:, :, :], xp[:, :, :], xph[:, :, :], ALU.subtract).then_inc(p_halves, 1)
            dve.wait_ge(b_in, 48)
            for m in range(2):
                dve.wait_ge(g_ready, m + 1)
                dve.scalar_tensor_tensor(out=gf[:, m * 4:m * 4 + 4, :], in0=pg[:, m, :].rearrange("p (a c) -> p a c", c=C1),
                                         scalar=1.0 / W_SCALE, in1=gbias[:, :].unsqueeze(1).broadcast_to([P, 4, C1]),
                                         op0=ALU.mult, op1=ALU.add).then_inc(gstep, 1)
            dve.wait_ge(gstep, 2)
            dve.tensor_copy(gh[:, :, :], gf[:, :, :]).then_inc(gstep, 1)
            dve.wait_ge(gstep, 3)
            dve.tensor_tensor(gl[:, :, :], gf[:, :, :], gh[:, :, :], ALU.subtract).then_inc(gstep, 1)
            dve.wait_ge(phf_ready, 2)
            dve.tensor_copy(kh[:, :], phf[:, :]).then_inc(gstep, 1)
            dve.wait_ge(gstep, 5)
            dve.tensor_tensor(kl[:, :], phf[:, :], kh[:, :], ALU.subtract).then_inc(gstep, 1)
            with dve.Fori(0, JQ // 2) as it:
                for u in range(2):
                    j = it * 2 + u
                    dve.wait_ge(thf_ready, j + 1)
                    to = lambda q: q[:, :].rearrange("p (r i) -> p i r", r=R1)[:, ds(j * (CHUNK // R1), CHUNK // R1), :]
                    src = thf[u][:, :].rearrange("p (i r) -> p i r", r=R1)
                    dve.tensor_copy(to(qh), src).then_inc(qh_ready, 1)
                    dve.wait_ge(qh_ready, j + 1)
                    dve.tensor_tensor(to(ql), src, to(qh), ALU.subtract).then_inc(ql_ready, 1)
            dve.wait_ge(gstep, 6)
            dve.wait_ge(ql_ready, JQ + 2)

        @block.gpsimd
        def _(pool):
            for q in range(XQ):
                c = slice(q * XC, (q + 1) * XC)
                pool.wait_ge(xh_ready, q + 1)
                pool.tensor_tensor(xl[:, :, c], xc[:, :, c], xh[:, :, c], ALU.subtract).then_inc(xl_ready, 1)
                pool.wait_ge(xl_ready, q + 1)

        @block.tensor
        def _(pe):
            def summed(to, pairs):
                for n, (lhs, rhs) in enumerate(pairs):
                    last = pe.matmul(to, lhs, rhs, start=(n == 0), stop=(n == len(pairs) - 1))
                return last

            pe.sem_inc(ql_ready, 2)
            pe.wait_ge(p_halves, 2)
            for m in range(2):
                c = slice(m * 512, (m + 1) * 512)
                last = summed(pph[:, m, :], [x for k in range(KB) for x in
                                            ((pw[0][:, k, :], xph[:, k, c]), (pw[1][:, k, :], xph[:, k, c]),
                                             (pw[0][:, k, :], xpl[:, k, c]))])
                last.then_inc(ph_ready, 1)
            for m in range(MT):
                c = slice(m * P, (m + 1) * P)
                last = summed(pg[:, m // 4, (m % 4) * C1:(m % 4 + 1) * C1],
                             [x for k in range(KB) for x in
                              ((xph[:, k, c], gw[0][:, k, :]), (xpl[:, k, c], gw[0][:, k, :]),
                               (xph[:, k, c], gw[1][:, k, :]))])
                if m % 4 == 3:
                    last.then_inc(g_ready, 1)
            pe.wait_ge(xl_ready, XQ)
            with pe.Fori(0, JQ // 2) as it:
                for u in range(2):
                    j = it * 2 + u
                    pe.wait_ge(ql_ready, j + 1)
                    last = summed(pth[u][:, :], [x for k in range(KB) for x in
                                                ((tw[0][:, k, :], xh[:, k, ds(j * CHUNK, CHUNK)]),
                                                 (tw[1][:, k, :], xh[:, k, ds(j * CHUNK, CHUNK)]),
                                                 (tw[0][:, k, :], xl[:, k, ds(j * CHUNK, CHUNK)]))])
                    last.then_inc(th_ready, 1)


def nonlocal_attention(nc, qh, ql, kh, kl, gh, gl, zw, ident32, tok, stats):
    ctx = ExitStack()
    with ctx:
        sb = lambda n, shape, dt=F32: ctx.enter_context(nc.sbuf_tensor("na_" + n, shape, dt))
        ps = lambda n, shape: ctx.enter_context(nc.psum_tensor("na_" + n, shape, F32))
        sem = lambda n: semaphore(nc, "na_" + n)
        prob = [sb(f"prob{u}", [P, M_KEYS]) for u in range(2)]
        pth = [sb(f"pth{u}", [P, M_KEYS], F16) for u in range(2)]
        ptl = [sb(f"ptl{u}", [P, M_KEYS], F16) for u in range(2)]
        negmax = [sb(f"negmax{u}", [P, 1]) for u in range(4)]
        den = [sb(f"den{u}", [P, 1]) for u in range(4)]
        rec = sb("rec", [P, 1])
        m3 = [sb(f"m3{u}", [P, C1]) for u in range(2)]
        m3h = [sb(f"m3h{u}", [P, C1], F16) for u in range(2)]
        m3l = [sb(f"m3l{u}", [P, C1], F16) for u in range(2)]
        score = [ps(f"score{u}", [P, M_KEYS]) for u in range(2)]
        turned = ps("turned", [P, M_KEYS])
        outp = ps("outp", [P, 512])
        proj = ps("proj", [P, 512])
        s_ready = sem("s_ready")
        max_ready = sem("max_ready")
        exp_ready = sem("exp_ready")
        t_ready = sem("t_ready")
        hi_ready = sem("hi_ready")
        lo_ready = sem("lo_ready")
        o_ready = sem("o_ready")
        m3_step = sem("m3_step")
        m3_ready = sem("m3_ready")
        half_ready = sem("half_ready")
        pool_going = sem("pool_going")
        z_ready = sem("z_ready")
        added = sem("added")
        block = ctx.enter_context(nc.Block())
        U = 4
        BODY = (R1 - 3) // U * U

        def pipelined(eng, step):
            with eng.Fori(0, BODY // U) as it:
                for u in range(U):
                    step(it * U + u, u, R1)
            for r in range(BODY, R1):
                step(r, r % U, R1 - r)

        @block.tensor
        def _(pe):
            def scores(r, u):
                pe.wait_ge(exp_ready, r + 1)
                q = ds(r * P, P)
                for m in range(2):
                    c = slice(m * 512, (m + 1) * 512)
                    to = score[u % 2][:, c]
                    pe.matmul(to, qh[:, q], kh[:, c], start=True, stop=False)
                    pe.matmul(to, qh[:, q], kl[:, c], start=False, stop=False)
                    last = pe.matmul(to, ql[:, q], kh[:, c], start=False, stop=True)
                last.then_inc(s_ready, 1)

            def turn(r, u):
                pe.wait_ge(exp_ready, r + 3)
                pe.wait_ge(lo_ready, r + 1)
                for m in range(MT):
                    c = slice(m * P, (m + 1) * P)
                    last = pe.transpose(turned[:, c], prob[u % 2][:, c], ident32[:, :])
                last.then_inc(t_ready, 1)

            def times_g(r, u):
                pe.wait_ge(lo_ready, r + 2)
                pe.wait_ge(m3_step, r * 2 + 1)
                for m in range(MT):
                    c = slice(m * P, (m + 1) * P)
                    to = outp[:, 0:C1]
                    pe.matmul(to, pth[u % 2][:, c], gh[:, m, :], start=(m == 0), stop=False)
                    pe.matmul(to, pth[u % 2][:, c], gl[:, m, :], start=False, stop=False)
                    last = pe.matmul(to, ptl[u % 2][:, c], gh[:, m, :], start=False, stop=(m == MT - 1))
                last.then_inc(o_ready, 1)

            def project(r, u):
                pe.wait_ge(m3_ready, r + 5)
                pe.wait_ge(added, r + 1)
                to = proj[:, 0:D]
                pe.matmul(to, m3h[u % 2][:, :], zw[0][:, 0, :], start=True, stop=False)
                pe.matmul(to, m3h[u % 2][:, :], zw[1][:, 0, :], start=False, stop=False)
                pe.matmul(to, m3l[u % 2][:, :], zw[0][:, 0, :], start=False, stop=True).then_inc(z_ready, 1)

            def step(r, u, left):
                if left > 3:
                    scores(r + 3, u + 3)
                if left > 2:
                    turn(r + 2, u + 2)
                if left > 1:
                    times_g(r + 1, u + 1)
                project(r, u)

            pe.sem_inc(t_ready, 2)
            pe.sem_inc(o_ready, 2)
            pe.sem_inc(z_ready, 2)
            scores(0, 0)
            scores(1, 1)
            turn(0, 0)
            scores(2, 2)
            turn(1, 1)
            times_g(0, 0)
            pipelined(pe, step)

        @block.scalar
        def _(act):
            def exps(r, u):
                act.wait_ge(max_ready, r + 1)
                act.wait_ge(t_ready, r + 1)
                act.wait_ge(m3_ready, r + 1)
                act.activation(prob[u % 2][:, :], score[u % 2][:, :], ACT.Exp, bias=negmax[u % 4][:, 0:1],
                               accum_out=den[u % 4][:, 0:1]).then_inc(exp_ready, 1)

            def high(r, u):
                act.wait_ge(t_ready, r + 3)
                act.wait_ge(o_ready, r + 1)
                act.activation(pth[u % 2][:, :], turned[:, :], ACT.Copy).then_inc(hi_ready, 1)

            def step(r, u, left):
                if left > 2:
                    high(r + 2, u + 2)
                if left > 3:
                    exps(r + 3, u + 3)

            act.sem_inc(exp_ready, 2)
            exps(0, 0)
            exps(1, 1)
            high(0, 0)
            exps(2, 2)
            high(1, 1)
            pipelined(act, step)

        @block.vector
        def _(dve):
            def maxima(r, u):
                dve.wait_ge(s_ready, r + 1)
                dve.tensor_reduce(negmax[u % 4][:, :], score[u % 2][:, :], AX.X, ALU.max, negate=True).then_inc(max_ready, 1)

            def low(r, u):
                dve.wait_ge(hi_ready, r + 1)
                dve.tensor_tensor(ptl[u % 2][:, :], turned[:, :], pth[u % 2][:, :], ALU.subtract).then_inc(lo_ready, 1)

            def image(r, u):
                dve.wait_ge(o_ready, r + 3)
                dve.wait_ge(m3_ready, r + 3)
                dve.reciprocal(rec[:, :], den[u % 4][:, :]).then_inc(m3_step, 1)
                dve.wait_ge(m3_step, r * 2 + 2)
                dve.tensor_scalar(m3[u % 2][:, :], outp[:, 0:C1], rec[:, 0:1], None, ALU.mult).then_inc(m3_step, 1)

            def add(r, u):
                dve.wait_ge(z_ready, r + 3)
                t = tok[:, ds(r, 1), :].squeeze(1)
                dve.scalar_tensor_tensor(out=t, in0=proj[:, 0:D], scalar=1.0 / W_SCALE, in1=t, op0=ALU.mult,
                                         op1=ALU.add).then_inc(added, 1)
                dve.wait_ge(added, r + 2)
                dve.bn_stats(stats[:, ds(r, 1), :].squeeze(1), t)

            def step(r, u, left):
                if left > 3:
                    maxima(r + 3, u + 3)
                if left > 2:
                    low(r + 2, u + 2)
                if left > 1:
                    image(r + 1, u + 1)
                add(r, u)

            dve.sem_inc(lo_ready, 1)
            dve.sem_inc(m3_step, 1)
            dve.sem_inc(added, 1)
            maxima(0, 0)
            maxima(1, 1)
            low(0, 0)
            maxima(2, 2)
            low(1, 1)
            image(0, 0)
            pipelined(dve, step)

        @block.gpsimd
        def _(pool):
            def split(r, u):
                pool.wait_ge(m3_step, r * 2 + 3)
                pool.wait_ge(z_ready, r + 1)
                pool.sem_inc(pool_going, 1)
                pool.tensor_copy(m3h[u % 2][:, :], m3[u % 2][:, :]).then_inc(half_ready, 1)
                pool.wait_ge(half_ready, r + 1)
                pool.tensor_tensor(m3l[u % 2][:, :], m3[u % 2][:, :], m3h[u % 2][:, :], ALU.subtract).then_inc(m3_ready, 1)

            def step(r, u, left):
                if left > 1:
                    split(r + 1, u + 1)

            pool.sem_inc(m3_ready, 4)
            split(0, 0)
            pipelined(pool, step)


def layer1_attention(nc, tok, stats, theta_w, theta_b, phi_w, phi_b, g_w, g_b, wz_w, wz_b, ident32):
    ctx = ExitStack()
    with ctx:
        sb = lambda n, shape, dt=F16: ctx.enter_context(nc.sbuf_tensor("l1_" + n, shape, dt))
        mean = sb("mean", [P, NT], F32)
        rstd = sb("rstd", [P, NT], F32)
        tw = [sb(f"tw{i}", [P, KB, C1]) for i in range(2)]
        pw = [sb(f"pw{i}", [P, KB, C1]) for i in range(2)]
        gw = [sb(f"gw{i}", [P, KB, C1]) for i in range(2)]
        zw = [sb(f"zw{i}", [P, 1, D]) for i in range(2)]
        qh, ql = sb("qh", [P, S]), sb("ql", [P, S])
        kh, kl = sb("kh", [P, M_KEYS]), sb("kl", [P, M_KEYS])
        gh, gl = sb("gh", [P, MT, C1]), sb("gl", [P, MT, C1])
        turn_and_split_weights(nc, "l1w_", [(w, rows, cols, to[0][:, :, :], to[1][:, :, :]) for w, rows, cols, to in
                                            ((theta_w, C1, D, tw), (phi_w, C1, D, pw), (g_w, C1, D, gw),
                                             (wz_w, D, C1, zw))], ident32)
        token_norm(nc, "l1n", stats, LN_C_EPS, mean, rstd)
        with nc.sbuf_tensor("l1_xc", [P, KB, S], F32) as xc:
            tokens_to_channels(nc, "tc", tok, mean, rstd, wz_b, ident32, xc)
            keys_and_queries(nc, xc, tw, pw, gw, theta_b, phi_b, g_b, qh, ql, kh, kl, gh, gl)
        nonlocal_attention(nc, qh, ql, kh, kl, gh, gl, zw, ident32, tok, stats)


def build(nc, x, w_qkv, w_proj, temperature, router_w, w1_0, b1_0, w2_0, b2_0, theta_w, theta_b, phi_w, phi_b,
          g_w, g_b, wz_w, wz_b, gate_w, gate_b, w1_1, b1_1, w2_1, b2_1, out):
    IN_USE.clear()
    sorted_dram = nc.dram_tensor("sorted_rows", (ROWS, 2 * D), F16, kind="Internal").ap()
    y_dram = nc.dram_tensor("expert_rows", (ROWS, D), F32, kind="Internal").ap()
    ctx = ExitStack()
    with ctx:
        sb = lambda name, shape, dt: ctx.enter_context(nc.sbuf_tensor(name, shape, dt))
        ident32 = sb("ident32", [P, P], F32)
        ident16 = sb("ident16", [P, P], F16)
        below = sb("below", [P, P], F16)
        ones = sb("ones", [P, P], F16)
        steps = sb("steps", [P, S // ET], F32)
        first = sb("first", [P, E_N], F32)
        stats = sb("stats", [P, NT, 6], F32)
        tile_no = sb("tile_no", [P, MAXT], F32)
        consts = (below, ones, steps, first, tile_no)
        make_identities(nc, ident32, ident16)
        make_routing_constants(nc, *consts)
        tok = sb("tok", [P, NT, D], F32)
        image = tok[:, :, :].rearrange("p t c -> p (t c)").rearrange("p (k s) -> p k s", k=KB)
        with ExitStack() as c2:
            sb2 = lambda name, shape, dt: c2.enter_context(nc.sbuf_tensor(name, shape, dt))
            tau = sb2("tau", [P, HEADS], F32)
            rstd = sb2("rstd", [P, NT], F32)
            qk = sb2("qk", [P, NT, HEADS, 4 * DH], F16)
            vs = sb2("vs", [P, NT, HEADS, VW], F16)
            with nc.sbuf_tensor("xh", [P, KB, S], F16) as xh, nc.sbuf_tensor("xl", [P, KB, S], F16) as xl, \
                    nc.sbuf_tensor("wh", [P, KB, 3 * D], F16) as wh, nc.sbuf_tensor("wl", [P, KB, 3 * D], F16) as wl:
                xp = qk[:, :, :, :].rearrange("p t h c -> p (t h c)")[:, 0:2 * KB * S].bitcast(F32)
                load_and_split_tokens(nc, x, w_qkv, temperature, ident32, image,
                                      xp.rearrange("p (k s) -> p k s", k=KB), xh, xl, rstd, tau, wh, wl)
                project_qkv(nc, xh, xl, rstd, tau, wh, wl, image, qk, vs)
            attention(nc, qk, vs, tau, ident16, image, sorted_dram)
        project_attention(nc, x, w_proj, image, ident32, tok, stats)
        moe(nc, "m0", tok, D, True, router_w, True, None, w1_0, b1_0, w2_0, b2_0, sorted_dram, y_dram, ident16,
            ident32, consts, True, stats, None)
        clear_semaphores(nc)
        layer1_attention(nc, tok, stats, theta_w, theta_b, phi_w, phi_b, g_w, g_b, wz_w, wz_b, ident32)
        moe(nc, "m1", tok, 4 * D, False, gate_w, False, gate_b, w1_1, b1_1, w2_1, b2_1, sorted_dram, y_dram, ident16,
            ident32, consts, False, stats, out)


_INS = ['x', 'L0_conv_w_qkv', 'L0_conv_w_proj', 'L0_conv_temperature', 'L0_ffn_router_w', 'L0_ffn_w1', 'L0_ffn_b1',
        'L0_ffn_w2', 'L0_ffn_b2', 'L1_conv_theta_w', 'L1_conv_theta_b', 'L1_conv_phi_w', 'L1_conv_phi_b', 'L1_conv_g_w',
        'L1_conv_g_b', 'L1_conv_wz_w', 'L1_conv_wz_b', 'L1_ffn_Wg', 'L1_ffn_bg', 'L1_ffn_W1', 'L1_ffn_b1', 'L1_ffn_W2',
        'L1_ffn_b2']
_OUTS = [((1, D, HW, HW), 'float32')]


def kernel(**inputs):
    import numpy as _np
    import concourse.bacc as _bacc
    from concourse import mybir as _mybir
    from concourse.bass_utils import run_bass_kernel_spmd as _run

    nc = _bacc.Bacc("TRN2", target_bir_lowering=False, num_devices=1)
    arrays, args = {}, []
    for name in _INS:
        a = _np.ascontiguousarray(inputs[name])
        arrays[f"in_{name}_dram"] = a
        args.append(nc.dram_tensor(f"in_{name}_dram", a.shape, _mybir.dt.from_np(a.dtype), kind="ExternalInput").ap())
    for i, (shape, dtype) in enumerate(_OUTS):
        dt = _mybir.dt.from_np(_np.dtype(dtype))
        args.append(nc.dram_tensor(f"out_{i}_dram", shape, dt, kind="ExternalOutput").ap())
    build(nc, *args)
    r = _run(nc, [arrays], core_ids=[0])
    got = tuple(r.results[0][f"out_{i}_dram"] for i in range(len(_OUTS)))
    return got[0]
```
